# Optimizing a Trainium2 kernel written in Bass

```python
import numpy as np
import jax
import jax.numpy as jnp

def _softmax(x, axis=-1):
    return jax.nn.softmax(x, axis=axis)

def _gelu(x):
    return jax.nn.gelu(x, approximate=True)

def _silu(x):
    return jax.nn.silu(x)

def _sigmoid(x):
    return jax.nn.sigmoid(x)

def _layernorm(x, axis=-1, eps=1e-05):
    m = jnp.mean(x, axis=axis, keepdims=True)
    v = jnp.var(x, axis=axis, keepdims=True)
    return (x - m) / jnp.sqrt(v + eps)

def _scatter_add(tgt, idx, src, axis=0):
    return tgt.at[idx].add(src)

def _segment_sum(src, seg, n):
    return jax.ops.segment_sum(src, seg, n)
kernel_name = 'mk_gnn_preln_d4_gnn_r64_fdc7d8'

def setup_inputs(seed: int=0):
    np.random.seed(seed)
    _w = jnp.asarray

    def _rec_inputs():
        import jax
        import jax.numpy as jnp
        _gk = jax.random.key(seed)
        x = -0.000202 + 1 * jax.random.normal(jax.random.fold_in(_gk, 1), (50000, 128), jnp.float32)
        src = jax.random.randint(jax.random.fold_in(_gk, 2), (12500,), 0, 50000, jnp.int32)
        dst = jnp.minimum((50000 * jax.random.uniform(jax.random.fold_in(_gk, 3), (12500,)) ** 2.0).astype(jnp.int32), 49999)
        _o = jnp.argsort(dst, stable=True)
        src = src[_o]
        dst = dst[_o]
        return (x, src, dst)
    x, src, dst = _rec_inputs()

    def _L0_gnn_setup():
        import jax, jax.numpy as jnp
        import numpy as np
        N = 50000
        E = 9375
        D = 128
        L = 4
        key = jax.random.key(seed)
        k0, k1, k2, k3 = jax.random.split(key, 4)
        scale = 1.0 / np.sqrt(D)
        node_embedding = jax.random.normal(k0, (N, D), jnp.float32)
        edge_index = jax.random.randint(k1, (2, E), 0, N, dtype=jnp.int32)
        Ws_rel = jax.random.normal(k2, (L, D, D), jnp.float32) * scale
        bs_rel = jnp.zeros((L, D), jnp.float32)
        Ws_root = jax.random.normal(k3, (L, D, D), jnp.float32) * scale
        return {'node_embedding': node_embedding, 'edge_index': edge_index, 'Ws_rel': Ws_rel, 'bs_rel': bs_rel, 'Ws_root': Ws_root}
    _L0_gnn_all = _L0_gnn_setup()
    _L0_gnn_in = {k: v for k, v in _L0_gnn_all.items() if k in ('Ws_rel', 'bs_rel', 'Ws_root')}
    del _L0_gnn_all

    def _L1_gnn_setup():
        import jax, jax.numpy as jnp
        import numpy as np
        N = 3125
        F_IN = 128
        H = 32

        def gcn_conv(x, W, b, src, dst, n):
            h = x @ W
            loops = jnp.arange(n, dtype=src.dtype)
            src2 = jnp.concatenate([src, loops])
            dst2 = jnp.concatenate([dst, loops])
            deg = jax.ops.segment_sum(jnp.ones_like(dst2, dtype=h.dtype), dst2, num_segments=n)
            dinv = jnp.where(deg > 0, jax.lax.rsqrt(deg), 0.0)
            norm = dinv[src2] * dinv[dst2]
            msg = h[src2] * norm[:, None]
            out = jax.ops.segment_sum(msg, dst2, num_segments=n)
            return out + b
        key = jax.random.key(seed)
        ks = jax.random.split(key, 10)
        E = 100000
        x = jax.random.normal(ks[0], (N, F_IN), dtype=jnp.float32)
        edge_index = jax.random.randint(ks[1], (2, E), 0, N, dtype=jnp.int64)

        def glorot(k, fan_in, fan_out):
            s = jnp.sqrt(6.0 / (fan_in + fan_out))
            return jax.random.uniform(k, (fan_in, fan_out), dtype=jnp.float32, minval=-s, maxval=s)
        return {'x': x, 'edge_index': edge_index, 'W1': glorot(ks[2], F_IN, H), 'b1': jnp.zeros((H,), jnp.float32), 'W2': glorot(ks[3], H, H), 'b2': jnp.zeros((H,), jnp.float32), 'W3': glorot(ks[4], H, H), 'b3': jnp.zeros((H,), jnp.float32), 'Wlin': glorot(ks[5], H, F_IN), 'blin': jnp.zeros((F_IN,), jnp.float32)}
    _L1_gnn_all = _L1_gnn_setup()
    _L1_gnn_in = {k: v for k, v in _L1_gnn_all.items() if k in ('W1', 'b1', 'W2', 'b2', 'W3', 'b3', 'Wlin', 'blin')}
    del _L1_gnn_all

    def _L2_gnn_setup():
        import jax, jax.numpy as jnp
        import numpy as np
        N_NODES = 50000
        N_EDGES = 12500
        NODE_DIM = 128
        HIDDEN = 256

        def _glorot(key, shape):
            fan_in, fan_out = (shape[0], shape[1])
            lim = np.sqrt(6.0 / (fan_in + fan_out)).astype(np.float32)
            return jax.random.uniform(key, shape, jnp.float32, -lim, lim)
        key = jax.random.key(seed)
        ks = jax.random.split(key, 12)
        node_features = jax.random.normal(ks[0], (N_NODES, NODE_DIM), jnp.float32)
        edge_index = jax.random.randint(ks[1], (2, N_EDGES), 0, N_NODES, jnp.int64)
        return {'node_features': node_features, 'edge_index': edge_index, 'Wm1': _glorot(ks[2], (2 * NODE_DIM, HIDDEN)), 'bm1': jnp.zeros((HIDDEN,), jnp.float32), 'Wm2': _glorot(ks[3], (HIDDEN, HIDDEN)), 'bm2': jnp.zeros((HIDDEN,), jnp.float32), 'Wm3': _glorot(ks[4], (HIDDEN, NODE_DIM)), 'bm3': jnp.zeros((NODE_DIM,), jnp.float32), 'Wn1': _glorot(ks[5], (2 * NODE_DIM, HIDDEN)), 'bn1': jnp.zeros((HIDDEN,), jnp.float32), 'Wn2': _glorot(ks[6], (HIDDEN, NODE_DIM)), 'bn2': jnp.zeros((NODE_DIM,), jnp.float32)}
    _L2_gnn_all = _L2_gnn_setup()
    _L2_gnn_in = {k: v for k, v in _L2_gnn_all.items() if k in ('Wm1', 'bm1', 'Wm2', 'bm2', 'Wm3', 'bm3', 'Wn1', 'bn1', 'Wn2', 'bn2')}
    del _L2_gnn_all

    def _L3_gnn_setup():
        import jax, jax.numpy as jnp
        import numpy as np
        N_NODES = 100000
        N_EDGES = 25000
        D_FEAT = 128
        ALPHA = 0.1
        K = 10
        key = jax.random.key(seed)
        k1, k2, k3 = jax.random.split(key, 3)
        h = jax.random.normal(k1, (N_NODES, D_FEAT), dtype=jnp.float32)
        src = jax.random.randint(k2, (N_EDGES,), 0, N_NODES, dtype=jnp.int64 if jax.config.jax_enable_x64 else jnp.int32)
        dst = jax.random.randint(k3, (N_EDGES,), 0, N_NODES, dtype=jnp.int64 if jax.config.jax_enable_x64 else jnp.int32)
        deg = jax.ops.segment_sum(jnp.ones((N_EDGES,), jnp.float32), dst, num_segments=N_NODES)
        norm = jnp.where(deg > 0, jax.lax.rsqrt(jnp.maximum(deg, 1.0)), 0.0)[:, None]
        return {'h': h, 'norm': norm, 'src': src, 'dst': dst}
    _L3_gnn_all = _L3_gnn_setup()
    _L3_gnn_in = {k: v for k, v in _L3_gnn_all.items() if k in ()}
    del _L3_gnn_all
    return {'x': x, 'src': src, 'dst': dst, 'L0_gnn_Ws_rel': _L0_gnn_in['Ws_rel'], 'L0_gnn_bs_rel': _L0_gnn_in['bs_rel'], 'L0_gnn_Ws_root': _L0_gnn_in['Ws_root'], 'L1_gnn_W1': _L1_gnn_in['W1'], 'L1_gnn_b1': _L1_gnn_in['b1'], 'L1_gnn_W2': _L1_gnn_in['W2'], 'L1_gnn_b2': _L1_gnn_in['b2'], 'L1_gnn_W3': _L1_gnn_in['W3'], 'L1_gnn_b3': _L1_gnn_in['b3'], 'L1_gnn_Wlin': _L1_gnn_in['Wlin'], 'L1_gnn_blin': _L1_gnn_in['blin'], 'L2_gnn_Wm1': _L2_gnn_in['Wm1'], 'L2_gnn_bm1': _L2_gnn_in['bm1'], 'L2_gnn_Wm2': _L2_gnn_in['Wm2'], 'L2_gnn_bm2': _L2_gnn_in['bm2'], 'L2_gnn_Wm3': _L2_gnn_in['Wm3'], 'L2_gnn_bm3': _L2_gnn_in['bm3'], 'L2_gnn_Wn1': _L2_gnn_in['Wn1'], 'L2_gnn_bn1': _L2_gnn_in['bn1'], 'L2_gnn_Wn2': _L2_gnn_in['Wn2'], 'L2_gnn_bn2': _L2_gnn_in['bn2']}

def reference(x, src, dst, L0_gnn_Ws_rel, L0_gnn_bs_rel, L0_gnn_Ws_root, L1_gnn_W1, L1_gnn_b1, L1_gnn_W2, L1_gnn_b2, L1_gnn_W3, L1_gnn_b3, L1_gnn_Wlin, L1_gnn_blin, L2_gnn_Wm1, L2_gnn_bm1, L2_gnn_Wm2, L2_gnn_bm2, L2_gnn_Wm3, L2_gnn_bm3, L2_gnn_Wn1, L2_gnn_bn1, L2_gnn_Wn2, L2_gnn_bn2):
    import jax
    import jax.numpy as jnp

    def _L0_gnn_ref(node_embedding, edge_index, Ws_rel, bs_rel, Ws_root):
        import jax, jax.numpy as jnp
        import numpy as np
        N = 50000
        E = 9375
        D = 128
        L = 4
        n = node_embedding.shape[0]
        src, dst = (edge_index[0], edge_index[1])
        ones = jnp.ones((edge_index.shape[1],), node_embedding.dtype)
        deg = jax.ops.segment_sum(ones, dst, num_segments=n)
        inv_deg = (1.0 / jnp.maximum(deg, 1.0))[:, None]
        X = node_embedding
        for l in range(Ws_rel.shape[0]):
            agg = jax.ops.segment_sum(X[src], dst, num_segments=n) * inv_deg
            out = agg @ Ws_rel[l] + bs_rel[l] + X @ Ws_root[l]
            X = jax.nn.elu(out)
        return X

    def _L1_gnn_ref(x, edge_index, W1, b1, W2, b2, W3, b3, Wlin, blin):
        import jax, jax.numpy as jnp
        import numpy as np
        N = 3125
        F_IN = 128
        H = 32

        def gcn_conv(x, W, b, src, dst, n):
            h = x @ W
            loops = jnp.arange(n, dtype=src.dtype)
            src2 = jnp.concatenate([src, loops])
            dst2 = jnp.concatenate([dst, loops])
            deg = jax.ops.segment_sum(jnp.ones_like(dst2, dtype=h.dtype), dst2, num_segments=n)
            dinv = jnp.where(deg > 0, jax.lax.rsqrt(deg), 0.0)
            norm = dinv[src2] * dinv[dst2]
            msg = h[src2] * norm[:, None]
            out = jax.ops.segment_sum(msg, dst2, num_segments=n)
            return out + b
        src, dst = (edge_index[0], edge_index[1])
        n = x.shape[0]
        h = jax.nn.sigmoid(gcn_conv(x, W1, b1, src, dst, n))
        h = jax.nn.sigmoid(gcn_conv(h, W2, b2, src, dst, n))
        h = gcn_conv(h, W3, b3, src, dst, n)
        return jax.nn.sigmoid(h @ Wlin + blin)

    def _L2_gnn_ref(node_features, edge_index, Wm1, bm1, Wm2, bm2, Wm3, bm3, Wn1, bn1, Wn2, bn2):
        import jax, jax.numpy as jnp
        import numpy as np
        N_NODES = 50000
        N_EDGES = 12500
        NODE_DIM = 128
        HIDDEN = 256

        def _glorot(key, shape):
            fan_in, fan_out = (shape[0], shape[1])
            lim = np.sqrt(6.0 / (fan_in + fan_out)).astype(np.float32)
            return jax.random.uniform(key, shape, jnp.float32, -lim, lim)
        num_nodes = node_features.shape[0]
        row, col = (edge_index[0], edge_index[1])
        msg_in = jnp.concatenate([node_features[row], node_features[col]], axis=-1)
        h = jax.nn.relu(msg_in @ Wm1 + bm1)
        h = jax.nn.relu(h @ Wm2 + bm2)
        messages = h @ Wm3 + bm3
        agg = jax.ops.segment_sum(messages, col, num_segments=num_nodes)
        count = jax.ops.segment_sum(jnp.ones((messages.shape[0],), messages.dtype), col, num_segments=num_nodes)
        agg = agg / jnp.clip(count, 1.0)[:, None]
        node_in = jnp.concatenate([node_features, agg], axis=-1)
        upd = jax.nn.relu(node_in @ Wn1 + bn1) @ Wn2 + bn2
        return node_features + upd

    def _L3_gnn_ref(h, norm, src, dst):
        import jax, jax.numpy as jnp
        import numpy as np
        N_NODES = 100000
        N_EDGES = 25000
        D_FEAT = 128
        ALPHA = 0.1
        K = 10
        'APPNP-style propagation: k iterations of norm-scale, SpMM (copy_src+sum), norm-scale, residual mix.'
        h0 = h
        for _ in range(K):
            hs = h * norm
            msgs = hs[src]
            agg = jax.ops.segment_sum(msgs, dst, num_segments=h.shape[0])
            h = agg * norm * (1.0 - ALPHA) + h0 * ALPHA
        return h
    edge_index = jnp.stack([src, dst])
    deg = jnp.maximum(jax.ops.segment_sum(jnp.ones(dst.shape, jnp.float32), dst, num_segments=50000), 1.0)
    deg_isqrt = deg ** (-0.5)
    h = jnp.maximum(_layernorm(x, axis=-1), 0.0)
    x = x + _L0_gnn_ref(h, edge_index, L0_gnn_Ws_rel, L0_gnn_bs_rel, L0_gnn_Ws_root)
    h = jnp.maximum(_layernorm(x, axis=-1), 0.0)
    x = x + _L1_gnn_ref(h, edge_index, L1_gnn_W1, L1_gnn_b1, L1_gnn_W2, L1_gnn_b2, L1_gnn_W3, L1_gnn_b3, L1_gnn_Wlin, L1_gnn_blin)
    h = jnp.maximum(_layernorm(x, axis=-1), 0.0)
    x = x + _L2_gnn_ref(h, edge_index, L2_gnn_Wm1, L2_gnn_bm1, L2_gnn_Wm2, L2_gnn_bm2, L2_gnn_Wm3, L2_gnn_bm3, L2_gnn_Wn1, L2_gnn_bn1, L2_gnn_Wn2, L2_gnn_bn2)
    h = jnp.maximum(_layernorm(x, axis=-1), 0.0)
    x = x + _L3_gnn_ref(h, deg_isqrt[:, None], src, dst)
    return x

_drawn_inputs = setup_inputs


def setup_inputs(seed=0):
    import zlib

    import numpy as np

    out = dict(_drawn_inputs(seed))
    spreads = {'L0_gnn_bs_rel': (0.0, 0.1),
     'L1_gnn_b1': (0.0, 0.8),
     'L1_gnn_b2': (0.0, 0.8),
     'L1_gnn_b3': (0.0, 0.613),
     'L1_gnn_blin': (0.0, 0.393),
     'L2_gnn_bm1': (0.0, 0.8),
     'L2_gnn_bm2': (0.0, 0.8),
     'L2_gnn_bm3': (0.0, 0.574),
     'L2_gnn_bn1': (0.0, 0.1),
     'L2_gnn_bn2': (0.0, 0.1)}
    factors = {'L1_gnn_W1': 8.0, 'L1_gnn_W2': 5.234}
    for name, (base, spread) in spreads.items():
        noise = np.random.default_rng([zlib.crc32(name.encode()), seed]).standard_normal(out[name].shape)
        drawn = base * np.exp(spread * noise) if base else spread * noise
        out[name] = jnp.asarray(drawn.astype(out[name].dtype))
    for name, factor in factors.items():
        out[name] = (out[name] * factor).astype(out[name].dtype)
    return out
```

```python
import numpy as np
import concourse.bass as bass
from concourse import mybir
from contextlib import ExitStack

F32 = mybir.dt.float32
I32 = mybir.dt.int32
U8 = mybir.dt.uint8
ALU = mybir.AluOpType
ACT = mybir.ActivationFunctionType

N = 50000
D = 128
E = 12500
HG = 32
LAYERS = 4
HOPS = 10
ALPHA = 0.1
EPS = 1e-5
P = 128
TPC = 4
CH = TPC * P
NCH = -(-E // CH)
NT = NCH * TPC
NE = NCH * CH
PAD = NE - E
FAR = 1 << 20
NODE_ROWS = -(-(N + 1) // P) * P


class Events:

    def __init__(self, sem, names, chunks, lead=0):
        self.sem, self.names, self.chunks, self.lead = sem, names, chunks, lead
        self.size = len(names) * chunks

    def at(self, i, name, u, before=0):
        return i * self.size + ((self.lead - before) * self.size + self.names.index(name) * self.chunks + u + 1)


def tiles(ap):
    return ap.rearrange("p (t f) -> p t f", t=TPC)


class Phase(ExitStack):

    def __init__(self, nc):
        super().__init__()
        self.nc, self.sems = nc, []
        self.callback(self.clear)

    def sem(self, name):
        self.sems.append(self.nc.alloc_semaphore(name))
        return self.sems[-1]

    def clear(self):
        self.nc.clear_and_free_semaphores(self.sems)
        self.nc.all_engine_barrier()


def load_weights(nc, a, sb, pb, sem):
    w = {}

    def tile(name, shape):
        w[name] = sb("w_" + name, shape, F32)
        return w[name]

    root, rel = tile("root", [P, LAYERS, D]), tile("rel", [P, LAYERS, D])
    b_rel = tile("b_rel", [P, LAYERS])
    w1, wlin = tile("w1", [P, HG]), tile("wlin", [HG, D])
    w3t = tile("w3t", [HG, TPC, HG])
    bd2, wc = tile("bd2", [P, P]), tile("wc", [P, TPC, D])
    b3 = tile("b3", [HG, 1])
    b1row, b2row, bm3row = tile("b1row", [P, HG]), tile("b2row", [P, HG]), tile("bm3row", [P, D])
    wm1, wm2, wm3 = tile("wm1", [P, 2, 256]), tile("wm2", [P, 2, 256]), tile("wm3", [P, 2, D])
    wn1, wn2 = tile("wn1", [P, 2, 256]), tile("wn2", [P, 2, D])
    bm1, bm2, bn1 = tile("bm1", [P, 2]), tile("bm2", [P, 2]), tile("bn1", [P, 2])
    raw = tile("raw", [P, 4])
    iso_b1, iso_b2, iso_bz = tile("iso_b1", [P, 1]), tile("iso_b2", [P, 1]), tile("iso_bz", [P, 1])
    dst_bz, bn2h = tile("dst_bz", [P, 1]), tile("bn2h", [P, 1])
    ones, ident = tile("ones", [P, 1]), tile("ident", [P, P])
    bz = tile("bz", [P, 1])
    power = tile("power", [P, CH // P * 2])
    with Phase(nc) as ctx:
        ps = ctx.enter_context(nc.psum_tensor("ps_setup", [P, 3, 512], F32))
        loaded, zeroed, made, folded, summed = (ctx.sem(s) for s in (
            "weights_loaded", "bd2_zeroed", "ident_made", "pe_folded", "dve_summed"))
        block = ctx.enter_context(nc.Block())
        column = lambda ap: ap.unsqueeze(1)
        plain = [
            (root[:], a["L0_gnn_Ws_root"].rearrange("l k m -> k l m")),
            (rel[:], a["L0_gnn_Ws_rel"].rearrange("l k m -> k l m")),
            (b_rel[:], a["L0_gnn_bs_rel"].rearrange("l m -> m l")),
            (w1[:], a["L1_gnn_W1"]), (wlin[:], a["L1_gnn_Wlin"]),
            (b3[:], column(a["L1_gnn_b3"])),
            (b1row[:], a["L1_gnn_b1"].partition_broadcast(P)), (b2row[:], a["L1_gnn_b2"].partition_broadcast(P)),
            (bm3row[:], a["L2_gnn_bm3"].partition_broadcast(P)),
            (wm1[:], a["L2_gnn_Wm1"].rearrange("(b k) m -> k b m", b=2)),
            (wm2[:], a["L2_gnn_Wm2"].rearrange("(b k) m -> k b m", b=2)),
            (wm3[:], a["L2_gnn_Wm3"].rearrange("(b k) m -> k b m", b=2)),
            (wn1[:], a["L2_gnn_Wn1"].rearrange("(b k) m -> k b m", b=2)),
            (wn2[:], a["L2_gnn_Wn2"].rearrange("(b k) m -> k b m", b=2)),
            (bm1[:], a["L2_gnn_bm1"].rearrange("(b k) -> k b", b=2)),
            (bm2[:], a["L2_gnn_bm2"].rearrange("(b k) -> k b", b=2)),
            (bn1[:], a["L2_gnn_bn1"].rearrange("(b k) -> k b", b=2)),
            (raw[:, 2:3], column(a["L1_gnn_blin"])), (raw[:, 3:4], column(a["L2_gnn_bn2"])),
        ]
        packed = []
        for t in range(TPC):
            rows = slice(t * HG, (t + 1) * HG)
            packed += [(raw[rows, 0:1], column(a["L1_gnn_b1"])), (raw[rows, 1:2], column(a["L1_gnn_b2"])),
                       (bd2[rows, rows], a["L1_gnn_W2"]),
                       (w3t[:, t, :], a["L1_gnn_W3"].rearrange("i k -> k i"))]

        @block.sync
        def _(sp):
            with nc.allow_non_contiguous_dma("small weights and biases, once"):
                for dst, src in plain:
                    sp.dma_start(dst, src).then_inc(loaded, 16)
                sp.wait_ge(zeroed, 1)
                for dst, src in packed:
                    sp.dma_start(dst, src).then_inc(loaded, 16)

        @block.gpsimd
        def _(pool):
            pool.memset(ident[:], 0.0).then_inc(made, 1)
            pool.wait_ge(made, 1)
            pool.affine_select(out=ident[:], in_=ident[:], compare_op=ALU.not_equal, fill=1.0, base=0,
                               pattern=[[-1, P]], channel_multiplier=1).then_inc(made, 1)

        @block.tensor
        def _(pe):
            pe.wait_ge(loaded, 16 * (len(plain) + len(packed)))
            pe.wait_ge(summed, 1)
            pe.matmul(ps[:, 0, 0:D], w3t[:].rearrange("k t i -> k (t i)"), wlin[:], start=True, stop=True)
            pe.matmul(ps[:, 1, 0:1], bd2[:], ones[:], start=True, stop=True)
            pe.matmul(ps[:, 2, 0:1], wlin[:], b3[:], start=True, stop=True).then_inc(folded, 1)
            pe.wait_ge(summed, 2)
            pe.matmul(ps[:, 0, 0:1], wc[:, 0, :], ones[:], start=True, stop=True).then_inc(folded, 1)

        @block.vector
        def _(dve):
            dve.memset(bd2[:], 0.0).then_inc(zeroed, 1)
            dve.memset(power[:], -0.5)
            dve.memset(wc[:], 0.0)
            dve.memset(ones[:], 1.0).then_inc(summed, 1)
            dve.wait_ge(loaded, 16 * (len(plain) + len(packed)))
            dve.tensor_scalar(iso_b1[:], raw[:, 0:1], 0.5, None, ALU.mult)
            dve.tensor_scalar(iso_b2[:], raw[:, 1:2], 0.5, None, ALU.mult)
            dve.tensor_scalar(bn2h[:], raw[:, 3:4], 0.5, None, ALU.add)
            dve.wait_ge(folded, 1)
            dve.tensor_copy(bz[:], ps[:, 2, 0:1])
            dve.wait_ge(summed, 1)
            for t in range(TPC):
                g = slice(t * HG, (t + 1) * HG)
                ins = dve.tensor_copy(wc[g, t, :], ps[g, 0, 0:D])
            ins.then_inc(summed, 1)
            dve.wait_ge(summed, 2)
            dve.scalar_tensor_tensor(out=iso_b2[:], in0=ps[:, 1, 0:1], scalar=0.25, in1=iso_b2[:],
                                     op0=ALU.mult, op1=ALU.add)
            dve.tensor_tensor(bz[:], bz[:], raw[:, 2:3], ALU.add).then_inc(summed, 1)
            dve.wait_ge(summed, 3)
            dve.tensor_scalar(dst_bz[:], bz[:], 0.5, None, ALU.mult).then_inc(summed, 1)
            dve.wait_ge(folded, 2)
            dve.wait_ge(summed, 4)
            dve.scalar_tensor_tensor(out=iso_bz[:], in0=ps[:, 0, 0:1], scalar=0.25, in1=dst_bz[:],
                                     op0=ALU.mult, op1=ALU.add)
    return w


def isolated_rows(nc, a, w, name, chunks, passes, taps=None, slots=None):
    U = chunks
    whole = taps is None
    PE_ = (["t0"] + [f"l{l}" for l in range(LAYERS)] + ["tx1", "t1", "g1", "g2", "g3", "tx2", "t2", "na", "nb", "up"]
           + ["tx3"])
    if not whole:
        PE_ = ["t0", "l0", "p1", "l1", "p2", "l2", "p3", "l3", "tx1", "t1", "g1", "pg", "ps1", "g2", "ps2", "g3",
               "tx2", "t2", "na", "nb", "up", "tx3"]
    ACT_ = ["h0", "e0", "e1", "e2", "e3", "h1", "s1", "s2", "tT", "h2", "na", "nb", "uT"]
    if not whole:
        ACT_ = ["h0", "e0", "e1", "e2", "e3", "h1", "pg", "s1", "s2", "tT", "h2", "na", "nb", "uT"]
    ln = [[f"st{k}", f"ag{k}", f"ve{k}", f"xn{k}"] for k in range(4)]
    elu = [[f"m{l}", f"h{l}"] for l in range(LAYERS)]
    if whole:
        DVE_ = ln[0] + sum(elu, []) + ["x1"] + ln[1] + ["x2"] + ln[2] + ["x3a", "x3"] + ln[3] + ["r", "o"]
    else:
        DVE_ = (ln[0] + ["q0"] + elu[0] + ["q1"] + elu[1] + ["q2"] + elu[2] + ["q3"] + elu[3] + ["x1"] + ln[1]
                + ["q4", "s1", "q5", "s2", "q6", "x2"] + ln[2] + ["q7", "x3a", "x3"] + ln[3] + ["q8", "q9"])
    with Phase(nc) as ctx:
        sb = lambda n, shape: [ctx.enter_context(nc.sbuf_tensor(f"{name}_{n}{u}", shape, F32)) for u in range(U)]
        sem = lambda n: ctx.sem(f"{name}_{n}")
        xin, xw, xn, ex, em, hT, out = (sb(n, [P, CH]) for n in ("xin", "xw", "xn", "ex", "em", "hT", "out"))
        sT, sU, nT = sb("sT", [P, P]), sb("sU", [P, P]), sb("nT", [P, 2, CH])
        st, mv, ve, rs = sb("st", [P, TPC, 6]), sb("mv", [P, TPC, 2]), sb("ve", [P, TPC]), sb("rs", [P, TPC])
        ps = [ctx.enter_context(nc.psum_tensor(f"{name}_ps{u}", [P, CH], F32)) for u in range(U)]
        x_in = [sem(f"x_in{u}") for u in range(U)]
        x_used = [sem(f"x_used{u}") for u in range(U)]
        stored = [sem(f"stored{u}") for u in range(U)]
        pe_ev = Events(sem("pe_done"), PE_, U)
        act_ev = Events(sem("act_done"), ACT_, U)
        dve_ev = Events(sem("dve_done"), DVE_, U)
        pool_ev = Events(sem("pool_done"), [f"rs{k}" for k in range(4)], U)
        held = sem("held")
        NTAP = 10
        if not whole:
            tap = [sb(f"tap{k}", [P, CH]) for k in range(2)]
            idx = [ctx.enter_context(nc.sbuf_tensor(f"{name}_idx{u}", [P, TPC], I32)) for u in range(U)]
            idx_in = sem("idx_in")
            tap_stored = [[sem(f"tap{k}_stored{u}") for u in range(U)] for k in range(2)]
        block = ctx.enter_context(nc.Block())
        last = passes - 1

        def wait(eng, ev, i, what, u):
            eng.wait_ge(ev.sem, ev.at(i, what, u))

        def loop(eng, body):
            with eng.Fori(0, last) as i:
                body(i)
            body(last)

        def row0(i, u):
            if isinstance(i, int) and whole:
                return min((i * U + u) * CH, N - CH)
            return i * (U * CH) + u * CH

        def dram(t, i, u):
            r0 = row0(i, u)
            rows = t[bass.ds(r0, CH), :] if not isinstance(r0, int) else t[r0:r0 + CH, :]
            return rows.rearrange("(p t) f -> p (t f)", t=TPC)

        @block.sync
        def _(sp):
            def body(i):
                if whole:
                    for u in range(U):
                        sp.wait_ge(x_used[u], i + 1)
                        sp.dma_start(xin[u][:], dram(a["x"], i, u)).then_inc(x_in[u], 16)
                    for u in range(U):
                        wait(sp, dve_ev, i, "o", u)
                        if not isinstance(i, int) or u < U - 1:
                            pass
                        else:
                            sp.wait_ge(stored[u - 1], 16 * (i + 2))
                        sp.dma_start(dram(a["out"], i, u), out[u][:]).then_inc(stored[u], 16)
                else:
                    for k in range(NTAP):
                        for u in range(U):
                            wait(sp, dve_ev, i, f"q{k}", u)
                            wide = taps[k].shape[1] == D
                            src = tap[k % 2][u][:] if wide else tap[k % 2][u][:, 0:P]
                            sp.dma_start(dram(taps[k], i, u), src).then_inc(tap_stored[k % 2][u], 16)
            for u in range(U):
                sp.sem_inc(stored[u], 16)
                if not whole:
                    for k in range(2):
                        sp.sem_inc(tap_stored[k][u], 16)
            loop(sp, body)
            for u in range(U):
                if whole:
                    sp.wait_ge(stored[u], 16 * passes + 16)
                else:
                    for k in range(2):
                        sp.wait_ge(tap_stored[k][u], 16 * passes * NTAP // 2 + 16)

        @block.gpsimd
        def _(pool):
            if not whole:
                def fetch(i):
                    for u in range(U):
                        pool.wait_ge(x_used[u], i + 1)
                        c0 = i * (U * TPC) + u * TPC
                        pool.tensor_copy(idx[u][:], slots[:, bass.ds(c0, TPC)] if not isinstance(c0, int)
                                         else slots[:, c0:c0 + TPC]).then_inc(idx_in, 1)
                        pool.wait_ge(idx_in, i * U + (u + 1))
                        pool.sem_inc(held, 1)
                        for t in range(TPC):
                            pool.indirect_dma_start(
                                xin[u][:, t * D:(t + 1) * D], None, a["x"],
                                bass.IndirectOffsetOnAxis(idx[u][:, t:t + 1], 0),
                                bounds_check=bound, oob_is_err=False).then_inc(x_in[u], 16)

            bound = pool.to_reg(N - 1)

            def body(i):
                if not whole:
                    fetch(i)
                for k in range(4):
                    for u in range(U):
                        wait(pool, dve_ev, i, f"ve{k}", u)
                        pool.tensor_tensor(rs[u][:], ve[u][:], w["power"][:, 0:TPC], ALU.pow).then_inc(pool_ev.sem, 1)
            loop(pool, body)

        @block.tensor
        def _(pe):
            def done(ins):
                ins.then_inc(pe_ev.sem, 1)

            def to_features(i, u, k):
                wait(pe, dve_ev, i, f"xn{k}", u)
                for t in range(TPC):
                    c = slice(t * P, (t + 1) * P)
                    ins = pe.transpose(ps[u][:, c], xn[u][:, c], w["ident"][:])
                done(ins)

            def back(src, u):
                for t in range(TPC):
                    c = slice(t * P, (t + 1) * P)
                    ins = pe.transpose(ps[u][:, c], src[:, c], w["ident"][:])
                done(ins)

            def body(i):
                us = range(U)
                for u in us:
                    to_features(i, u, 0)
                for l in range(LAYERS):
                    for u in us:
                        if l == 0:
                            wait(pe, act_ev, i, "h0", u)
                        else:
                            wait(pe, dve_ev, i, f"h{l - 1}", u)
                            if not whole:
                                wait(pe, dve_ev, i, f"q{l}", u)
                        done(pe.matmul(ps[u][:], w["root"][:, l, :], hT[u][:], start=True, stop=True))
                    if not whole and l < LAYERS - 1:
                        for u in us:
                            wait(pe, dve_ev, i, f"h{l}", u)
                            back(hT[u], u)
                for u in us:
                    wait(pe, dve_ev, i, f"h{LAYERS - 1}", u)
                    back(hT[u], u)
                for u in us:
                    to_features(i, u, 1)
                for u in us:
                    wait(pe, act_ev, i, "h1", u)
                    for t in range(TPC):
                        ins = pe.matmul(ps[u][t * HG:(t + 1) * HG, 0:P], w["w1"][:], hT[u][:, t * P:(t + 1) * P],
                                        start=True, stop=True)
                    done(ins)
                if not whole:
                    for u in us:
                        wait(pe, act_ev, i, "s1", u)
                        done(pe.transpose(ps[u][:, P:2 * P], sU[u][:], w["ident"][:]))
                    for u in us:
                        wait(pe, dve_ev, i, "q4", u)
                        wait(pe, dve_ev, i, "s1", u)
                        done(pe.transpose(ps[u][:, 0:P], sU[u][:], w["ident"][:]))
                for u in us:
                    if whole:
                        wait(pe, act_ev, i, "s1", u)
                    else:
                        wait(pe, dve_ev, i, "q5", u)
                    done(pe.matmul(ps[u][:, 0:P], w["bd2"][:], sT[u][:], start=True, stop=True))
                if not whole:
                    for u in us:
                        wait(pe, dve_ev, i, "s2", u)
                        done(pe.transpose(ps[u][:, 0:P], xn[u][:, 0:P], w["ident"][:]))
                for u in us:
                    if whole:
                        wait(pe, act_ev, i, "s2", u)
                    else:
                        wait(pe, dve_ev, i, "q6", u)
                    for t in range(TPC):
                        ins = pe.matmul(ps[u][:, t * P:(t + 1) * P], w["wc"][:, t, :], sU[u][:], start=True, stop=True)
                    done(ins)
                for u in us:
                    wait(pe, act_ev, i, "tT", u)
                    back(ex[u], u)
                for u in us:
                    to_features(i, u, 2)
                for b, what in ((0, "na"), (1, "nb")):
                    for u in us:
                        wait(pe, act_ev, i, "h2" if b == 0 else "na", u)
                        done(pe.matmul(ps[u][:], w["wn1"][:, 0, b * P:(b + 1) * P], hT[u][:], start=True, stop=True))
                for u in us:
                    wait(pe, act_ev, i, "nb", u)
                    for b in range(2):
                        ins = pe.matmul(ps[u][:], w["wn2"][:, b, :], nT[u][:, b, :], start=b == 0, stop=b == 1)
                    done(ins)
                for u in us:
                    wait(pe, act_ev, i, "uT", u)
                    back(em[u], u)
            loop(pe, body)

        @block.scalar
        def _(act):
            def step(i, u, what, out_ap, func, producer, **kw):
                wait(act, pe_ev, i, producer, u)
                act.activation(out_ap, ps[u][:, 0:out_ap.shape[1]], func, **kw).then_inc(act_ev.sem, 1)

            def body(i):
                us = range(U)
                for u in us:
                    step(i, u, "h0", hT[u][:], ACT.Relu, "t0")
                for l in range(LAYERS):
                    for u in us:
                        step(i, u, f"e{l}", ex[u][:], ACT.Exp, f"l{l}", bias=w["b_rel"][:, l:l + 1])
                for u in us:
                    step(i, u, "h1", hT[u][:], ACT.Relu, "t1")
                if not whole:
                    for u in us:
                        step(i, u, "pg", sU[u][:], ACT.Identity, "g1")
                for u in us:
                    step(i, u, "s1", sT[u][:], ACT.Tanh, "g1", bias=w["iso_b1"][:], scale=0.5)
                for u in us:
                    if not whole:
                        wait(act, pe_ev, i, "ps1", u)
                    step(i, u, "s2", sU[u][:], ACT.Tanh, "g2", bias=w["iso_b2"][:], scale=0.25)
                for u in us:
                    step(i, u, "tT", ex[u][:], ACT.Tanh, "g3", bias=w["iso_bz"][:], scale=0.25)
                for u in us:
                    step(i, u, "h2", hT[u][:], ACT.Relu, "t2")
                for b, what in ((0, "na"), (1, "nb")):
                    for u in us:
                        step(i, u, what, nT[u][:, b, :], ACT.Relu, what, bias=w["bn1"][:, b:b + 1])
                for u in us:
                    step(i, u, "uT", em[u][:], ACT.Identity, "up", bias=w["bn2h"][:])
            loop(act, body)

        @block.vector
        def _(dve):
            def done(ins):
                ins.then_inc(dve_ev.sem, 1)

            def layernorm(i, k, x, before, used=None):
                us = range(U)
                for u in us:
                    if before == "x_in":
                        dve.wait_ge(x_in[u], (16 if whole else 64) * (i + 1))
                    else:
                        wait(dve, dve_ev, i, before, u)
                    for t in range(TPC):
                        ins = dve.bn_stats(st[u][:, t, :], x[u][:, t * D:(t + 1) * D])
                        if used is not None and t == 0:
                            ins.then_inc(used[u], 1)
                    done(ins)
                wait(dve, dve_ev, i, f"st{k}", U - 1)
                dve.sem_inc(held, 1)
                for u in us:
                    for t in range(TPC):
                        ins = dve.bn_aggr(mv[u][:, t, :], st[u][:, t, :])
                    done(ins)
                for u in us:
                    wait(dve, dve_ev, i, f"ag{k}", u)
                    done(dve.tensor_scalar(ve[u][:], mv[u][:, :, 1], EPS, None, ALU.add))
                for u in us:
                    wait(dve, pool_ev, i, f"rs{k}", u)
                    for t in range(TPC):
                        c = slice(t * D, (t + 1) * D)
                        ins = dve.tensor_scalar(xn[u][:, c], x[u][:, c], mv[u][:, t, 0:1], rs[u][:, t:t + 1],
                                                ALU.subtract, ALU.mult)
                    done(ins)

            def to_tap(i, k, make):
                for u in range(U):
                    dve.wait_ge(tap_stored[k % 2][u], i * (16 * NTAP // 2) + 16 * (k // 2 + 1))
                    done(make(u, tap[k % 2][u]))

            def body(i):
                us = range(U)
                layernorm(i, 0, xin, "x_in")
                if not whole:
                    def make0(u, to):
                        wait(dve, dve_ev, i, "xn0", u)
                        return dve.tensor_scalar(to[:], xn[u][:], 0.0, None, ALU.max)
                    to_tap(i, 0, make0)
                for l in range(LAYERS):
                    for u in us:
                        wait(dve, act_ev, i, f"e{l}", u)
                        done(dve.tensor_scalar(em[u][:], ex[u][:], 1.0, -1.0, ALU.min, ALU.add))
                    for u in us:
                        wait(dve, dve_ev, i, f"m{l}", u)
                        if l > 0 or not whole:
                            pass
                        done(dve.scalar_tensor_tensor(out=hT[u][:], in0=ps[u][:], scalar=w["b_rel"][:, l:l + 1],
                                                      in1=em[u][:], op0=ALU.add, op1=ALU.max))
                    if not whole and l < LAYERS - 1:
                        def make(u, to, l=l):
                            wait(dve, pe_ev, i, f"p{l + 1}", u)
                            return dve.tensor_copy(to[:], ps[u][:])
                        to_tap(i, l + 1, make)
                for u in us:
                    wait(dve, pe_ev, i, "tx1", u)
                    done(dve.tensor_tensor(xw[u][:], ps[u][:], xin[u][:], ALU.add))
                layernorm(i, 1, xw, "x1", x_used)
                if not whole:
                    def make4(u, to):
                        wait(dve, pe_ev, i, "pg", u)
                        return dve.tensor_copy(to[:, 0:P], ps[u][:, P:2 * P])
                    to_tap(i, 4, make4)
                    for u in us:
                        wait(dve, act_ev, i, "s1", u)
                        done(dve.tensor_scalar(sU[u][:], sT[u][:], 0.5, 0.5, ALU.mult, ALU.add))

                    def make5(u, to):
                        wait(dve, pe_ev, i, "ps1", u)
                        return dve.tensor_copy(to[:, 0:P], ps[u][:, 0:P])
                    to_tap(i, 5, make5)
                    for u in us:
                        wait(dve, act_ev, i, "s2", u)
                        done(dve.tensor_scalar(xn[u][:, 0:P], sU[u][:], 0.5, 0.5, ALU.mult, ALU.add))

                    def make6(u, to):
                        wait(dve, pe_ev, i, "ps2", u)
                        return dve.tensor_copy(to[:, 0:P], ps[u][:, 0:P])
                    to_tap(i, 6, make6)
                for u in us:
                    wait(dve, pe_ev, i, "tx2", u)
                    done(dve.scalar_tensor_tensor(out=xw[u][:], in0=ps[u][:], scalar=0.5, in1=xw[u][:],
                                                  op0=ALU.mult, op1=ALU.add))
                layernorm(i, 2, xw, "x2")
                if not whole:
                    def make7(u, to):
                        wait(dve, dve_ev, i, "xn2", u)
                        return dve.tensor_scalar(to[:], xn[u][:], 0.0, None, ALU.max)
                    to_tap(i, 7, make7)
                for u in us:
                    wait(dve, pe_ev, i, "tx3", u)
                    done(dve.scalar_tensor_tensor(out=ex[u][:], in0=xn[u][:], scalar=0.0, in1=ps[u][:],
                                                  op0=ALU.max, op1=ALU.add))
                for u in us:
                    wait(dve, dve_ev, i, "x3a", u)
                    done(dve.tensor_tensor(xw[u][:], xw[u][:], ex[u][:], ALU.add))
                layernorm(i, 3, xw, "x3")
                if whole:
                    for u in us:
                        wait(dve, dve_ev, i, "xn3", u)
                        done(dve.tensor_scalar(ex[u][:], xn[u][:], 0.0, ALPHA, ALU.max, ALU.mult))
                    for u in us:
                        wait(dve, dve_ev, i, "r", u)
                        dve.wait_ge(stored[u], 16 * i + 16)
                        done(dve.tensor_tensor(out[u][:], xw[u][:], ex[u][:], ALU.add))
                else:
                    def make8(u, to):
                        wait(dve, dve_ev, i, "xn3", u)
                        return dve.tensor_scalar(to[:], xn[u][:], 0.0, None, ALU.max)
                    to_tap(i, 8, make8)

                    def make9(u, to):
                        return dve.tensor_scalar(to[:], xn[u][:], 0.0, ALPHA, ALU.max, ALU.mult)
                    to_tap(i, 9, make9)
            for u in range(U):
                dve.sem_inc(x_used[u], 1)
            loop(dve, body)


def constants(nc, sb, n):
    c = {}
    HI = NODE_ROWS // P
    c["row_i"] = sb("c_row_i", [P, HI], I32)
    c["row"] = sb("c_row", [P, HI], F32)
    c["part_i"] = sb("c_part_i", [P, 1], I32)
    c["part"] = sb("c_part", [P, 1], F32)
    c["below"] = sb("c_below", [P, P], F32)
    c["above"] = sb("c_above", [P, P], F32)
    c["slot1"] = sb("c_slot1", [P, NT], I32)
    c["pos1"] = sb("c_pos1", [P, P], F32)
    c["pos1_i"] = sb("c_pos1_i", [P, P], I32)
    with Phase(nc) as ctx:
        counted = ctx.sem(f"iota_written{n}")
        cast = ctx.sem(f"iota_cast{n}")
        block = ctx.enter_context(nc.Block())

        @block.gpsimd
        def _(pool):
            pool.iota(c["row_i"][:], [[1, HI]], base=0, channel_multiplier=0)
            pool.iota(c["part_i"][:], [[1, 1]], base=0, channel_multiplier=1)
            pool.iota(c["slot1"][:], [[CH, NCH], [1, TPC]], base=1, channel_multiplier=TPC)
            pool.iota(c["pos1_i"][:], [[1, P]], base=1, channel_multiplier=P).then_inc(counted, 1)

        @block.vector
        def _(dve):
            dve.wait_ge(counted, 1)
            dve.tensor_copy(c["pos1"][:], c["pos1_i"][:])
            dve.tensor_copy(c["row"][:], c["row_i"][:])
            dve.tensor_copy(c["part"][:], c["part_i"][:]).then_inc(cast, 1)
            dve.wait_ge(cast, 1)
            dve.tensor_scalar(c["below"][:], c["row"][:, 0:P], c["part"][:], None, ALU.is_lt)
            dve.tensor_scalar(c["above"][:], c["row"][:, 0:P], c["part"][:], None, ALU.is_gt)
    return c


def sort_edges(nc, a, w, c, pairs):
    BF = mybir.dt.bfloat16
    HI = NODE_ROWS // P
    FULL, REST = E // P, E % P
    U = TPC
    with Phase(nc) as ctx:
        sb = lambda n, shape, dt=F32: ctx.enter_context(nc.sbuf_tensor("sort_" + n, shape, dt))
        sem = lambda n: ctx.sem("sort_" + n)
        dst_r, src_r, lo_r = sb("dst_r", [NT, P], I32), sb("src_r", [NT, P], I32), sb("lo_r", [NT, P], I32)
        rows_f = sb("rows_f", [NT, 3, P])
        cols = sb("cols", [P, 3, NT])
        dst_c, src_c, hi_c = (sb(n, [P, NT], I32) for n in ("dst_c", "src_c", "hi_c"))
        hi_f = sb("hi_f", [P, NT])
        guard = sb("guard", [1, 4], I32)
        dst_b, lo_b = sb("dst_b", [P, NE]), sb("lo_b", [P, NE])
        zero = sb("zero", [P, P], BF)
        count, total, upto, start = (sb(n, [P, HI]) for n in ("count", "total", "upto", "start"))
        ones = sb("ones", [P, P])
        ring = lambda n, width, dt=F32: [sb(f"{n}{u}", [P, width], dt) for u in range(U)]
        hot_lo, hot_hi, lo_t, table = ring("hot_lo", P, BF), ring("hot_hi", HI, BF), ring("lo_t", P), ring("table", HI)
        same, looked, rank, base = ring("same", P), ring("looked", HI), ring("rank", 1), ring("base", 1)
        to, pair = ring("to", 1, I32), ring("pair", 2, I32)
        ps_t = [ctx.enter_context(nc.psum_tensor(f"sort_ps_t{k}", [P, 512], F32)) for k in range(3)]
        ps_c = ctx.enter_context(nc.psum_tensor("sort_ps_c", [P, 512], F32))
        ps_l = [ctx.enter_context(nc.psum_tensor(f"sort_ps_l{u}", [P, 512], F32)) for u in range(U)]
        flat = nc.dram_tensor("sort_flat", (2, NE), F32, kind="Internal").ap()
        padded, loaded, link = sem("padded"), sem("loaded"), sem("dve_link")
        rows_made, turned, counted, tot_made = (sem(n) for n in ("rows_made", "turned", "counted", "totals_made"))
        flat_out, guard_out, b_in, started = sem("flat_out"), sem("guard_out"), sem("broadcasts_in"), sem("started")
        hot = Events(sem("hot_made"), ["hot"], U)
        hot_used = [sem(f"hot_used{u}") for u in range(U)]
        copied, looked_up = sem("table_copied"), sem("looked_up")
        walk = Events(sem("dve_walk"), ["hot", "same", "rank", "base", "pair", "place"], U)
        scattered = [sem(f"scattered{u}") for u in range(U)]
        held = sem("pool_held")
        block = ctx.enter_context(nc.Block())

        @block.sync
        def _(sp):
            sp.wait_ge(padded, 1)
            for to_sb, of in ((dst_r, a["dst"]), (src_r, a["src"])):
                sp.dma_start(to_sb[0:FULL, :], of[0:FULL * P].rearrange("(r e) -> r e", e=P)).then_inc(loaded, 16)
                sp.dma_start(to_sb[FULL:FULL + 1, 0:REST], of[FULL * P:E].unsqueeze(0)).then_inc(loaded, 16)
            sp.dma_start(pairs[0:1, :], guard[:, 0:2]).then_inc(guard_out, 16)
            sp.dma_start(pairs[NE + 1:NE + 2, :], guard[:, 2:4]).then_inc(guard_out, 16)
            sp.wait_ge(rows_made, 1)
            for k in range(2):
                sp.dma_start(flat[k, :].rearrange("(r e) -> r e", e=P), rows_f[:, k, :]).then_inc(flat_out, 16)
            sp.wait_ge(flat_out, 32)
            for k, to_sb in ((0, dst_b), (1, lo_b)):
                sp.dma_start(to_sb[:], flat[k, :].partition_broadcast(P)).then_inc(b_in, 16)
            sp.wait_ge(guard_out, 32)

        @block.gpsimd
        def _(pool):
            bound = pool.to_reg(NE)
            with pool.Fori(0, NCH) as i:
                for u in range(U):
                    pool.wait_ge(walk.sem, walk.at(i, "place", u))
                    pool.sem_inc(held, 1)
                    pool.indirect_dma_start(pairs, bass.IndirectOffsetOnAxis(to[u][:], 0), pair[u][:], None,
                                            bounds_check=bound, oob_is_err=False).then_inc(scattered[u], 16)
            for u in range(U):
                pool.wait_ge(scattered[u], 16 * NCH)

        @block.tensor
        def _(pe):
            for u in range(U):
                pe.sem_inc(hot_used[u], 1)
            pe.wait_ge(rows_made, 1)
            for k in range(3):
                ins = pe.transpose(ps_t[k][:, 0:NT], rows_f[:, k, :], w["ident"][0:NT, 0:NT])
            ins.then_inc(turned, 1)
            pe.wait_ge(hot.sem, hot.at(0, "hot", 0))
            pe.matmul(ps_c[:, 0:HI], zero[:], hot_hi[0][:], start=True, stop=True, skip_group_check=True)
            with pe.Fori(0, NCH) as i:
                for u in range(U):
                    pe.wait_ge(hot.sem, hot.at(i, "hot", u))
                    pe.matmul(ps_c[:, 0:HI], hot_lo[u][:], hot_hi[u][:], start=False, stop=True,
                              skip_group_check=True).then_inc(hot_used[u], 1)
            pe.wait_ge(tot_made, 1)
            pe.matmul(ps_l[0][:, 0:HI], ones[:], count[:], start=True, stop=True)
            pe.matmul(ps_l[1][:, 0:HI], c["above"][:], count[:], start=True, stop=True).then_inc(counted, 1)
            pe.wait_ge(started, 1)
            pe.matmul(ps_c[:, 0:HI], w["ident"][:], start[:], start=True, stop=True,
                      skip_group_check=True).then_inc(looked_up, 1)
            with pe.Fori(0, NCH) as i:
                for u in range(U):
                    pe.wait_ge(walk.sem, walk.at(i, "hot", u))
                    pe.wait_ge(copied, i * U + (u + 1))
                    pe.matmul(ps_l[u][:, 0:HI], lo_t[u][:], table[u][:], start=True, stop=True)
                    pe.matmul(ps_c[:, 0:HI], hot_lo[u][:], hot_hi[u][:], start=False, stop=True,
                              skip_group_check=True).then_inc(looked_up, 1)

        @block.scalar
        def _(act):
            with act.Fori(0, NCH) as i:
                for u in range(U):
                    act.wait_ge(looked_up, i * U + (u + 1))
                    act.activation(table[u][:], ps_c[:, 0:HI], ACT.Identity).then_inc(copied, 1)

        @block.vector
        def _(dve):
            n = [0]

            def linked(ins):
                n[0] += 1
                ins.then_inc(link, 1)
                dve.wait_ge(link, n[0])

            def hot_rows(i, u, t):
                dve.tensor_scalar(hot_lo[u][:], c["row"][:, 0:P], cols[:, 1, bass.ds(t, 1)], None, ALU.is_equal)
                return dve.tensor_scalar(hot_hi[u][:], c["row"][:], hi_f[:, bass.ds(t, 1)], None, ALU.is_equal)

            dve.memset(guard[:, 0:2], -1)
            dve.memset(guard[:, 2:4], -2)
            dve.memset(src_r[:], 0)
            dve.memset(ones[:], 1.0)
            dve.memset(zero[:], 0.0)
            dve.memset(dst_r[:], N).then_inc(padded, 1)
            dve.wait_ge(loaded, 64)
            dve.tensor_copy(rows_f[:, 0, :], dst_r[:])
            dve.tensor_copy(rows_f[:, 2, :], src_r[:])
            linked(dve.tensor_scalar(lo_r[:], dst_r[:], P - 1, None, ALU.bitwise_and))
            dve.tensor_copy(rows_f[:, 1, :], lo_r[:]).then_inc(rows_made, 1)
            dve.wait_ge(turned, 1)
            for k in range(3):
                ins = dve.tensor_copy(cols[:, k, :], ps_t[k][:, 0:NT])
            linked(ins)
            dve.tensor_copy(src_c[:], cols[:, 2, :])
            linked(dve.tensor_copy(dst_c[:], cols[:, 0, :]))
            linked(dve.tensor_scalar(hi_c[:], dst_c[:], 7, None, ALU.arith_shift_right))
            linked(dve.tensor_copy(hi_f[:], hi_c[:]))
            with dve.Fori(0, NCH) as i:
                for u in range(U):
                    dve.wait_ge(hot_used[u], i + 1)
                    hot_rows(i, u, i * U + u).then_inc(hot.sem, 1)
            for u in range(U):
                dve.wait_ge(hot_used[u], NCH + 1)
            dve.tensor_copy(count[:], ps_c[:, 0:HI]).then_inc(tot_made, 1)
            dve.wait_ge(counted, 1)
            linked(dve.tensor_copy(total[:], ps_l[0][:, 0:HI]))
            linked(dve.tensor_tensor_scan(upto[:], total[:], total[:], 0.0, ALU.add, ALU.bypass))
            linked(dve.tensor_tensor(upto[:], upto[:], total[:], ALU.subtract))
            dve.tensor_tensor(start[:], upto[:], ps_l[1][:, 0:HI], ALU.add).then_inc(started, 1)
            dve.wait_ge(b_in, 32)
            def tile_walk(i):
                def mine(name, u):
                    dve.wait_ge(walk.sem, walk.at(i, name, u))

                def done(ins):
                    ins.then_inc(walk.sem, 1)

                for u in range(U):
                    e = bass.ds(i * CH + u * P, P)
                    dve.tensor_scalar(lo_t[u][:], lo_b[:, e], c["part"][:], None, ALU.is_equal)
                    done(hot_rows(i, u, i * U + u))
                for u in range(U):
                    e = bass.ds(i * CH + u * P, P)
                    done(dve.tensor_scalar(same[u][:], dst_b[:, e], cols[:, 0, bass.ds(i * U + u, 1)], None,
                                           ALU.is_equal))
                for u in range(U):
                    mine("same", u)
                    done(dve.tensor_tensor_reduce(out=same[u][:], in0=same[u][:], in1=c["below"][:], scale=1.0,
                                                  scalar=1.0, op0=ALU.mult, op1=ALU.add, accum_out=rank[u][:]))
                for u in range(U):
                    dve.wait_ge(looked_up, i * U + (u + 2))
                    done(dve.tensor_tensor_reduce(out=looked[u][:], in0=ps_l[u][:, 0:HI], in1=hot_hi[u][:], scale=1.0,
                                                  scalar=0.0, op0=ALU.mult, op1=ALU.add, accum_out=base[u][:]))
                for u in range(U):
                    if not isinstance(i, int):
                        dve.wait_ge(scattered[u], i * 16)
                    dve.tensor_copy(pair[u][:, 0:1], dst_c[:, bass.ds(i * U + u, 1)])
                    done(dve.tensor_copy(pair[u][:, 1:2], src_c[:, bass.ds(i * U + u, 1)]))
                for u in range(U):
                    mine("base", u)
                    done(dve.tensor_tensor(to[u][:], base[u][:], rank[u][:], ALU.add))

            tile_walk(0)
            with dve.Fori(1, NCH) as i:
                tile_walk(i)


def edge_tables(nc, a, w, c, pairs, g, flat):
    with Phase(nc) as ctx:
        t_ = lambda n, shape, dt=F32: ctx.enter_context(nc.sbuf_tensor("idx_" + n, shape, dt))
        sem = lambda n: ctx.sem("idx_" + n)
        near = [t_(f"near{k}", [NT, P, 2], I32) for k in range(3)]
        d = [t_(f"d{k}", [NT, P]) for k in range(3)]
        first, last, f_idx, l_idx, far = (t_(n, [NT, P]) for n in ("first", "lastr", "f_idx", "l_idx", "far"))
        out_r = t_("out_r", [NT, 5, P])
        cols = t_("cols", [P, 5, NT])
        row_f, row_l, carry_f, carry_l = (t_(n, [1, P + 1]) for n in ("row_f", "row_l", "carry_f", "carry_l"))
        back_f, back_l = t_("back_f", [NT, 1]), t_("back_l", [NT, 1])
        deg1, tmp = t_("deg1", [P, NT]), t_("tmp", [P, NT])
        half = t_("half", [P, NT])
        zero = t_("zero", [P, NODE_ROWS // P], I32)
        found = t_("found", [P, NT], I32)
        found_f = t_("found_f", [P, NT])
        bc = t_("bc", [P, NE])
        ps = [ctx.enter_context(nc.psum_tensor(f"idx_ps{k}", [P, 512], F32)) for k in range(6)]
        node_row = nc.dram_tensor("node_row", (NODE_ROWS, 1), I32, kind="Internal").ap()
        loaded, link, made, turned, flat_out, b_in, zeroed, zero_out = (sem(n) for n in (
            "loaded", "dve_link", "made", "turned", "flat_out", "b_in", "zeroed", "zero_out"))
        scattered, fetched, powers, cols_made = sem("scattered"), sem("fetched"), sem("powers"), sem("cols_made")
        block = ctx.enter_context(nc.Block())

        @block.sync
        def _(sp):
            for k in range(3):
                sp.dma_start(near[k][:].rearrange("r e k -> r (e k)"),
                             pairs[k:k + NE, :].rearrange("(r e) k -> r (e k)", e=P)).then_inc(loaded, 16)
            sp.wait_ge(zeroed, 1)
            sp.dma_start(node_row.rearrange("(p f) o -> p (f o)", p=P), zero[:]).then_inc(zero_out, 16)
            sp.wait_ge(made, 1)
            sp.dma_start(flat.rearrange("(r e) -> r e", e=P), d[1][:]).then_inc(flat_out, 16)
            sp.wait_ge(flat_out, 16)
            sp.dma_start(bc[:], flat.partition_broadcast(P)).then_inc(b_in, 16)

        @block.gpsimd
        def _(pool):
            pool.wait_ge(cols_made, 1)
            pool.tensor_tensor(g["norm"][:], cols[:, 2, :], half[:], ALU.pow).then_inc(powers, 1)
            pool.wait_ge(cols_made, 2)
            pool.tensor_tensor(g["dinv"][:], deg1[:], half[:], ALU.pow).then_inc(powers, 1)
            pool.wait_ge(zero_out, 16)
            pool.wait_ge(cols_made, 3)
            for t in range(NT):
                pool.indirect_dma_start(node_row, bass.IndirectOffsetOnAxis(g["last"][:, t:t + 1], 0),
                                        c["slot1"][:, t:t + 1], None, bounds_check=NODE_ROWS - 1,
                                        oob_is_err=False).then_inc(scattered, 16)
            pool.wait_ge(scattered, 16 * NT)
            for t in range(NT):
                pool.indirect_dma_start(found[:, t:t + 1], None, node_row,
                                        bass.IndirectOffsetOnAxis(g["src"][:, t:t + 1], 0),
                                        bounds_check=N - 1, oob_is_err=False).then_inc(fetched, 16)

        @block.tensor
        def _(pe):
            pe.wait_ge(made, 2)
            pe.transpose(ps[0][0:1, 0:NT], f_idx[:, P - 1:P], w["ident"][0:NT, 0:NT])
            pe.transpose(ps[1][0:1, 0:NT], l_idx[:, 0:1], w["ident"][0:NT, 0:NT]).then_inc(turned, 1)
            pe.wait_ge(made, 3)
            pe.transpose(ps[2][0:NT, 0:1], carry_f[:, 0:NT], w["ident"][0:1, 0:1])
            pe.transpose(ps[3][0:NT, 0:1], carry_l[:, 1:NT + 1], w["ident"][0:1, 0:1]).then_inc(turned, 1)
            pe.wait_ge(made, 4)
            for k in range(5):
                ins = pe.transpose(ps[(4, 5, 0, 1, 4)[k]][:, (0, 0, 0, 0, 128)[k]:(0, 0, 0, 0, 128)[k] + NT],
                                   out_r[:, k, :], w["ident"][0:NT, 0:NT])
            ins.then_inc(turned, 1)

        @block.vector
        def _(dve):
            n = [0]

            def linked(ins):
                n[0] += 1
                ins.then_inc(link, 1)
                dve.wait_ge(link, n[0])

            BIG = float(4 * NE)
            dve.memset(half[:], -0.5)
            dve.memset(far[:], float(FAR))
            dve.memset(carry_f[:], 0.0)
            dve.memset(carry_l[:], BIG)
            dve.memset(g["cont"][:, 0:P], 0)
            dve.memset(zero[:], 0).then_inc(zeroed, 1)
            dve.wait_ge(loaded, 48)
            dve.tensor_copy(d[0][:], near[0][:, :, 0])
            dve.tensor_copy(d[2][:], near[2][:, :, 0])
            dve.tensor_copy(out_r[:, 1, :], near[1][:, :, 1])
            dve.tensor_copy(d[1][:], near[1][:, :, 0]).then_inc(made, 1)
            dve.wait_ge(made, 1)
            dve.tensor_tensor(first[:], d[1][:], d[0][:], ALU.not_equal)
            linked(dve.tensor_tensor(last[:], d[1][:], d[2][:], ALU.not_equal))
            dve.tensor_tensor(f_idx[:], first[:], c["pos1"][0:NT, :], ALU.mult)
            linked(dve.tensor_tensor(l_idx[:], last[:], c["pos1"][0:NT, :], ALU.mult))
            linked(dve.tensor_scalar(far[:], last[:], -BIG, BIG, ALU.mult, ALU.add))
            linked(dve.tensor_tensor(l_idx[:], l_idx[:], far[:], ALU.add))
            linked(dve.tensor_tensor_scan(f_idx[:], f_idx[:], f_idx[:], 0.0, ALU.max, ALU.max))
            dve.tensor_tensor_scan(l_idx[:, ::-1], l_idx[:, ::-1], l_idx[:, ::-1], BIG, ALU.min,
                                   ALU.min).then_inc(made, 1)
            dve.wait_ge(turned, 1)
            dve.tensor_copy(row_f[:, 0:NT], ps[0][0:1, 0:NT])
            linked(dve.tensor_copy(row_l[:, 0:NT], ps[1][0:1, 0:NT]))
            dve.tensor_tensor_scan(carry_f[:, 1:NT + 1], row_f[:, 0:NT], row_f[:, 0:NT], 0.0, ALU.max, ALU.max)
            dve.tensor_tensor_scan(carry_l[:, 0:NT][:, ::-1], row_l[:, 0:NT][:, ::-1], row_l[:, 0:NT][:, ::-1], BIG,
                                   ALU.min, ALU.min).then_inc(made, 1)
            dve.wait_ge(turned, 2)
            dve.tensor_copy(back_f[:], ps[2][0:NT, 0:1])
            linked(dve.tensor_copy(back_l[:], ps[3][0:NT, 0:1]))
            dve.tensor_scalar(f_idx[:], f_idx[:], back_f[:], None, ALU.max)
            linked(dve.tensor_scalar(l_idx[:], l_idx[:], back_l[:], None, ALU.min))
            linked(dve.tensor_tensor(out_r[:, 2, :], l_idx[:], f_idx[:], ALU.subtract))
            dve.tensor_scalar(out_r[:, 2, :], out_r[:, 2, :], 1.0, None, ALU.add)
            dve.tensor_copy(out_r[:, 0, :], d[1][:])
            dve.tensor_scalar(out_r[:, 4, :], d[1][:], float(N - 1), None, ALU.min)
            linked(dve.tensor_scalar(far[:], last[:], -float(FAR), float(FAR), ALU.mult, ALU.add))
            dve.tensor_tensor(out_r[:, 3, :], d[1][:], far[:], ALU.add).then_inc(made, 1)
            dve.wait_ge(turned, 3)
            for k in range(5):
                ins = dve.tensor_copy(cols[:, k, :], ps[(4, 5, 0, 1, 4)[k]][:, (0, 0, 0, 0, 128)[k]:(0, 0, 0, 0, 128)[k] + NT])
            ins.then_inc(cols_made, 1)
            dve.wait_ge(cols_made, 1)
            dve.tensor_scalar(deg1[:], cols[:, 2, :], 1.0, None, ALU.add).then_inc(cols_made, 1)
            dve.tensor_copy(g["src"][:], cols[:, 1, :])
            dve.tensor_copy(g["dst"][:], cols[:, 4, :])
            dve.tensor_copy(g["last"][:], cols[:, 3, :]).then_inc(cols_made, 1)
            linked(dve.reciprocal(g["inv_deg"][:], cols[:, 2, :]))
            dve.wait_ge(powers, 2)
            dve.tensor_tensor(g["root_deg"][:], cols[:, 2, :], g["norm"][:], ALU.mult)
            dve.tensor_tensor(g["f1"][:], cols[:, 2, :], g["dinv"][:], ALU.mult)
            dve.wait_ge(b_in, 16)
            for t in range(NT):
                e = slice(t * P, (t + 1) * P)
                dve.tensor_scalar(g["mean"][:, e], bc[:, e], cols[:, 0, t:t + 1], g["inv_deg"][:, t:t + 1],
                                  ALU.is_equal, ALU.mult)
                if t:
                    dve.tensor_scalar(g["cont"][:, e], bc[:, e], bc[:, t * P - 1:t * P], None, ALU.is_equal)
            dve.wait_ge(fetched, 16 * NT)
            linked(dve.tensor_copy(found_f[:], found[:]))
            linked(dve.tensor_scalar(tmp[:], found_f[:], 0.0, float(FAR), ALU.is_equal, ALU.mult))
            linked(dve.tensor_tensor(tmp[:], tmp[:], found_f[:], ALU.add))
            linked(dve.tensor_scalar(tmp[:], tmp[:], -1.0, None, ALU.add))
            linked(dve.tensor_copy(g["row"][:], tmp[:]))


def edge_table_tiles(sb):
    g = {}
    for name in ("inv_deg", "norm", "root_deg", "dinv", "f1"):
        g[name] = sb("g_" + name, [P, NT], F32)
    for name in ("src", "dst", "last", "row"):
        g[name] = sb("g_" + name, [P, NT], I32)
    g["mean"] = sb("g_mean", [P, NE], F32)
    g["cont"] = sb("g_cont", [P, NE], U8)
    return g


def slot_pass(nc, a, w, c, g, kind, shared, table=None, ahead=None, out_table=None, xd=None, rows_in=None, layer=0):
    U = 5
    passes = NCH // U
    last = passes - 1
    gcn = kind in ("gcn1", "gcn2", "gcn3")
    width = HG if gcn else D
    YT, own = shared["YT"], shared["own"]
    LN = ["st", "ag", "ve", "xn"]
    final_layer = kind == "layer" and layer == LAYERS - 1
    if kind == "start":
        PE_, ACT_, DVE_ = ["t"], ["h"], LN + ["row"]
    elif final_layer:
        PE_, ACT_, DVE_ = ["agg", "l", "tx", "t", "g"], ["e", "h"], ["m", "h", "x"] + LN + ["row"]
    elif kind == "layer":
        PE_, ACT_, DVE_ = ["agg", "l", "tx"], ["e", "y"], ["m", "h", "row"]
    elif kind == "gcn1":
        PE_, ACT_, DVE_ = ["agg", "tr"], ["s"], ["a", "b", "u", "ub", "sg", "row"]
    elif kind == "gcn2":
        PE_, ACT_, DVE_ = ["agg", "tr", "tu", "z"], ["uT", "s"], ["a", "b", "u", "ub", "sg", "row"]
    elif kind == "gcn3":
        PE_, ACT_, DVE_ = ["agg", "tr", "tu", "z", "tx", "t"], ["uT", "tT", "h"], ["a", "b", "u", "x"] + LN + ["row"]
    elif kind == "edge":
        PE_ = ["tv", "ma", "mb", "mc", "md", "m3", "agg", "na", "nb", "up", "tx"]
        ACT_ = ["vT", "ma", "mb", "mc", "md", "na", "nb", "uT"]
        DVE_ = ["msg", "xa", "x"] + LN + ["row", "c"]
    elif kind == "hop":
        PE_, ACT_, DVE_ = ["agg", "tx"], [], ["row"]
    elif kind == "last_hop":
        PE_, ACT_, DVE_ = ["agg", "tx"], [], ["row", "o"]
    has_x = kind in ("gcn3", "edge", "last_hop") or final_layer
    makes_x = kind in ("start", "gcn3", "edge") or final_layer
    has_ln = "xn" in DVE_
    name = kind + str(layer)
    with Phase(nc) as ctx:
        def sb(n, shape, dt=F32, when=True):
            return [ctx.enter_context(nc.sbuf_tensor(f"{name}_{n}{u}", shape, dt)) for u in range(U)] if when else None
        sem = lambda n: ctx.sem(f"{name}_{n}")
        per_u = lambda n: [sem(f"{n}{u}") for u in range(U)]
        pair = lambda n: sb(n, [P, 2, CH])
        half_of = lambda tiles_, k: [t[:, k, :] for t in tiles_]
        wide = lambda n: sb(n, [P, CH])
        aggT = ex = em = hT = rows = xn = xr = mA = mB = hr = None
        if kind == "start":
            xr, xn, rows = wide("xr"), wide("xn"), wide("rows")
        elif kind == "layer":
            V, aggT, em, hT = wide("V"), wide("aggT"), wide("em"), wide("hT")
            ex, xn = aggT, em
            if final_layer:
                xr = wide("xr")
            else:
                rows = wide("rows")
        elif gcn:
            V, aggT = sb("V", [P, P]), wide("aggT")
            if kind == "gcn3":
                xr, xn, rows = wide("xr"), wide("xn"), wide("rows")
                ex = xn
        elif kind == "edge":
            mB, mA, hT, xr, hr = pair("mB"), pair("mA"), wide("hT"), wide("xr"), wide("hr")
            V, aggT = half_of(mB, 0), half_of(mB, 1)
            em, ex, xn, rows = half_of(mA, 0), half_of(mA, 1), hT, hr
        else:
            V, aggT, rows = wide("V"), wide("aggT"), wide("rows")
            if kind == "last_hop":
                xr, em = wide("xr"), wide("em")
        tail = ctx.enter_context(nc.sbuf_tensor(f"{name}_tail", [P, 1], F32))
        bA, bB, bU, bT = (sb(n, [P, P], when=gcn) for n in ("bA", "bB", "bU", "bT"))
        st, mv, ve, rs = sb("st", [P, TPC, 6]), sb("mv", [P, TPC, 2]), sb("ve", [P, TPC]), sb("rs", [P, TPC])
        idx = sb("idx", [P, TPC], I32)
        idx2 = sb("idx2", [P, TPC], I32, when=kind == "last_hop")
        ps = [ctx.enter_context(nc.psum_tensor(f"{name}_ps{u}", [P, CH], F32)) for u in range(U)]
        pe_ev, act_ev, dve_ev = (Events(sem(n), names or ["none"], U, 1) for n, names in (
            ("pe_done", PE_), ("act_done", ACT_), ("dve_done", DVE_)))
        carried = Events(sem("carried"), ["c"], U * TPC + 1, 1)
        pool_ev = Events(sem("pool_done"), (["idx"] if True else []) + (["rs"] if has_ln else []), U, 1)
        z_in, v_in, x_in, row_out, x_out = (per_u(n) for n in ("z_in", "v_in", "x_in", "row_out", "x_out"))
        held, link, idx2_made = sem("held"), sem("link"), sem("idx2_made")
        block = ctx.enter_context(nc.Block())

        def wait(eng, ev, i, what, u, before=0):
            eng.wait_ge(ev.sem, ev.at(i, what, u, before))

        def chunk_rows(t, i, u):
            return t[bass.ds(i * (U * CH) + u * CH, CH), :].rearrange("(p t) f -> p (t f)", t=TPC)

        def cols(i, u, t=0, n=CH):
            return bass.ds(i * (U * CH) + (u * CH + t * P), n)

        def factors(name, i, u):
            f = g[name][:, bass.ds(i * (U * TPC) + u * TPC, TPC)]
            return f.unsqueeze(2).to_broadcast([P, TPC, HG])

        def factor(name, i, u, t):
            return g[name][:, bass.ds(i * (U * TPC) + (u * TPC + t), 1)]

        def by_tile(ap):
            return ap.rearrange("p (t f) -> p t f", t=TPC)

        def own_of(i, u):
            return own[:, bass.ds(i * (U * P) + u * P, P)]

        @block.sync
        def _(sp):
            for u in range(U):
                sp.sem_inc(x_out[u], 16)
                if kind != "last_hop":
                    sp.sem_inc(row_out[u], 16)

            def prefill(i):
                for u in range(U):
                    wait(sp, pe_ev, i, "agg", u, before=1)
                    sp.dma_start(V[u][:, 0:TPC * width], chunk_rows(ahead, i, u)).then_inc(z_in[u], 16)

            def load_x(i):
                for u in range(U):
                    if kind == "last_hop":
                        wait(sp, dve_ev, i, "o", u, before=1)
                    else:
                        sp.wait_ge(x_out[u], i * 16 + 16)
                    sp.dma_start(xr[u][:], chunk_rows(xd, i, u)).then_inc(x_in[u], 16)
                    if kind == "edge":
                        sp.wait_ge(row_out[u], i * 16 + 16)
                        sp.sem_inc(held, 1)
                        wait(sp, dve_ev, i, "c", u, before=1)
                        sp.sem_inc(held, 1)
                        sp.dma_start(hr[u][:], chunk_rows(rows_in, i, u)).then_inc(x_in[u], 16)

            def store(i):
                for u in range(U):
                    if makes_x:
                        wait(sp, dve_ev, i, "st" if kind == "start" else "x", u)
                        sp.dma_start(chunk_rows(xd, i, u), xr[u][:]).then_inc(x_out[u], 16)
                for u in range(U):
                    if kind != "last_hop":
                        wait(sp, dve_ev, i, "row", u)
                        src = own_of(i, u) if kind in ("gcn1", "gcn2") or final_layer else rows[u][:]
                        sp.dma_start(chunk_rows(out_table, i, u), src).then_inc(row_out[u], 16)

            if kind != "start":
                prefill(0)
            with sp.Fori(0, last) as i:
                if has_x:
                    load_x(i)
                if kind != "start":
                    prefill(i + 1)
                store(i)
            if has_x:
                load_x(last)
            store(last)
            for u in range(U):
                if makes_x:
                    sp.wait_ge(x_out[u], 16 * passes + 16)
                if kind != "last_hop":
                    sp.wait_ge(row_out[u], 16 * passes + 16)

        @block.gpsimd
        def _(pool):
            bound = pool.to_reg((N if kind == "start" else NE) - 1)
            out_bound = pool.to_reg(N - 1)
            pool.sem_inc(pool_ev.sem, pool_ev.size)

            def copy_indices(i):
                for u in range(U):
                    if kind == "start":
                        wait(pool, dve_ev, i, "st", u, before=1)
                    else:
                        wait(pool, pe_ev, i, "agg", u, before=1)
                    what = g["dst" if kind == "start" else "row"]
                    pool.tensor_copy(idx[u][:], what[:, bass.ds(i * (U * TPC) + u * TPC, TPC)]).then_inc(pool_ev.sem, 1)

            def gather(i):
                for u in range(U):
                    wait(pool, pool_ev, i, "idx", u)
                    if kind == "start":
                        pool.wait_ge(x_out[u], i * 16 + 16)
                        wait(pool, dve_ev, i, "xn", u, before=1)
                    else:
                        pool.wait_ge(z_in[u], (i + 1) * 16)
                    pool.sem_inc(held, 1)
                    to, sem_, of = (xr[u], x_in[u], a["x"]) if kind == "start" else (V[u], v_in[u], table)
                    for t in range(TPC):
                        pool.indirect_dma_start(to[:, t * width:(t + 1) * width], None, of,
                                                bass.IndirectOffsetOnAxis(idx[u][:, t:t + 1], 0),
                                                bounds_check=bound, oob_is_err=False).then_inc(sem_, 16)

            def rest(i):
                if has_ln:
                    for u in range(U):
                        wait(pool, dve_ev, i, "ve", u)
                        pool.tensor_tensor(rs[u][:], ve[u][:], w["power"][:, 0:TPC], ALU.pow).then_inc(pool_ev.sem, 1)
                if kind == "last_hop":
                    for u in range(U):
                        if not isinstance(i, int):
                            pool.wait_ge(row_out[u], i * 64)
                        pool.tensor_copy(idx2[u][:], g["last"][:, bass.ds(i * (U * TPC) + u * TPC, TPC)]).then_inc(idx2_made, 1)
                        pool.wait_ge(idx2_made, i * U + (u + 1))
                        wait(pool, dve_ev, i, "o", u)
                        pool.sem_inc(held, 1)
                        for t in range(TPC):
                            pool.indirect_dma_start(a["out"], bass.IndirectOffsetOnAxis(idx2[u][:, t:t + 1], 0),
                                                    em[u][:, t * D:(t + 1) * D], None,
                                                    bounds_check=out_bound, oob_is_err=False).then_inc(row_out[u], 16)

            def body(i):
                copy_indices(i)
                gather(i)
                rest(i)

            if kind == "last_hop":
                body(0)
            with pool.Fori(1 if kind == "last_hop" else 0, passes) as i:
                body(i)
            if kind == "last_hop":
                for u in range(U):
                    pool.wait_ge(row_out[u], 64 * passes)

        @block.tensor
        def _(pe):
            pe.sem_inc(pe_ev.sem, pe_ev.size)

            def done(ins):
                ins.then_inc(pe_ev.sem, 1)

            def turn(src, u):
                for t in range(TPC):
                    e = slice(t * P, (t + 1) * P)
                    ins = pe.transpose(ps[u][:, e], src[:, e], w["ident"][:])
                done(ins)

            def body(i):
                us = range(U)
                if kind == "edge":
                    for u in us:
                        pe.wait_ge(v_in[u], i * 64 + 64)
                        wait(pe, dve_ev, i, "xa", u, before=1)
                        turn(V[u], u)
                    for b, what in ((0, "ma"), (1, "mb")):
                        for u in us:
                            wait(pe, act_ev, i, "vT" if b == 0 else "ma", u)
                            pe.matmul(ps[u][:], w["wm1"][:, 0, b * P:(b + 1) * P], hT[u][:], start=True, stop=False)
                            done(pe.matmul(ps[u][:], w["wm1"][:, 1, b * P:(b + 1) * P], YT[:, cols(i, u)],
                                           start=False, stop=True))
                    for b, what in ((0, "mc"), (1, "md")):
                        for u in us:
                            wait(pe, act_ev, i, "mb" if b == 0 else "mc", u)
                            for k in range(2):
                                ins = pe.matmul(ps[u][:], w["wm2"][:, k, b * P:(b + 1) * P], mA[u][:, k, :],
                                                start=k == 0, stop=k == 1)
                            done(ins)
                    for u in us:
                        wait(pe, act_ev, i, "md", u)
                        for t in range(TPC):
                            e = slice(t * P, (t + 1) * P)
                            for k in range(2):
                                ins = pe.matmul(ps[u][:, e], mB[u][:, k, e], w["wm3"][:, k, :], start=k == 0, stop=k == 1)
                        done(ins)
                if kind != "start":
                    for u in us:
                        if kind == "edge":
                            wait(pe, dve_ev, i, "msg", u)
                        else:
                            pe.wait_ge(v_in[u], i * 64 + 64)
                            if before_agg is not None:
                                wait(pe, before_agg[0], i, before_agg[1], u, before=1)
                        for t in range(TPC):
                            ins = pe.matmul(ps[u][0:width, t * P:(t + 1) * P], V[u][:, t * width:(t + 1) * width],
                                            g["mean"][:, cols(i, u, t, P)], start=True, stop=True)
                        done(ins)
                if kind == "layer":
                    for u in us:
                        wait(pe, carried, i, "c", u * TPC + TPC)
                        pe.matmul(ps[u][:], w["rel"][:, layer, :], aggT[u][:], start=True, stop=False)
                        done(pe.matmul(ps[u][:], w["root"][:, layer, :], YT[:, cols(i, u)], start=False, stop=True))
                    for u in us:
                        wait(pe, dve_ev, i, "h", u)
                        turn(hT[u], u)
                if gcn:
                    for u in us:
                        wait(pe, carried, i, "c", u * TPC + TPC)
                        pe.sem_inc(held, 1)
                        for t in range(TPC):
                            ins = pe.transpose(ps[u][:, t * HG:(t + 1) * HG], aggT[u][0:HG, t * P:(t + 1) * P],
                                               w["ident"][0:HG, 0:HG])
                        done(ins)
                if kind in ("gcn2", "gcn3"):
                    for u in us:
                        wait(pe, dve_ev, i, "u", u)
                        done(pe.transpose(ps[u][:, 0:P], bU[u][:], w["ident"][:]))
                    for u in us:
                        wait(pe, act_ev, i, "uT", u)
                        if kind == "gcn2":
                            ins = pe.matmul(ps[u][:, 0:P], bT[u][:], w["bd2"][:], start=True, stop=True)
                        else:
                            for t in range(TPC):
                                ins = pe.matmul(ps[u][:, t * P:(t + 1) * P], w["wc"][:, t, :], bT[u][:],
                                                start=True, stop=True)
                        done(ins)
                if kind == "gcn3":
                    for u in us:
                        wait(pe, act_ev, i, "tT", u)
                        turn(ex[u], u)
                if kind == "edge":
                    for b, what in ((0, "na"), (1, "nb")):
                        for u in us:
                            if b == 0:
                                wait(pe, carried, i, "c", u * TPC + TPC)
                            else:
                                wait(pe, act_ev, i, "na", u)
                            pe.matmul(ps[u][:], w["wn1"][:, 1, b * P:(b + 1) * P], aggT[u][:], start=True, stop=False)
                            done(pe.matmul(ps[u][:], w["wn1"][:, 0, b * P:(b + 1) * P], YT[:, cols(i, u)],
                                           start=False, stop=True))
                    for u in us:
                        wait(pe, act_ev, i, "nb", u)
                        for k in range(2):
                            ins = pe.matmul(ps[u][:], w["wn2"][:, k, :], mA[u][:, k, :], start=k == 0, stop=k == 1)
                        done(ins)
                    for u in us:
                        wait(pe, act_ev, i, "uT", u)
                        turn(em[u], u)
                if kind in ("hop", "last_hop"):
                    for u in us:
                        wait(pe, carried, i, "c", u * TPC + TPC)
                        turn(aggT[u], u)
                if kind in ("start", "gcn3") or final_layer:
                    for u in us:
                        wait(pe, dve_ev, i, "xn", u)
                        if kind == "start":
                            wait(pe, act_ev, i, "h", u, before=1)
                        turn(xn[u], u)
                if final_layer:
                    for u in us:
                        wait(pe, act_ev, i, "h", u)
                        for t in range(TPC):
                            ins = pe.matmul(ps[u][:, t * HG:(t + 1) * HG], hT[u][:, t * P:(t + 1) * P], w["w1"][:],
                                            start=True, stop=True)
                        done(ins)

            before_agg = {"layer": (dve_ev, "row"), "gcn1": (dve_ev, "a"), "gcn2": (dve_ev, "ub"),
                          "gcn3": (act_ev, "h"), "hop": (dve_ev, "row"), "last_hop": (dve_ev, "row")}.get(kind)
            with pe.Fori(0, passes) as i:
                body(i)

        @block.scalar
        def _(act):
            act.sem_inc(act_ev.sem, act_ev.size)

            def step(i, what, to, func, producer, n=CH, **kw):
                for u in range(U):
                    wait(act, pe_ev, i, producer, u)
                    act.activation(to(u), ps[u][:, 0:n], func, **kw).then_inc(act_ev.sem, 1)

            def body(i):
                if kind == "start":
                    step(i, "h", lambda u: YT[:, cols(i, u)], ACT.Relu, "t")
                if kind == "layer":
                    step(i, "e", lambda u: ex[u][:], ACT.Exp, "l", bias=w["b_rel"][:, layer:layer + 1])
                    if not final_layer:
                        for u in range(U):
                            wait(act, dve_ev, i, "h", u)
                            act.activation(YT[:, cols(i, u)], hT[u][:], ACT.Identity).then_inc(act_ev.sem, 1)
                    else:
                        step(i, "h", lambda u: hT[u][:], ACT.Relu, "t")
                if kind in ("gcn2", "gcn3"):
                    step(i, "uT", lambda u: bT[u][:], ACT.Identity, "tu", P)
                if kind in ("gcn1", "gcn2"):
                    for u in range(U):
                        wait(act, dve_ev, i, "ub", u)
                        act.activation(bA[u][:], bU[u][:], ACT.Tanh, scale=0.5).then_inc(act_ev.sem, 1)
                if kind == "gcn3":
                    step(i, "tT", lambda u: ex[u][:], ACT.Tanh, "z", bias=w["dst_bz"][:], scale=0.5)
                    step(i, "h", lambda u: YT[:, cols(i, u)], ACT.Relu, "t")
                if kind == "edge":
                    for u in range(U):
                        wait(act, dve_ev, i, "row", u, before=1)
                        wait(act, pe_ev, i, "tv", u)
                        act.activation(hT[u][:], ps[u][:], ACT.Identity).then_inc(act_ev.sem, 1)
                    for b, what in ((0, "ma"), (1, "mb")):
                        step(i, what, lambda u, b=b: mA[u][:, b, :], ACT.Relu, what, bias=w["bm1"][:, b:b + 1])
                    for b, what in ((0, "mc"), (1, "md")):
                        step(i, what, lambda u, b=b: mB[u][:, b, :], ACT.Relu, what, bias=w["bm2"][:, b:b + 1])
                    for b, what in ((0, "na"), (1, "nb")):
                        step(i, what, lambda u, b=b: mA[u][:, b, :], ACT.Relu, what, bias=w["bn1"][:, b:b + 1])
                    step(i, "uT", lambda u: em[u][:], ACT.Identity, "up", bias=w["bn2h"][:])

            if ACT_:
                with act.Fori(0, passes) as i:
                    body(i)

        @block.vector
        def _(dve):
            dve.sem_inc(dve_ev.sem, dve_ev.size)
            dve.sem_inc(carried.sem, carried.size)

            def done(ins):
                ins.then_inc(dve_ev.sem, 1)

            def carry(i):
                for u in range(U):
                    wait(dve, pe_ev, i, "agg", u)
                    for t in range(TPC):
                        wait(dve, carried, i, "c", u * TPC + t - 1)
                        before = (aggT[u][0:width, t * P - 1:t * P] if t else
                                  aggT[u - 1][0:width, CH - 1:CH] if u else tail[0:width, :])
                        e = slice(t * P, (t + 1) * P)
                        dve.scalar_tensor_tensor(out=aggT[u][0:width, e], in0=g["cont"][0:width, cols(i, u, t, P)],
                                                 scalar=before, in1=ps[u][0:width, e], op0=ALU.mult,
                                                 op1=ALU.add).then_inc(carried.sem, 1)
                wait(dve, carried, i, "c", U * TPC - 1)
                dve.tensor_copy(tail[0:width, :], aggT[U - 1][0:width, CH - 1:CH]).then_inc(carried.sem, 1)

            def layernorm(i, x, before):
                for u in range(U):
                    if before == "x_in":
                        dve.wait_ge(x_in[u], 64 * i + 64)
                    else:
                        wait(dve, dve_ev, i, before, u)
                    for t in range(TPC):
                        ins = dve.bn_stats(st[u][:, t, :], x[u][:, t * D:(t + 1) * D])
                    done(ins)
                wait(dve, dve_ev, i, "st", U - 1)
                dve.sem_inc(held, 1)
                for u in range(U):
                    for t in range(TPC):
                        ins = dve.bn_aggr(mv[u][:, t, :], st[u][:, t, :])
                    done(ins)
                for u in range(U):
                    wait(dve, dve_ev, i, "ag", u)
                    done(dve.tensor_scalar(ve[u][:], mv[u][:, :, 1], EPS, None, ALU.add))
                for u in range(U):
                    wait(dve, pool_ev, i, "rs", u)
                    if kind == "start":
                        wait(dve, pe_ev, i, "t", u, before=1)
                    for t in range(TPC):
                        e = slice(t * D, (t + 1) * D)
                        ins = dve.tensor_scalar(xn[u][:, e], x[u][:, e], mv[u][:, t, 0:1], rs[u][:, t:t + 1],
                                                ALU.subtract, ALU.mult)
                    done(ins)

            def body(i):
                us = range(U)
                if kind == "start":
                    layernorm(i, xr, "x_in")
                    for u in us:
                        wait(dve, dve_ev, i, "xn", u)
                        dve.wait_ge(row_out[u], 16 * i + 16)
                        done(dve.tensor_scalar(rows[u][:], xn[u][:], 0.0, None, ALU.max))
                    return
                if kind == "edge":
                    for u in us:
                        wait(dve, pe_ev, i, "m3", u)
                        done(dve.tensor_tensor(by_tile(V[u][:]), by_tile(ps[u][:]),
                                               w["bm3row"][:].unsqueeze(1).to_broadcast([P, TPC, D]), ALU.add))
                carry(i)
                if kind == "layer":
                    for u in us:
                        wait(dve, act_ev, i, "e", u)
                        done(dve.tensor_scalar(em[u][:], ex[u][:], 1.0, -1.0, ALU.min, ALU.add))
                    for u in us:
                        wait(dve, dve_ev, i, "m", u)
                        if not final_layer:
                            wait(dve, act_ev, i, "y", u, before=1)
                        done(dve.scalar_tensor_tensor(out=hT[u][:], in0=ps[u][:], scalar=w["b_rel"][:, layer:layer + 1],
                                                      in1=em[u][:], op0=ALU.add, op1=ALU.max))
                    if not final_layer:
                        for u in us:
                            wait(dve, pe_ev, i, "tx", u)
                            dve.wait_ge(row_out[u], 16 * i + 16)
                            done(dve.tensor_copy(rows[u][:], ps[u][:]))
                    else:
                        for u in us:
                            wait(dve, pe_ev, i, "tx", u)
                            dve.wait_ge(x_in[u], 16 * (i + 1))
                            done(dve.tensor_tensor(xr[u][:], ps[u][:], xr[u][:], ALU.add))
                        layernorm(i, xr, "x")
                        for u in us:
                            wait(dve, pe_ev, i, "g", u)
                            done(dve.tensor_tensor(by_tile(own_of(i, u)), by_tile(ps[u][:, 0:P]), factors("dinv", i, u),
                                                   ALU.mult))
                if gcn:
                    for u in us:
                        wait(dve, pe_ev, i, "tr", u)
                        if kind != "gcn3":
                            wait(dve, dve_ev, i, "sg", u, before=1)
                        done(dve.tensor_tensor(by_tile(bA[u][:]), by_tile(ps[u][:, 0:P]), factors("f1", i, u), ALU.mult))
                    for u in us:
                        done(dve.tensor_tensor(by_tile(bB[u][:]), by_tile(own_of(i, u)), factors("dinv", i, u), ALU.mult))
                    for u in us:
                        wait(dve, dve_ev, i, "b", u)
                        done(dve.tensor_tensor(bU[u][:], bA[u][:], bB[u][:], ALU.add))
                if kind in ("gcn1", "gcn2"):
                    for u in us:
                        if kind == "gcn1":
                            wait(dve, dve_ev, i, "u", u)
                        else:
                            wait(dve, pe_ev, i, "z", u)
                        done(dve.tensor_tensor(by_tile(bU[u][:]), by_tile(bU[u][:] if kind == "gcn1" else ps[u][:, 0:P]),
                                               w["b1row" if kind == "gcn1" else "b2row"][:].unsqueeze(1)
                                               .to_broadcast([P, TPC, HG]), ALU.add))
                    for u in us:
                        wait(dve, act_ev, i, "s", u)
                        done(dve.tensor_scalar(bB[u][:], bA[u][:], 0.5, 0.5, ALU.mult, ALU.add))
                    for u in us:
                        wait(dve, dve_ev, i, "sg", u)
                        done(dve.tensor_tensor(by_tile(own_of(i, u)), by_tile(bB[u][:]), factors("dinv", i, u), ALU.mult))
                if kind == "gcn3":
                    for u in us:
                        wait(dve, pe_ev, i, "tx", u)
                        dve.wait_ge(x_in[u], 16 * (i + 1))
                        done(dve.scalar_tensor_tensor(out=xr[u][:], in0=ps[u][:], scalar=0.5, in1=xr[u][:],
                                                      op0=ALU.mult, op1=ALU.add))
                    layernorm(i, xr, "x")
                    for u in us:
                        wait(dve, dve_ev, i, "xn", u)
                        dve.wait_ge(row_out[u], 16 * i + 16)
                        done(dve.tensor_scalar(rows[u][:], xn[u][:], 0.0, None, ALU.max))
                if kind == "edge":
                    for u in us:
                        wait(dve, pe_ev, i, "tx", u)
                        dve.wait_ge(x_in[u], 32 * (i + 1))
                        done(dve.tensor_tensor(ex[u][:], ps[u][:], hr[u][:], ALU.add))
                    for u in us:
                        wait(dve, dve_ev, i, "xa", u)
                        done(dve.tensor_tensor(xr[u][:], xr[u][:], ex[u][:], ALU.add))
                    layernorm(i, xr, "x")
                    for u in us:
                        wait(dve, dve_ev, i, "xn", u)
                        dve.wait_ge(row_out[u], 16 * i + 16)
                        for t in range(TPC):
                            e = slice(t * D, (t + 1) * D)
                            ins = dve.tensor_scalar(rows[u][:, e], xn[u][:, e], 0.0, factor("norm", i, u, t),
                                                    ALU.max, ALU.mult)
                        done(ins)
                    for u in us:
                        wait(dve, dve_ev, i, "row", u)
                        done(dve.tensor_scalar(YT[:, cols(i, u)], rows[u][:], ALPHA, None, ALU.mult))
                if kind in ("hop", "last_hop"):
                    to = rows
                    for u in us:
                        wait(dve, pe_ev, i, "tx", u)
                        if kind == "hop":
                            dve.wait_ge(row_out[u], 16 * i + 16)
                        done(dve.scalar_tensor_tensor(out=to[u][:], in0=ps[u][:], scalar=1.0 - ALPHA,
                                                      in1=YT[:, cols(i, u)], op0=ALU.mult, op1=ALU.add))
                    if kind == "last_hop":
                        for u in us:
                            wait(dve, dve_ev, i, "row", u)
                            dve.wait_ge(x_in[u], 16 * (i + 1))
                            if not isinstance(i, int):
                                dve.wait_ge(row_out[u], 64 * i)
                            for t in range(TPC):
                                e = slice(t * D, (t + 1) * D)
                                ins = dve.scalar_tensor_tensor(out=em[u][:, e], in0=rows[u][:, e],
                                                               scalar=factor("root_deg", i, u, t), in1=xr[u][:, e],
                                                               op0=ALU.mult, op1=ALU.add)
                            done(ins)

            if kind != "start":
                dve.memset(tail[:], 0.0).then_inc(link, 1)
                dve.wait_ge(link, 1)
            if kind == "last_hop":
                body(0)
            with dve.Fori(1 if kind == "last_hop" else 0, passes) as i:
                body(i)


def complete_slots(nc, YT, dst_flat):
    with Phase(nc) as ctx:
        bc = ctx.enter_context(nc.sbuf_tensor("fix_dst", [P, NE], F32))
        mask = ctx.enter_context(nc.sbuf_tensor("fix_mask", [P, P], F32))
        diff = ctx.enter_context(nc.sbuf_tensor("fix_diff", [P, P], F32))
        bc_in = ctx.sem("fix_dst_in")
        ev = Events(ctx.sem("fix_done"), ["mask", "diff", "slots"], 1, 1)
        block = ctx.enter_context(nc.Block())

        @block.sync
        def _(sp):
            sp.dma_start(bc[:], dst_flat.partition_broadcast(P)).then_inc(bc_in, 16)

        @block.vector
        def _(dve):
            dve.sem_inc(ev.sem, ev.size)
            dve.wait_ge(bc_in, 16)
            with dve.Fori(0, NT - 1) as i:
                tile, following = bass.ds((NT - 2) * P - i * P, P), bass.ds((NT - 1) * P - i * P, 1)
                dve.wait_ge(ev.sem, ev.at(i, "slots", 0, before=1))
                dve.tensor_scalar(mask[:], bc[:, tile], bc[:, following], None, ALU.is_equal).then_inc(ev.sem, 1)
                dve.wait_ge(ev.sem, ev.at(i, "mask", 0))
                dve.scalar_tensor_tensor(out=diff[:], in0=YT[:, tile], scalar=YT[:, following], in1=mask[:],
                                         op0=ALU.subtract, op1=ALU.mult).then_inc(ev.sem, 1)
                dve.wait_ge(ev.sem, ev.at(i, "diff", 0))
                dve.tensor_tensor(YT[:, tile], YT[:, tile], diff[:], ALU.subtract).then_inc(ev.sem, 1)


def gnn_kernel(nc, a):
    with ExitStack() as ctx:
        sb = lambda name, shape, dt: ctx.enter_context(nc.sbuf_tensor(name, shape, dt))
        dram = lambda name, shape, dt=F32: nc.dram_tensor(name, shape, dt, kind="Internal").ap()
        w = load_weights(nc, a, sb, None, None)
        isolated_rows(nc, a, w, "all", 7, 14)
        pairs = dram("pairs", (NE + 2, 2), I32)
        dst_flat = dram("dst_flat", (NE,))
        with ExitStack() as early:
            c = constants(nc, lambda name, shape, dt: early.enter_context(nc.sbuf_tensor("s" + name, shape, dt)), 0)
            sort_edges(nc, a, w, c, pairs)
        g = edge_table_tiles(sb)
        with ExitStack() as early:
            c = constants(nc, lambda name, shape, dt: early.enter_context(nc.sbuf_tensor(name, shape, dt)), 1)
            edge_tables(nc, a, w, c, pairs, g, dst_flat)
        taps = [dram(f"tap{k}", (NE, HG if k in (4, 5, 6) else D)) for k in range(10)]
        isolated_rows(nc, a, w, "src", 5, NCH // 5, taps, g["src"])
        shared = {"YT": sb("YT", [P, NE], F32), "own": None}
        xd = dram("xd", (NE, D))
        T = [dram(f"table{k}", (NE, HG if k in (4, 5, 6) else D)) for k in range(8)]
        H = [dram(f"hop_table{k}", (NE, D)) for k in range(2)]
        step = lambda kind, **kw: slot_pass(nc, a, w, c, g, kind, shared, **kw)
        step("start", out_table=T[0], xd=xd)
        for l in range(LAYERS - 1):
            step("layer", layer=l, table=T[l], ahead=taps[l], out_table=T[l + 1])
        with nc.sbuf_tensor("own", [P, NT * HG], F32) as own:
            shared["own"] = own
            step("layer", layer=LAYERS - 1, table=T[3], ahead=taps[3], out_table=T[4], xd=xd)
            step("gcn1", table=T[4], ahead=taps[4], out_table=T[5])
            step("gcn2", table=T[5], ahead=taps[5], out_table=T[6])
            step("gcn3", table=T[6], ahead=taps[6], out_table=T[7], xd=xd)
        complete_slots(nc, shared["YT"], dst_flat)
        step("edge", table=T[7], ahead=taps[7], out_table=H[0], xd=xd, rows_in=T[7])
        for k in range(HOPS - 1):
            step("hop", layer=k, table=H[k % 2], ahead=taps[8 if k == 0 else 9], out_table=H[(k + 1) % 2])
        step("last_hop", table=H[(HOPS - 1) % 2], ahead=taps[9], xd=xd)


_INS = ["x", "src", "dst", "L0_gnn_Ws_rel", "L0_gnn_bs_rel", "L0_gnn_Ws_root",
        "L1_gnn_W1", "L1_gnn_b1", "L1_gnn_W2", "L1_gnn_b2", "L1_gnn_W3", "L1_gnn_b3", "L1_gnn_Wlin", "L1_gnn_blin",
        "L2_gnn_Wm1", "L2_gnn_bm1", "L2_gnn_Wm2", "L2_gnn_bm2", "L2_gnn_Wm3", "L2_gnn_bm3",
        "L2_gnn_Wn1", "L2_gnn_bn1", "L2_gnn_Wn2", "L2_gnn_bn2"]


def kernel(**inputs):
    import numpy as _np
    import concourse.bacc as _bacc
    from concourse import mybir as _mybir
    from concourse.bass_utils import run_bass_kernel_spmd as _run

    nc = _bacc.Bacc("TRN2", target_bir_lowering=False, num_devices=1)
    arrays, aps = {}, {}
    for name in _INS:
        a = _np.ascontiguousarray(inputs[name])
        arrays[f"in_{name}"] = a
        aps[name] = nc.dram_tensor(f"in_{name}", a.shape, _mybir.dt.from_np(a.dtype), kind="ExternalInput").ap()
    aps["out"] = nc.dram_tensor("out_0", (50000, 128), _mybir.dt.float32, kind="ExternalOutput").ap()
    gnn_kernel(nc, aps)
    r = _run(nc, [arrays], core_ids=[0])
    return r.results[0]["out_0"]
```

```python
import numpy as np
import concourse.bass as bass
from concourse import mybir
from contextlib import ExitStack

F32 = mybir.dt.float32
I32 = mybir.dt.int32
U8 = mybir.dt.uint8
ALU = mybir.AluOpType
ACT = mybir.ActivationFunctionType

N = 50000
D = 128
E = 12500
HG = 32
LAYERS = 4
HOPS = 10
ALPHA = 0.1
EPS = 1e-5
P = 128
TPC = 4
CH = TPC * P
NCH = -(-E // CH)
NT = NCH * TPC
NE = NCH * CH
PAD = NE - E
FAR = 1 << 20
NODE_ROWS = -(-(N + 1) // P) * P


class Events:

    def __init__(self, sem, names, chunks, lead=0):
        self.sem, self.names, self.chunks, self.lead = sem, names, chunks, lead
        self.size = len(names) * chunks

    def at(self, i, name, u, before=0):
        return i * self.size + ((self.lead - before) * self.size + self.names.index(name) * self.chunks + u + 1)


def tiles(ap):
    return ap.rearrange("p (t f) -> p t f", t=TPC)


class Phase(ExitStack):

    def __init__(self, nc):
        super().__init__()
        self.nc, self.sems = nc, []
        self.callback(self.clear)

    def sem(self, name):
        self.sems.append(self.nc.alloc_semaphore(name))
        return self.sems[-1]

    def clear(self):
        self.nc.clear_and_free_semaphores(self.sems)
        self.nc.all_engine_barrier()


def load_weights(nc, a, sb, pb, sem):
    w = {}

    def tile(name, shape):
        w[name] = sb("w_" + name, shape, F32)
        return w[name]

    root, rel = tile("root", [P, LAYERS, D]), tile("rel", [P, LAYERS, D])
    b_rel = tile("b_rel", [P, LAYERS])
    w1, wlin = tile("w1", [P, HG]), tile("wlin", [HG, D])
    w3t = tile("w3t", [HG, TPC, HG])
    bd2, wc = tile("bd2", [P, P]), tile("wc", [P, TPC, D])
    b3 = tile("b3", [HG, 1])
    b1row, b2row, bm3row = tile("b1row", [P, HG]), tile("b2row", [P, HG]), tile("bm3row", [P, D])
    wm1, wm2, wm3 = tile("wm1", [P, 2, 256]), tile("wm2", [P, 2, 256]), tile("wm3", [P, 2, D])
    wn1, wn2 = tile("wn1", [P, 2, 256]), tile("wn2", [P, 2, D])
    bm1, bm2, bn1 = tile("bm1", [P, 2]), tile("bm2", [P, 2]), tile("bn1", [P, 2])
    raw = tile("raw", [P, 4])
    iso_b1, iso_b2, iso_bz = tile("iso_b1", [P, 1]), tile("iso_b2", [P, 1]), tile("iso_bz", [P, 1])
    dst_bz, bn2h = tile("dst_bz", [P, 1]), tile("bn2h", [P, 1])
    ones, ident = tile("ones", [P, 1]), tile("ident", [P, P])
    bz = tile("bz", [P, 1])
    power = tile("power", [P, CH // P * 2])
    with Phase(nc) as ctx:
        ps = ctx.enter_context(nc.psum_tensor("ps_setup", [P, 3, 512], F32))
        loaded, zeroed, made, folded, summed = (ctx.sem(s) for s in (
            "weights_loaded", "bd2_zeroed", "ident_made", "pe_folded", "dve_summed"))
        block = ctx.enter_context(nc.Block())
        column = lambda ap: ap.unsqueeze(1)
        plain = [
            (root[:], a["L0_gnn_Ws_root"].rearrange("l k m -> k l m")),
            (rel[:], a["L0_gnn_Ws_rel"].rearrange("l k m -> k l m")),
            (b_rel[:], a["L0_gnn_bs_rel"].rearrange("l m -> m l")),
            (w1[:], a["L1_gnn_W1"]), (wlin[:], a["L1_gnn_Wlin"]),
            (b3[:], column(a["L1_gnn_b3"])),
            (b1row[:], a["L1_gnn_b1"].partition_broadcast(P)), (b2row[:], a["L1_gnn_b2"].partition_broadcast(P)),
            (bm3row[:], a["L2_gnn_bm3"].partition_broadcast(P)),
            (wm1[:], a["L2_gnn_Wm1"].rearrange("(b k) m -> k b m", b=2)),
            (wm2[:], a["L2_gnn_Wm2"].rearrange("(b k) m -> k b m", b=2)),
            (wm3[:], a["L2_gnn_Wm3"].rearrange("(b k) m -> k b m", b=2)),
            (wn1[:], a["L2_gnn_Wn1"].rearrange("(b k) m -> k b m", b=2)),
            (wn2[:], a["L2_gnn_Wn2"].rearrange("(b k) m -> k b m", b=2)),
            (bm1[:], a["L2_gnn_bm1"].rearrange("(b k) -> k b", b=2)),
            (bm2[:], a["L2_gnn_bm2"].rearrange("(b k) -> k b", b=2)),
            (bn1[:], a["L2_gnn_bn1"].rearrange("(b k) -> k b", b=2)),
            (raw[:, 2:3], column(a["L1_gnn_blin"])), (raw[:, 3:4], column(a["L2_gnn_bn2"])),
        ]
        packed = []
        for t in range(TPC):
            rows = slice(t * HG, (t + 1) * HG)
            packed += [(raw[rows, 0:1], column(a["L1_gnn_b1"])), (raw[rows, 1:2], column(a["L1_gnn_b2"])),
                       (bd2[rows, rows], a["L1_gnn_W2"]),
                       (w3t[:, t, :], a["L1_gnn_W3"].rearrange("i k -> k i"))]

        @block.sync
        def _(sp):
            with nc.allow_non_contiguous_dma("small weights and biases, once"):
                for dst, src in plain:
                    sp.dma_start(dst, src).then_inc(loaded, 16)
                sp.wait_ge(zeroed, 1)
                for dst, src in packed:
                    sp.dma_start(dst, src).then_inc(loaded, 16)

        @block.gpsimd
        def _(pool):
            pool.memset(ident[:], 0.0).then_inc(made, 1)
            pool.wait_ge(made, 1)
            pool.affine_select(out=ident[:], in_=ident[:], compare_op=ALU.not_equal, fill=1.0, base=0,
                               pattern=[[-1, P]], channel_multiplier=1).then_inc(made, 1)

        @block.tensor
        def _(pe):
            pe.wait_ge(loaded, 16 * (len(plain) + len(packed)))
            pe.wait_ge(summed, 1)
            pe.matmul(ps[:, 0, 0:D], w3t[:].rearrange("k t i -> k (t i)"), wlin[:], start=True, stop=True)
            pe.matmul(ps[:, 1, 0:1], bd2[:], ones[:], start=True, stop=True)
            pe.matmul(ps[:, 2, 0:1], wlin[:], b3[:], start=True, stop=True).then_inc(folded, 1)
            pe.wait_ge(summed, 2)
            pe.matmul(ps[:, 0, 0:1], wc[:, 0, :], ones[:], start=True, stop=True).then_inc(folded, 1)

        @block.vector
        def _(dve):
            dve.memset(bd2[:], 0.0).then_inc(zeroed, 1)
            dve.memset(power[:], -0.5)
            dve.memset(wc[:], 0.0)
            dve.memset(ones[:], 1.0).then_inc(summed, 1)
            dve.wait_ge(loaded, 16 * (len(plain) + len(packed)))
            dve.tensor_scalar(iso_b1[:], raw[:, 0:1], 0.5, None, ALU.mult)
            dve.tensor_scalar(iso_b2[:], raw[:, 1:2], 0.5, None, ALU.mult)
            dve.tensor_scalar(bn2h[:], raw[:, 3:4], 0.5, None, ALU.add)
            dve.wait_ge(folded, 1)
            dve.tensor_copy(bz[:], ps[:, 2, 0:1])
            dve.wait_ge(summed, 1)
            for t in range(TPC):
                g = slice(t * HG, (t + 1) * HG)
                ins = dve.tensor_copy(wc[g, t, :], ps[g, 0, 0:D])
            ins.then_inc(summed, 1)
            dve.wait_ge(summed, 2)
            dve.scalar_tensor_tensor(out=iso_b2[:], in0=ps[:, 1, 0:1], scalar=0.25, in1=iso_b2[:],
                                     op0=ALU.mult, op1=ALU.add)
            dve.tensor_tensor(bz[:], bz[:], raw[:, 2:3], ALU.add).then_inc(summed, 1)
            dve.wait_ge(summed, 3)
            dve.tensor_scalar(dst_bz[:], bz[:], 0.5, None, ALU.mult).then_inc(summed, 1)
            dve.wait_ge(folded, 2)
            dve.wait_ge(summed, 4)
            dve.scalar_tensor_tensor(out=iso_bz[:], in0=ps[:, 0, 0:1], scalar=0.25, in1=dst_bz[:],
                                     op0=ALU.mult, op1=ALU.add)
    return w


def isolated_rows(nc, a, w, name, chunks, passes, taps=None, slots=None):
    U = chunks
    whole = taps is None
    PE_ = (["t0"] + [f"l{l}" for l in range(LAYERS)] + ["tx1", "t1", "g1", "g2", "g3", "tx2", "t2", "na", "nb", "up"]
           + ["tx3"])
    if not whole:
        PE_ = ["t0", "l0", "p1", "l1", "p2", "l2", "p3", "l3", "tx1", "t1", "g1", "pg", "ps1", "g2", "ps2", "g3",
               "tx2", "t2", "na", "nb", "up", "tx3"]
    ACT_ = ["h0", "e0", "e1", "e2", "e3", "h1", "s1", "s2", "tT", "h2", "na", "nb", "uT"]
    if not whole:
        ACT_ = ["h0", "e0", "e1", "e2", "e3", "h1", "pg", "s1", "s2", "tT", "h2", "na", "nb", "uT"]
    ln = [[f"st{k}", f"ag{k}", f"ve{k}", f"xn{k}"] for k in range(4)]
    elu = [[f"m{l}", f"h{l}"] for l in range(LAYERS)]
    if whole:
        DVE_ = ln[0] + sum(elu, []) + ["x1"] + ln[1] + ["x2"] + ln[2] + ["x3a", "x3"] + ln[3] + ["r", "o"]
    else:
        DVE_ = (ln[0] + ["q0"] + elu[0] + ["q1"] + elu[1] + ["q2"] + elu[2] + ["q3"] + elu[3] + ["x1"] + ln[1]
                + ["q4", "s1", "q5", "s2", "q6", "x2"] + ln[2] + ["q7", "x3a", "x3"] + ln[3] + ["q8", "q9"])
    with Phase(nc) as ctx:
        sb = lambda n, shape: [ctx.enter_context(nc.sbuf_tensor(f"{name}_{n}{u}", shape, F32)) for u in range(U)]
        sem = lambda n: ctx.sem(f"{name}_{n}")
        xin, xw, xn, ex, em, hT, out = (sb(n, [P, CH]) for n in ("xin", "xw", "xn", "ex", "em", "hT", "out"))
        sT, sU, nT = sb("sT", [P, P]), sb("sU", [P, P]), sb("nT", [P, 2, CH])
        st, mv, ve, rs = sb("st", [P, TPC, 6]), sb("mv", [P, TPC, 2]), sb("ve", [P, TPC]), sb("rs", [P, TPC])
        ps = [ctx.enter_context(nc.psum_tensor(f"{name}_ps{u}", [P, CH], F32)) for u in range(U)]
        x_in = [sem(f"x_in{u}") for u in range(U)]
        x_used = [sem(f"x_used{u}") for u in range(U)]
        stored = [sem(f"stored{u}") for u in range(U)]
        pe_ev = Events(sem("pe_done"), PE_, U)
        act_ev = Events(sem("act_done"), ACT_, U)
        dve_ev = Events(sem("dve_done"), DVE_, U)
        pool_ev = Events(sem("pool_done"), [f"rs{k}" for k in range(4)], U)
        held = sem("held")
        NTAP = 10
        if not whole:
            tap = [sb(f"tap{k}", [P, CH]) for k in range(2)]
            idx = [ctx.enter_context(nc.sbuf_tensor(f"{name}_idx{u}", [P, TPC], I32)) for u in range(U)]
            idx_in = sem("idx_in")
            tap_stored = [[sem(f"tap{k}_stored{u}") for u in range(U)] for k in range(2)]
        block = ctx.enter_context(nc.Block())
        last = passes - 1

        def wait(eng, ev, i, what, u):
            eng.wait_ge(ev.sem, ev.at(i, what, u))

        def loop(eng, body):
            if last:
                with eng.Fori(0, last) as i:
                    body(i)
            body(last)

        def row0(i, u):
            if isinstance(i, int) and whole:
                return min((i * U + u) * CH, N - CH)
            return i * (U * CH) + u * CH

        def dram(t, i, u):
            r0 = row0(i, u)
            rows = t[bass.ds(r0, CH), :] if not isinstance(r0, int) else t[r0:r0 + CH, :]
            return rows.rearrange("(p t) f -> p (t f)", t=TPC)

        @block.sync
        def _(sp):
            def body(i):
                if whole:
                    for u in range(U):
                        sp.wait_ge(x_used[u], i + 1)
                        sp.dma_start(xin[u][:], dram(a["x"], i, u)).then_inc(x_in[u], 16)
                    for u in range(U):
                        wait(sp, dve_ev, i, "o", u)
                        if not isinstance(i, int) or u < U - 1:
                            pass
                        else:
                            sp.wait_ge(stored[u - 1], 16 * (i + 2))
                        sp.dma_start(dram(a["out"], i, u), out[u][:]).then_inc(stored[u], 16)
                else:
                    for k in range(NTAP):
                        for u in range(U):
                            wait(sp, dve_ev, i, f"q{k}", u)
                            wide = taps[k].shape[1] == D
                            src = tap[k % 2][u][:] if wide else tap[k % 2][u][:, 0:P]
                            sp.dma_start(dram(taps[k], i, u), src).then_inc(tap_stored[k % 2][u], 16)
            for u in range(U):
                sp.sem_inc(stored[u], 16)
                if not whole:
                    for k in range(2):
                        sp.sem_inc(tap_stored[k][u], 16)
            loop(sp, body)
            for u in range(U):
                if whole:
                    sp.wait_ge(stored[u], 16 * passes + 16)
                else:
                    for k in range(2):
                        sp.wait_ge(tap_stored[k][u], 16 * passes * NTAP // 2 + 16)

        @block.gpsimd
        def _(pool):
            if not whole:
                def fetch(i):
                    for u in range(U):
                        pool.wait_ge(x_used[u], i + 1)
                        c0 = i * (U * TPC) + u * TPC
                        pool.tensor_copy(idx[u][:], slots[:, bass.ds(c0, TPC)] if not isinstance(c0, int)
                                         else slots[:, c0:c0 + TPC]).then_inc(idx_in, 1)
                        pool.wait_ge(idx_in, i * U + (u + 1))
                        pool.sem_inc(held, 1)
                        for t in range(TPC):
                            pool.indirect_dma_start(
                                xin[u][:, t * D:(t + 1) * D], None, a["x"],
                                bass.IndirectOffsetOnAxis(idx[u][:, t:t + 1], 0),
                                bounds_check=bound, oob_is_err=False).then_inc(x_in[u], 16)

            bound = pool.to_reg(N - 1)

            def body(i):
                if not whole:
                    fetch(i)
                for k in range(4):
                    for u in range(U):
                        wait(pool, dve_ev, i, f"ve{k}", u)
                        pool.tensor_tensor(rs[u][:], ve[u][:], w["power"][:, 0:TPC], ALU.pow).then_inc(pool_ev.sem, 1)
            loop(pool, body)

        @block.tensor
        def _(pe):
            def done(ins):
                ins.then_inc(pe_ev.sem, 1)

            def to_features(i, u, k):
                wait(pe, dve_ev, i, f"xn{k}", u)
                for t in range(TPC):
                    c = slice(t * P, (t + 1) * P)
                    ins = pe.transpose(ps[u][:, c], xn[u][:, c], w["ident"][:])
                done(ins)

            def back(src, u):
                for t in range(TPC):
                    c = slice(t * P, (t + 1) * P)
                    ins = pe.transpose(ps[u][:, c], src[:, c], w["ident"][:])
                done(ins)

            def body(i):
                us = range(U)
                for u in us:
                    to_features(i, u, 0)
                for l in range(LAYERS):
                    for u in us:
                        if l == 0:
                            wait(pe, act_ev, i, "h0", u)
                        else:
                            wait(pe, dve_ev, i, f"h{l - 1}", u)
                            if not whole:
                                wait(pe, dve_ev, i, f"q{l}", u)
                        done(pe.matmul(ps[u][:], w["root"][:, l, :], hT[u][:], start=True, stop=True))
                    if not whole and l < LAYERS - 1:
                        for u in us:
                            wait(pe, dve_ev, i, f"h{l}", u)
                            back(hT[u], u)
                for u in us:
                    wait(pe, dve_ev, i, f"h{LAYERS - 1}", u)
                    back(hT[u], u)
                for u in us:
                    to_features(i, u, 1)
                for u in us:
                    wait(pe, act_ev, i, "h1", u)
                    for t in range(TPC):
                        ins = pe.matmul(ps[u][t * HG:(t + 1) * HG, 0:P], w["w1"][:], hT[u][:, t * P:(t + 1) * P],
                                        start=True, stop=True)
                    done(ins)
                if not whole:
                    for u in us:
                        wait(pe, act_ev, i, "s1", u)
                        done(pe.transpose(ps[u][:, P:2 * P], sU[u][:], w["ident"][:]))
                    for u in us:
                        wait(pe, dve_ev, i, "q4", u)
                        wait(pe, dve_ev, i, "s1", u)
                        done(pe.transpose(ps[u][:, 0:P], sU[u][:], w["ident"][:]))
                for u in us:
                    if whole:
                        wait(pe, act_ev, i, "s1", u)
                    else:
                        wait(pe, dve_ev, i, "q5", u)
                    done(pe.matmul(ps[u][:, 0:P], w["bd2"][:], sT[u][:], start=True, stop=True))
                if not whole:
                    for u in us:
                        wait(pe, dve_ev, i, "s2", u)
                        done(pe.transpose(ps[u][:, 0:P], xn[u][:, 0:P], w["ident"][:]))
                for u in us:
                    if whole:
                        wait(pe, act_ev, i, "s2", u)
                    else:
                        wait(pe, dve_ev, i, "q6", u)
                    for t in range(TPC):
                        ins = pe.matmul(ps[u][:, t * P:(t + 1) * P], w["wc"][:, t, :], sU[u][:], start=True, stop=True)
                    done(ins)
                for u in us:
                    wait(pe, act_ev, i, "tT", u)
                    back(ex[u], u)
                for u in us:
                    to_features(i, u, 2)
                for b, what in ((0, "na"), (1, "nb")):
                    for u in us:
                        wait(pe, act_ev, i, "h2" if b == 0 else "na", u)
                        done(pe.matmul(ps[u][:], w["wn1"][:, 0, b * P:(b + 1) * P], hT[u][:], start=True, stop=True))
                for u in us:
                    wait(pe, act_ev, i, "nb", u)
                    for b in range(2):
                        ins = pe.matmul(ps[u][:], w["wn2"][:, b, :], nT[u][:, b, :], start=b == 0, stop=b == 1)
                    done(ins)
                for u in us:
                    wait(pe, act_ev, i, "uT", u)
                    back(em[u], u)
            loop(pe, body)

        @block.scalar
        def _(act):
            def step(i, u, what, out_ap, func, producer, **kw):
                wait(act, pe_ev, i, producer, u)
                act.activation(out_ap, ps[u][:, 0:out_ap.shape[1]], func, **kw).then_inc(act_ev.sem, 1)

            def body(i):
                us = range(U)
                for u in us:
                    step(i, u, "h0", hT[u][:], ACT.Relu, "t0")
                for l in range(LAYERS):
                    for u in us:
                        step(i, u, f"e{l}", ex[u][:], ACT.Exp, f"l{l}", bias=w["b_rel"][:, l:l + 1])
                for u in us:
                    step(i, u, "h1", hT[u][:], ACT.Relu, "t1")
                if not whole:
                    for u in us:
                        step(i, u, "pg", sU[u][:], ACT.Identity, "g1")
                for u in us:
                    step(i, u, "s1", sT[u][:], ACT.Tanh, "g1", bias=w["iso_b1"][:], scale=0.5)
                for u in us:
                    if not whole:
                        wait(act, pe_ev, i, "ps1", u)
                    step(i, u, "s2", sU[u][:], ACT.Tanh, "g2", bias=w["iso_b2"][:], scale=0.25)
                for u in us:
                    step(i, u, "tT", ex[u][:], ACT.Tanh, "g3", bias=w["iso_bz"][:], scale=0.25)
                for u in us:
                    step(i, u, "h2", hT[u][:], ACT.Relu, "t2")
                for b, what in ((0, "na"), (1, "nb")):
                    for u in us:
                        step(i, u, what, nT[u][:, b, :], ACT.Relu, what, bias=w["bn1"][:, b:b + 1])
                for u in us:
                    step(i, u, "uT", em[u][:], ACT.Identity, "up", bias=w["bn2h"][:])
            loop(act, body)

        @block.vector
        def _(dve):
            def done(ins):
                ins.then_inc(dve_ev.sem, 1)

            def layernorm(i, k, x, before, used=None):
                us = range(U)
                for u in us:
                    if before == "x_in":
                        dve.wait_ge(x_in[u], (16 if whole else 64) * (i + 1))
                    else:
                        wait(dve, dve_ev, i, before, u)
                    for t in range(TPC):
                        ins = dve.bn_stats(st[u][:, t, :], x[u][:, t * D:(t + 1) * D])
                        if used is not None and t == 0:
                            ins.then_inc(used[u], 1)
                    done(ins)
                wait(dve, dve_ev, i, f"st{k}", U - 1)
                dve.sem_inc(held, 1)
                for u in us:
                    for t in range(TPC):
                        ins = dve.bn_aggr(mv[u][:, t, :], st[u][:, t, :])
                    done(ins)
                for u in us:
                    wait(dve, dve_ev, i, f"ag{k}", u)
                    done(dve.tensor_scalar(ve[u][:], mv[u][:, :, 1], EPS, None, ALU.add))
                for u in us:
                    wait(dve, pool_ev, i, f"rs{k}", u)
                    for t in range(TPC):
                        c = slice(t * D, (t + 1) * D)
                        ins = dve.tensor_scalar(xn[u][:, c], x[u][:, c], mv[u][:, t, 0:1], rs[u][:, t:t + 1],
                                                ALU.subtract, ALU.mult)
                    done(ins)

            def to_tap(i, k, make):
                for u in range(U):
                    dve.wait_ge(tap_stored[k % 2][u], i * (16 * NTAP // 2) + 16 * (k // 2 + 1))
                    done(make(u, tap[k % 2][u]))

            def body(i):
                us = range(U)
                layernorm(i, 0, xin, "x_in")
                if not whole:
                    def make0(u, to):
                        wait(dve, dve_ev, i, "xn0", u)
                        return dve.tensor_scalar(to[:], xn[u][:], 0.0, None, ALU.max)
                    to_tap(i, 0, make0)
                for l in range(LAYERS):
                    for u in us:
                        wait(dve, act_ev, i, f"e{l}", u)
                        done(dve.tensor_scalar(em[u][:], ex[u][:], 1.0, -1.0, ALU.min, ALU.add))
                    for u in us:
                        wait(dve, dve_ev, i, f"m{l}", u)
                        if l > 0 or not whole:
                            pass
                        done(dve.scalar_tensor_tensor(out=hT[u][:], in0=ps[u][:], scalar=w["b_rel"][:, l:l + 1],
                                                      in1=em[u][:], op0=ALU.add, op1=ALU.max))
                    if not whole and l < LAYERS - 1:
                        def make(u, to, l=l):
                            wait(dve, pe_ev, i, f"p{l + 1}", u)
                            return dve.tensor_copy(to[:], ps[u][:])
                        to_tap(i, l + 1, make)
                for u in us:
                    wait(dve, pe_ev, i, "tx1", u)
                    done(dve.tensor_tensor(xw[u][:], ps[u][:], xin[u][:], ALU.add))
                layernorm(i, 1, xw, "x1", x_used)
                if not whole:
                    def make4(u, to):
                        wait(dve, pe_ev, i, "pg", u)
                        return dve.tensor_copy(to[:, 0:P], ps[u][:, P:2 * P])
                    to_tap(i, 4, make4)
                    for u in us:
                        wait(dve, act_ev, i, "s1", u)
                        done(dve.tensor_scalar(sU[u][:], sT[u][:], 0.5, 0.5, ALU.mult, ALU.add))

                    def make5(u, to):
                        wait(dve, pe_ev, i, "ps1", u)
                        return dve.tensor_copy(to[:, 0:P], ps[u][:, 0:P])
                    to_tap(i, 5, make5)
                    for u in us:
                        wait(dve, act_ev, i, "s2", u)
                        done(dve.tensor_scalar(xn[u][:, 0:P], sU[u][:], 0.5, 0.5, ALU.mult, ALU.add))

                    def make6(u, to):
                        wait(dve, pe_ev, i, "ps2", u)
                        return dve.tensor_copy(to[:, 0:P], ps[u][:, 0:P])
                    to_tap(i, 6, make6)
                for u in us:
                    wait(dve, pe_ev, i, "tx2", u)
                    done(dve.scalar_tensor_tensor(out=xw[u][:], in0=ps[u][:], scalar=0.5, in1=xw[u][:],
                                                  op0=ALU.mult, op1=ALU.add))
                layernorm(i, 2, xw, "x2")
                if not whole:
                    def make7(u, to):
                        wait(dve, dve_ev, i, "xn2", u)
                        return dve.tensor_scalar(to[:], xn[u][:], 0.0, None, ALU.max)
                    to_tap(i, 7, make7)
                for u in us:
                    wait(dve, pe_ev, i, "tx3", u)
                    done(dve.scalar_tensor_tensor(out=ex[u][:], in0=xn[u][:], scalar=0.0, in1=ps[u][:],
                                                  op0=ALU.max, op1=ALU.add))
                for u in us:
                    wait(dve, dve_ev, i, "x3a", u)
                    done(dve.tensor_tensor(xw[u][:], xw[u][:], ex[u][:], ALU.add))
                layernorm(i, 3, xw, "x3")
                if whole:
                    for u in us:
                        wait(dve, dve_ev, i, "xn3", u)
                        done(dve.tensor_scalar(ex[u][:], xn[u][:], 0.0, ALPHA, ALU.max, ALU.mult))
                    for u in us:
                        wait(dve, dve_ev, i, "r", u)
                        dve.wait_ge(stored[u], 16 * i + 16)
                        done(dve.tensor_tensor(out[u][:], xw[u][:], ex[u][:], ALU.add))
                else:
                    def make8(u, to):
                        wait(dve, dve_ev, i, "xn3", u)
                        return dve.tensor_scalar(to[:], xn[u][:], 0.0, None, ALU.max)
                    to_tap(i, 8, make8)

                    def make9(u, to):
                        return dve.tensor_scalar(to[:], xn[u][:], 0.0, ALPHA, ALU.max, ALU.mult)
                    to_tap(i, 9, make9)
            for u in range(U):
                dve.sem_inc(x_used[u], 1)
            loop(dve, body)


def constants(nc, sb, n):
    c = {}
    HI = NODE_ROWS // P
    c["row_i"] = sb("c_row_i", [P, HI], I32)
    c["row"] = sb("c_row", [P, HI], F32)
    c["part_i"] = sb("c_part_i", [P, 1], I32)
    c["part"] = sb("c_part", [P, 1], F32)
    c["below"] = sb("c_below", [P, P], F32)
    c["above"] = sb("c_above", [P, P], F32)
    c["slot1"] = sb("c_slot1", [P, NT], I32)
    c["pos1"] = sb("c_pos1", [P, P], F32)
    c["pos1_i"] = sb("c_pos1_i", [P, P], I32)
    with Phase(nc) as ctx:
        counted = ctx.sem(f"iota_written{n}")
        cast = ctx.sem(f"iota_cast{n}")
        block = ctx.enter_context(nc.Block())

        @block.gpsimd
        def _(pool):
            pool.iota(c["row_i"][:], [[1, HI]], base=0, channel_multiplier=0)
            pool.iota(c["part_i"][:], [[1, 1]], base=0, channel_multiplier=1)
            pool.iota(c["slot1"][:], [[CH, NCH], [1, TPC]], base=1, channel_multiplier=TPC)
            pool.iota(c["pos1_i"][:], [[1, P]], base=1, channel_multiplier=P).then_inc(counted, 1)

        @block.vector
        def _(dve):
            dve.wait_ge(counted, 1)
            dve.tensor_copy(c["pos1"][:], c["pos1_i"][:])
            dve.tensor_copy(c["row"][:], c["row_i"][:])
            dve.tensor_copy(c["part"][:], c["part_i"][:]).then_inc(cast, 1)
            dve.wait_ge(cast, 1)
            dve.tensor_scalar(c["below"][:], c["row"][:, 0:P], c["part"][:], None, ALU.is_lt)
            dve.tensor_scalar(c["above"][:], c["row"][:, 0:P], c["part"][:], None, ALU.is_gt)
    return c


def sort_edges(nc, a, w, c, pairs):
    BF = mybir.dt.bfloat16
    HI = NODE_ROWS // P
    FULL, REST = E // P, E % P
    U = TPC
    with Phase(nc) as ctx:
        sb = lambda n, shape, dt=F32: ctx.enter_context(nc.sbuf_tensor("sort_" + n, shape, dt))
        sem = lambda n: ctx.sem("sort_" + n)
        dst_r, src_r, lo_r = sb("dst_r", [NT, P], I32), sb("src_r", [NT, P], I32), sb("lo_r", [NT, P], I32)
        rows_f = sb("rows_f", [NT, 3, P])
        cols = sb("cols", [P, 3, NT])
        dst_c, src_c, hi_c = (sb(n, [P, NT], I32) for n in ("dst_c", "src_c", "hi_c"))
        hi_f = sb("hi_f", [P, NT])
        guard = sb("guard", [1, 4], I32)
        dst_b, lo_b = sb("dst_b", [P, NE]), sb("lo_b", [P, NE])
        zero = sb("zero", [P, P], BF)
        count, total, upto, start = (sb(n, [P, HI]) for n in ("count", "total", "upto", "start"))
        ones = sb("ones", [P, P])
        ring = lambda n, width, dt=F32: [sb(f"{n}{u}", [P, width], dt) for u in range(U)]
        hot_lo, hot_hi, lo_t, table = ring("hot_lo", P, BF), ring("hot_hi", HI, BF), ring("lo_t", P), ring("table", HI)
        same, looked, rank, base = ring("same", P), ring("looked", HI), ring("rank", 1), ring("base", 1)
        to, pair = ring("to", 1, I32), ring("pair", 2, I32)
        ps_t = [ctx.enter_context(nc.psum_tensor(f"sort_ps_t{k}", [P, 512], F32)) for k in range(3)]
        ps_c = ctx.enter_context(nc.psum_tensor("sort_ps_c", [P, 512], F32))
        ps_l = [ctx.enter_context(nc.psum_tensor(f"sort_ps_l{u}", [P, 512], F32)) for u in range(U)]
        flat = nc.dram_tensor("sort_flat", (2, NE), F32, kind="Internal").ap()
        padded, loaded, link = sem("padded"), sem("loaded"), sem("dve_link")
        rows_made, turned, counted, tot_made = (sem(n) for n in ("rows_made", "turned", "counted", "totals_made"))
        flat_out, guard_out, b_in, started = sem("flat_out"), sem("guard_out"), sem("broadcasts_in"), sem("started")
        hot = Events(sem("hot_made"), ["hot"], U)
        hot_used = [sem(f"hot_used{u}") for u in range(U)]
        copied, looked_up = sem("table_copied"), sem("looked_up")
        walk = Events(sem("dve_walk"), ["hot", "same", "rank", "base", "pair", "place"], U)
        scattered = [sem(f"scattered{u}") for u in range(U)]
        held = sem("pool_held")
        block = ctx.enter_context(nc.Block())

        @block.sync
        def _(sp):
            sp.wait_ge(padded, 1)
            for to_sb, of in ((dst_r, a["dst"]), (src_r, a["src"])):
                sp.dma_start(to_sb[0:FULL, :], of[0:FULL * P].rearrange("(r e) -> r e", e=P)).then_inc(loaded, 16)
                sp.dma_start(to_sb[FULL:FULL + 1, 0:REST], of[FULL * P:E].unsqueeze(0)).then_inc(loaded, 16)
            sp.dma_start(pairs[0:1, :], guard[:, 0:2]).then_inc(guard_out, 16)
            sp.dma_start(pairs[NE + 1:NE + 2, :], guard[:, 2:4]).then_inc(guard_out, 16)
            sp.wait_ge(rows_made, 1)
            for k in range(2):
                sp.dma_start(flat[k, :].rearrange("(r e) -> r e", e=P), rows_f[:, k, :]).then_inc(flat_out, 16)
            sp.wait_ge(flat_out, 32)
            for k, to_sb in ((0, dst_b), (1, lo_b)):
                sp.dma_start(to_sb[:], flat[k, :].partition_broadcast(P)).then_inc(b_in, 16)
            sp.wait_ge(guard_out, 32)

        @block.gpsimd
        def _(pool):
            bound = pool.to_reg(NE)
            with pool.Fori(0, NCH) as i:
                for u in range(U):
                    pool.wait_ge(walk.sem, walk.at(i, "place", u))
                    pool.sem_inc(held, 1)
                    pool.indirect_dma_start(pairs, bass.IndirectOffsetOnAxis(to[u][:], 0), pair[u][:], None,
                                            bounds_check=bound, oob_is_err=False).then_inc(scattered[u], 16)
            for u in range(U):
                pool.wait_ge(scattered[u], 16 * NCH)

        @block.tensor
        def _(pe):
            for u in range(U):
                pe.sem_inc(hot_used[u], 1)
            pe.wait_ge(rows_made, 1)
            for k in range(3):
                ins = pe.transpose(ps_t[k][:, 0:NT], rows_f[:, k, :], w["ident"][0:NT, 0:NT])
            ins.then_inc(turned, 1)
            pe.wait_ge(hot.sem, hot.at(0, "hot", 0))
            pe.matmul(ps_c[:, 0:HI], zero[:], hot_hi[0][:], start=True, stop=True, skip_group_check=True)
            with pe.Fori(0, NCH) as i:
                for u in range(U):
                    pe.wait_ge(hot.sem, hot.at(i, "hot", u))
                    pe.matmul(ps_c[:, 0:HI], hot_lo[u][:], hot_hi[u][:], start=False, stop=True,
                              skip_group_check=True).then_inc(hot_used[u], 1)
            pe.wait_ge(tot_made, 1)
            pe.matmul(ps_l[0][:, 0:HI], ones[:], count[:], start=True, stop=True)
            pe.matmul(ps_l[1][:, 0:HI], c["above"][:], count[:], start=True, stop=True).then_inc(counted, 1)
            pe.wait_ge(started, 1)
            pe.matmul(ps_c[:, 0:HI], w["ident"][:], start[:], start=True, stop=True,
                      skip_group_check=True).then_inc(looked_up, 1)
            with pe.Fori(0, NCH) as i:
                for u in range(U):
                    pe.wait_ge(walk.sem, walk.at(i, "hot", u))
                    pe.wait_ge(copied, i * U + (u + 1))
                    pe.matmul(ps_l[u][:, 0:HI], lo_t[u][:], table[u][:], start=True, stop=True)
                    pe.matmul(ps_c[:, 0:HI], hot_lo[u][:], hot_hi[u][:], start=False, stop=True,
                              skip_group_check=True).then_inc(looked_up, 1)

        @block.scalar
        def _(act):
            with act.Fori(0, NCH) as i:
                for u in range(U):
                    act.wait_ge(looked_up, i * U + (u + 1))
                    act.activation(table[u][:], ps_c[:, 0:HI], ACT.Identity).then_inc(copied, 1)

        @block.vector
        def _(dve):
            n = [0]

            def linked(ins):
                n[0] += 1
                ins.then_inc(link, 1)
                dve.wait_ge(link, n[0])

            def hot_rows(i, u, t):
                dve.tensor_scalar(hot_lo[u][:], c["row"][:, 0:P], cols[:, 1, bass.ds(t, 1)], None, ALU.is_equal)
                return dve.tensor_scalar(hot_hi[u][:], c["row"][:], hi_f[:, bass.ds(t, 1)], None, ALU.is_equal)

            dve.memset(guard[:, 0:2], -1)
            dve.memset(guard[:, 2:4], -2)
            dve.memset(src_r[:], 0)
            dve.memset(ones[:], 1.0)
            dve.memset(zero[:], 0.0)
            dve.memset(dst_r[:], N).then_inc(padded, 1)
            dve.wait_ge(loaded, 64)
            dve.tensor_copy(rows_f[:, 0, :], dst_r[:])
            dve.tensor_copy(rows_f[:, 2, :], src_r[:])
            linked(dve.tensor_scalar(lo_r[:], dst_r[:], P - 1, None, ALU.bitwise_and))
            dve.tensor_copy(rows_f[:, 1, :], lo_r[:]).then_inc(rows_made, 1)
            dve.wait_ge(turned, 1)
            for k in range(3):
                ins = dve.tensor_copy(cols[:, k, :], ps_t[k][:, 0:NT])
            linked(ins)
            dve.tensor_copy(src_c[:], cols[:, 2, :])
            linked(dve.tensor_copy(dst_c[:], cols[:, 0, :]))
            linked(dve.tensor_scalar(hi_c[:], dst_c[:], 7, None, ALU.arith_shift_right))
            linked(dve.tensor_copy(hi_f[:], hi_c[:]))
            with dve.Fori(0, NCH) as i:
                for u in range(U):
                    dve.wait_ge(hot_used[u], i + 1)
                    hot_rows(i, u, i * U + u).then_inc(hot.sem, 1)
            for u in range(U):
                dve.wait_ge(hot_used[u], NCH + 1)
            dve.tensor_copy(count[:], ps_c[:, 0:HI]).then_inc(tot_made, 1)
            dve.wait_ge(counted, 1)
            linked(dve.tensor_copy(total[:], ps_l[0][:, 0:HI]))
            linked(dve.tensor_tensor_scan(upto[:], total[:], total[:], 0.0, ALU.add, ALU.bypass))
            linked(dve.tensor_tensor(upto[:], upto[:], total[:], ALU.subtract))
            dve.tensor_tensor(start[:], upto[:], ps_l[1][:, 0:HI], ALU.add).then_inc(started, 1)
            dve.wait_ge(b_in, 32)
            def tile_walk(i):
                def mine(name, u):
                    dve.wait_ge(walk.sem, walk.at(i, name, u))

                def done(ins):
                    ins.then_inc(walk.sem, 1)

                for u in range(U):
                    e = bass.ds(i * CH + u * P, P)
                    dve.tensor_scalar(lo_t[u][:], lo_b[:, e], c["part"][:], None, ALU.is_equal)
                    done(hot_rows(i, u, i * U + u))
                for u in range(U):
                    e = bass.ds(i * CH + u * P, P)
                    done(dve.tensor_scalar(same[u][:], dst_b[:, e], cols[:, 0, bass.ds(i * U + u, 1)], None,
                                           ALU.is_equal))
                for u in range(U):
                    mine("same", u)
                    done(dve.tensor_tensor_reduce(out=same[u][:], in0=same[u][:], in1=c["below"][:], scale=1.0,
                                                  scalar=1.0, op0=ALU.mult, op1=ALU.add, accum_out=rank[u][:]))
                for u in range(U):
                    dve.wait_ge(looked_up, i * U + (u + 2))
                    done(dve.tensor_tensor_reduce(out=looked[u][:], in0=ps_l[u][:, 0:HI], in1=hot_hi[u][:], scale=1.0,
                                                  scalar=0.0, op0=ALU.mult, op1=ALU.add, accum_out=base[u][:]))
                for u in range(U):
                    if not isinstance(i, int):
                        dve.wait_ge(scattered[u], i * 16)
                    dve.tensor_copy(pair[u][:, 0:1], dst_c[:, bass.ds(i * U + u, 1)])
                    done(dve.tensor_copy(pair[u][:, 1:2], src_c[:, bass.ds(i * U + u, 1)]))
                for u in range(U):
                    mine("base", u)
                    done(dve.tensor_tensor(to[u][:], base[u][:], rank[u][:], ALU.add))

            tile_walk(0)
            with dve.Fori(1, NCH) as i:
                tile_walk(i)


def edge_tables(nc, a, w, c, pairs, g, flat, mean_out):
    with Phase(nc) as ctx:
        t_ = lambda n, shape, dt=F32: ctx.enter_context(nc.sbuf_tensor("idx_" + n, shape, dt))
        sem = lambda n: ctx.sem("idx_" + n)
        near = [t_(f"near{k}", [NT, P, 2], I32) for k in range(3)]
        d = [t_(f"d{k}", [NT, P]) for k in range(3)]
        first, last, f_idx, l_idx, far = (t_(n, [NT, P]) for n in ("first", "lastr", "f_idx", "l_idx", "far"))
        out_r = t_("out_r", [NT, 5, P])
        cols = t_("cols", [P, 5, NT])
        row_f, row_l, carry_f, carry_l = (t_(n, [1, P + 1]) for n in ("row_f", "row_l", "carry_f", "carry_l"))
        back_f, back_l = t_("back_f", [NT, 1]), t_("back_l", [NT, 1])
        deg1, tmp = t_("deg1", [P, NT]), t_("tmp", [P, NT])
        half = t_("half", [P, NT])
        zero = t_("zero", [P, NODE_ROWS // P], I32)
        found = t_("found", [P, NT], I32)
        found_f = t_("found_f", [P, NT])
        bc = t_("bc", [P, NE])
        mean = t_("mean", [P, NE])
        ps = [ctx.enter_context(nc.psum_tensor(f"idx_ps{k}", [P, 512], F32)) for k in range(6)]
        node_row = nc.dram_tensor("node_row", (NODE_ROWS, 1), I32, kind="Internal").ap()
        loaded, link, made, turned, flat_out, b_in, zeroed, zero_out = (sem(n) for n in (
            "loaded", "dve_link", "made", "turned", "flat_out", "b_in", "zeroed", "zero_out"))
        scattered, fetched, powers, cols_made = sem("scattered"), sem("fetched"), sem("powers"), sem("cols_made")
        mean_made, mean_stored = sem("mean_made"), sem("mean_stored")
        block = ctx.enter_context(nc.Block())

        @block.sync
        def _(sp):
            for k in range(3):
                sp.dma_start(near[k][:].rearrange("r e k -> r (e k)"),
                             pairs[k:k + NE, :].rearrange("(r e) k -> r (e k)", e=P)).then_inc(loaded, 16)
            sp.wait_ge(zeroed, 1)
            sp.dma_start(node_row.rearrange("(p f) o -> p (f o)", p=P), zero[:]).then_inc(zero_out, 16)
            sp.wait_ge(made, 1)
            sp.dma_start(flat.rearrange("(r e) -> r e", e=P), d[1][:]).then_inc(flat_out, 16)
            sp.wait_ge(flat_out, 16)
            sp.dma_start(bc[:], flat.partition_broadcast(P)).then_inc(b_in, 16)
            sp.wait_ge(mean_made, 1)
            sp.dma_start(mean_out, mean[:]).then_inc(mean_stored, 16)
            sp.wait_ge(mean_stored, 16)

        @block.gpsimd
        def _(pool):
            pool.wait_ge(cols_made, 1)
            pool.tensor_tensor(g["norm"][:], cols[:, 2, :], half[:], ALU.pow).then_inc(powers, 1)
            pool.wait_ge(cols_made, 2)
            pool.tensor_tensor(g["dinv"][:], deg1[:], half[:], ALU.pow).then_inc(powers, 1)
            pool.wait_ge(zero_out, 16)
            pool.wait_ge(cols_made, 3)
            for t in range(NT):
                pool.indirect_dma_start(node_row, bass.IndirectOffsetOnAxis(g["last"][:, t:t + 1], 0),
                                        c["slot1"][:, t:t + 1], None, bounds_check=NODE_ROWS - 1,
                                        oob_is_err=False).then_inc(scattered, 16)
            pool.wait_ge(scattered, 16 * NT)
            for t in range(NT):
                pool.indirect_dma_start(found[:, t:t + 1], None, node_row,
                                        bass.IndirectOffsetOnAxis(g["src"][:, t:t + 1], 0),
                                        bounds_check=N - 1, oob_is_err=False).then_inc(fetched, 16)

        @block.tensor
        def _(pe):
            pe.wait_ge(made, 2)
            pe.transpose(ps[0][0:1, 0:NT], f_idx[:, P - 1:P], w["ident"][0:NT, 0:NT])
            pe.transpose(ps[1][0:1, 0:NT], l_idx[:, 0:1], w["ident"][0:NT, 0:NT]).then_inc(turned, 1)
            pe.wait_ge(made, 3)
            pe.transpose(ps[2][0:NT, 0:1], carry_f[:, 0:NT], w["ident"][0:1, 0:1])
            pe.transpose(ps[3][0:NT, 0:1], carry_l[:, 1:NT + 1], w["ident"][0:1, 0:1]).then_inc(turned, 1)
            pe.wait_ge(made, 4)
            for k in range(5):
                ins = pe.transpose(ps[(4, 5, 0, 1, 4)[k]][:, (0, 0, 0, 0, 128)[k]:(0, 0, 0, 0, 128)[k] + NT],
                                   out_r[:, k, :], w["ident"][0:NT, 0:NT])
            ins.then_inc(turned, 1)

        @block.vector
        def _(dve):
            n = [0]

            def linked(ins):
                n[0] += 1
                ins.then_inc(link, 1)
                dve.wait_ge(link, n[0])

            BIG = float(4 * NE)
            dve.memset(half[:], -0.5)
            dve.memset(far[:], float(FAR))
            dve.memset(carry_f[:], 0.0)
            dve.memset(carry_l[:], BIG)
            dve.memset(g["cont"][:, 0:P], 0)
            dve.memset(zero[:], 0).then_inc(zeroed, 1)
            dve.wait_ge(loaded, 48)
            dve.tensor_copy(d[0][:], near[0][:, :, 0])
            dve.tensor_copy(d[2][:], near[2][:, :, 0])
            dve.tensor_copy(out_r[:, 1, :], near[1][:, :, 1])
            dve.tensor_copy(d[1][:], near[1][:, :, 0]).then_inc(made, 1)
            dve.wait_ge(made, 1)
            dve.tensor_tensor(first[:], d[1][:], d[0][:], ALU.not_equal)
            linked(dve.tensor_tensor(last[:], d[1][:], d[2][:], ALU.not_equal))
            dve.tensor_tensor(f_idx[:], first[:], c["pos1"][0:NT, :], ALU.mult)
            linked(dve.tensor_tensor(l_idx[:], last[:], c["pos1"][0:NT, :], ALU.mult))
            linked(dve.tensor_scalar(far[:], last[:], -BIG, BIG, ALU.mult, ALU.add))
            linked(dve.tensor_tensor(l_idx[:], l_idx[:], far[:], ALU.add))
            linked(dve.tensor_tensor_scan(f_idx[:], f_idx[:], f_idx[:], 0.0, ALU.max, ALU.max))
            dve.tensor_tensor_scan(l_idx[:, ::-1], l_idx[:, ::-1], l_idx[:, ::-1], BIG, ALU.min,
                                   ALU.min).then_inc(made, 1)
            dve.wait_ge(turned, 1)
            dve.tensor_copy(row_f[:, 0:NT], ps[0][0:1, 0:NT])
            linked(dve.tensor_copy(row_l[:, 0:NT], ps[1][0:1, 0:NT]))
            dve.tensor_tensor_scan(carry_f[:, 1:NT + 1], row_f[:, 0:NT], row_f[:, 0:NT], 0.0, ALU.max, ALU.max)
            dve.tensor_tensor_scan(carry_l[:, 0:NT][:, ::-1], row_l[:, 0:NT][:, ::-1], row_l[:, 0:NT][:, ::-1], BIG,
                                   ALU.min, ALU.min).then_inc(made, 1)
            dve.wait_ge(turned, 2)
            dve.tensor_copy(back_f[:], ps[2][0:NT, 0:1])
            linked(dve.tensor_copy(back_l[:], ps[3][0:NT, 0:1]))
            dve.tensor_scalar(f_idx[:], f_idx[:], back_f[:], None, ALU.max)
            linked(dve.tensor_scalar(l_idx[:], l_idx[:], back_l[:], None, ALU.min))
            linked(dve.tensor_tensor(out_r[:, 2, :], l_idx[:], f_idx[:], ALU.subtract))
            dve.tensor_scalar(out_r[:, 2, :], out_r[:, 2, :], 1.0, None, ALU.add)
            dve.tensor_copy(out_r[:, 0, :], d[1][:])
            dve.tensor_scalar(out_r[:, 4, :], d[1][:], float(N - 1), None, ALU.min)
            linked(dve.tensor_scalar(far[:], last[:], -float(FAR), float(FAR), ALU.mult, ALU.add))
            dve.tensor_tensor(out_r[:, 3, :], d[1][:], far[:], ALU.add).then_inc(made, 1)
            dve.wait_ge(turned, 3)
            for k in range(5):
                ins = dve.tensor_copy(cols[:, k, :], ps[(4, 5, 0, 1, 4)[k]][:, (0, 0, 0, 0, 128)[k]:(0, 0, 0, 0, 128)[k] + NT])
            ins.then_inc(cols_made, 1)
            dve.wait_ge(cols_made, 1)
            dve.tensor_scalar(deg1[:], cols[:, 2, :], 1.0, None, ALU.add).then_inc(cols_made, 1)
            dve.tensor_copy(g["src"][:], cols[:, 1, :])
            dve.tensor_copy(g["dst"][:], cols[:, 4, :])
            dve.tensor_copy(g["last"][:], cols[:, 3, :]).then_inc(cols_made, 1)
            linked(dve.reciprocal(g["inv_deg"][:], cols[:, 2, :]))
            dve.wait_ge(powers, 2)
            dve.tensor_tensor(g["root_deg"][:], cols[:, 2, :], g["norm"][:], ALU.mult)
            dve.tensor_tensor(g["f1"][:], cols[:, 2, :], g["dinv"][:], ALU.mult)
            dve.wait_ge(b_in, 16)
            for t in range(NT):
                e = slice(t * P, (t + 1) * P)
                dve.tensor_scalar(mean[:, e], bc[:, e], cols[:, 0, t:t + 1], g["inv_deg"][:, t:t + 1],
                                  ALU.is_equal, ALU.mult)
                if t:
                    dve.tensor_scalar(g["cont"][:, e], bc[:, e], bc[:, t * P - 1:t * P], None, ALU.is_equal)
            dve.memset(half[:, 0:1], 0.0).then_inc(mean_made, 1)
            dve.wait_ge(fetched, 16 * NT)
            linked(dve.tensor_copy(found_f[:], found[:]))
            linked(dve.tensor_scalar(tmp[:], found_f[:], 0.0, float(FAR), ALU.is_equal, ALU.mult))
            linked(dve.tensor_tensor(tmp[:], tmp[:], found_f[:], ALU.add))
            linked(dve.tensor_scalar(tmp[:], tmp[:], -1.0, None, ALU.add))
            linked(dve.tensor_copy(g["row"][:], tmp[:]))


def edge_table_tiles(sb):
    g = {}
    for name in ("inv_deg", "norm", "root_deg", "dinv", "f1"):
        g[name] = sb("g_" + name, [P, NT], F32)
    for name in ("src", "dst", "last", "row"):
        g[name] = sb("g_" + name, [P, NT], I32)
    g["cont"] = sb("g_cont", [P, NE], U8)
    return g


STAGES = {
    "A": ["A_load", "A_st", "A_ag", "A_ve", "A_rs", "A_xn", "A_t", "A_h", "A_l0", "A_e0", "A_m0", "A_h0",
          "A_l1", "A_e1", "A_m1", "A_h1"],
    "B": ["B_load", "B_l2", "B_e2", "B_m2", "B_h2", "B_l3", "B_e3", "B_m3", "B_h3", "B_tx", "B_x"],
    "C": ["C_st", "C_ag", "C_ve", "C_rs", "C_xn", "C_t", "C_h", "C_g1", "C_s1", "C_g2", "C_s2", "C_g3", "C_s3",
          "C_tx", "C_x"],
    "D": ["D_st", "D_ag", "D_ve", "D_rs", "D_xn", "D_t", "D_h", "D_na", "D_ra", "D_nb", "D_rb", "D_up", "D_u",
          "D_tx", "D_xa", "D_x"],
    "E": ["E_st", "E_ag", "E_ve", "E_rs", "E_xn", "E_r", "E_o", "E_store"],
}
STAGE_END = {"E": 0.85, "D": 0.94, "C": 0.96, "B": 0.98, "A": 0.90}


class Track:

    def __init__(self, sem, names, first=0):
        self.sem, self.names, self.first = sem, names, first

    def begin(self, eng):
        if self.names:
            eng.sem_inc(self.sem, len(self.names))

    def at(self, i, name, before=0):
        n = len(self.names)
        return (i - self.first) * n + ((1 - before) * n + self.names.index(name) + 1)


def stream_tiles(sb):
    wide = lambda n: sb("all_" + n, [P, CH], F32)
    b = {n: wide(n) for n in ("A_x", "A_xn", "A_m", "A_out", "B_x", "B_ex", "B_m", "B_h", "B_out", "C_xn",
                              "C_h", "C_out", "D_xn", "D_h", "D_out", "E_xn", "E_o")}
    b["A_h"] = b["A_x"]
    b["D_n"] = sb("all_D_n", [P, 2, CH], F32)
    b["C_s"], b["C_u"] = sb("all_C_s", [P, P], F32), sb("all_C_u", [P, P], F32)
    for s in "ACDE":
        b[s + "_st"], b[s + "_mv"] = sb(f"all_{s}_st", [P, TPC, 6], F32), sb(f"all_{s}_mv", [P, TPC, 2], F32)
        b[s + "_ve"], b[s + "_rs"] = sb(f"all_{s}_ve", [P, TPC], F32), sb(f"all_{s}_rs", [P, TPC], F32)
    return b


STREAM_PE = {"A": ["A_t", "A_l0", "A_l1"], "B": ["B_l2", "B_l3", "B_tx"],
             "C": ["C_t", "C_g1", "C_g2", "C_g3", "C_tx"], "D": ["D_t", "D_na", "D_nb", "D_up", "D_tx"], "E": []}
STREAM_ACT = {"A": ["A_h", "A_e0", "A_e1"], "B": ["B_e2", "B_e3"], "C": ["C_h", "C_s1", "C_s2", "C_s3"],
              "D": ["D_h", "D_ra", "D_rb", "D_u"], "E": []}
STREAM_DVE = {"A": ["A_st", "A_ag", "A_ve", "A_xn", "A_m0", "A_h0", "A_m1", "A_h1"],
              "B": ["B_m2", "B_h2", "B_m3", "B_h3", "B_x"],
              "C": ["C_st", "C_ag", "C_ve", "C_xn", "C_x"],
              "D": ["D_st", "D_ag", "D_ve", "D_xn", "D_xa", "D_x"],
              "E": ["E_st", "E_ag", "E_ve", "E_xn", "E_r", "E_o"]}
STREAM_POOL = {s: [f"{s}_rs"] if s in "ACDE" else [] for s in "ABCDE"}


class Stream:

    def __init__(self, nc, ctx, name, b, w, a, chunk0, first, ps):
        self.b, self.w, self.a, self.chunk0, self.ps = b, w, a, chunk0, ps
        self.first = first
        names = {"pe": STREAM_PE, "act": STREAM_ACT, "dve": STREAM_DVE, "pool": STREAM_POOL}
        self.tracks = {e: {s: Track(ctx.sem(f"{name}_all_{e}_{s}"), n[s], first[s]) for s in "ABCDE" if n[s]}
                       for e, n in names.items()}
        self.x_in = {s: ctx.sem(f"{name}_all_{s}_x_in") for s in "AB"}
        self.stored = ctx.sem(f"{name}_all_stored")
        self.held = ctx.sem(f"{name}_all_held")

    def begin(self, e, eng):
        for t in self.tracks[e].values():
            t.begin(eng)

    def wait(self, eng, e, what, i, before=0):
        t = self.tracks[e][what[0]]
        eng.wait_ge(t.sem, t.at(i, what, before))

    def mark(self, e, what, ins):
        ins.then_inc(self.tracks[e][what[0]].sem, 1)

    def rows(self, t, i, lag):
        chunk = self.chunk0 - lag + i
        r0 = min(chunk * CH, N - CH) if isinstance(i, int) else i * CH + (self.chunk0 - lag) * CH
        at = slice(r0, r0 + CH) if isinstance(r0, int) else bass.ds(r0, CH)
        return t[at, :].rearrange("(p t) f -> p (t f)", t=TPC)


def stream_sync(sp, s):
    b = s.b

    def load(stage, lag, freed):
        def step(i, active):
            s.wait(sp, *freed, i, before=1)
            sp.dma_start(b[stage + "_x"][:], s.rows(s.a["x"], i, lag)).then_inc(s.x_in[stage], 16)
        return step

    def store(i, active):
        s.wait(sp, "dve", "E_o", i)
        sp.dma_start(s.rows(s.a["out"], i, 4), b["E_o"][:]).then_inc(s.stored, 16)

    return {"A_load": load("A", 0, ("pe", "A_l1")), "B_load": load("B", 1, ("dve", "B_x")), "E_store": store}


def stream_gpsimd(pool, s):
    def root(stage):
        def step(i, active):
            s.wait(pool, "dve", stage + "_ve", i)
            s.mark("pool", stage + "_rs", pool.tensor_tensor(s.b[stage + "_rs"][:], s.b[stage + "_ve"][:],
                                                             s.w["power"][:, 0:TPC], ALU.pow))
        return step
    return {f"{k}_rs": root(k) for k in "ACDE"}


def stream_tensor(pe, s):
    b, w = s.b, s.w
    steps = {}

    def turn(what, src, waits):
        def step(i, active):
            for e, v in waits:
                s.wait(pe, e, v, i)
            if what in ("A_t", "C_t", "D_t"):
                s.wait(pe, "dve", {"A": "A_h1", "C": "C_x", "D": "D_xa"}[what[0]], i, before=1)
            for t in range(TPC):
                e = slice(t * P, (t + 1) * P)
                ins = pe.transpose(s.ps[what[0]][:, e], src[:, e], w["ident"][:])
            s.mark("pe", what, ins)
        steps[what] = step

    def product(what, lhsT, rhs, waits, n=CH):
        def step(i, active):
            for e, v, before in waits:
                s.wait(pe, e, v, i, before)
            for k, (l, r) in enumerate(zip(lhsT, rhs)):
                ins = pe.matmul(s.ps[what[0]][:, 0:n], l, r, start=k == 0, stop=k == len(lhsT) - 1)
            s.mark("pe", what, ins)
        steps[what] = step

    root = lambda l: [w["root"][:, l, :]]
    turn("A_t", b["A_xn"], [("dve", "A_xn")])
    product("A_l0", root(0), [b["A_h"][:]], [("act", "A_h", 0)])
    product("A_l1", root(1), [b["A_h"][:]], [("dve", "A_h0", 0)])
    product("B_l2", root(2), [b["A_out"][:]], [("dve", "A_h1", 1), ("dve", "B_x", 1)])
    product("B_l3", root(3), [b["B_h"][:]], [("dve", "B_h2", 0)])
    turn("B_tx", b["B_h"], [("dve", "B_h3")])
    turn("C_t", b["C_xn"], [("dve", "C_xn")])

    def g1(i, active):
        s.wait(pe, "act", "C_h", i)
        for t in range(TPC):
            ins = pe.matmul(s.ps["C"][t * HG:(t + 1) * HG, 0:P], w["w1"][:], b["C_h"][:, t * P:(t + 1) * P],
                            start=True, stop=True)
        s.mark("pe", "C_g1", ins)

    def g3(i, active):
        s.wait(pe, "act", "C_s2", i)
        for t in range(TPC):
            ins = pe.matmul(s.ps["C"][:, t * P:(t + 1) * P], w["wc"][:, t, :], b["C_u"][:], start=True, stop=True)
        s.mark("pe", "C_g3", ins)

    steps["C_g1"], steps["C_g3"] = g1, g3
    product("C_g2", [w["bd2"][:]], [b["C_s"][:]], [("act", "C_s1", 0)], P)
    turn("C_tx", b["C_h"], [("act", "C_s3")])
    turn("D_t", b["D_xn"], [("dve", "D_xn")])
    product("D_na", [w["wn1"][:, 0, 0:P]], [b["D_h"][:]], [("act", "D_h", 0)])
    product("D_nb", [w["wn1"][:, 0, P:2 * P]], [b["D_h"][:]], [("act", "D_ra", 0)])
    product("D_up", [w["wn2"][:, k, :] for k in range(2)], [b["D_n"][:, k, :] for k in range(2)], [("act", "D_rb", 0)])
    turn("D_tx", b["D_h"], [("act", "D_u")])
    return steps


def stream_scalar(act, s):
    b, w = s.b, s.w
    steps = {}

    def step(what, to, func, producer, n=CH, freed=None, **kw):
        def run(i, active):
            s.wait(act, "pe", producer, i)
            if freed:
                s.wait(act, *freed, i, before=1)
            s.mark("act", what, act.activation(to, s.ps[what[0]][:, 0:n], func, **kw))
        steps[what] = run

    step("A_h", b["A_h"][:], ACT.Relu, "A_t")
    for st, l in (("A", 0), ("A", 1), ("B", 2), ("B", 3)):
        step(f"{st}_e{l}", b["A_xn" if st == "A" else "B_ex"][:], ACT.Exp, f"{st}_l{l}", bias=w["b_rel"][:, l:l + 1])
    step("C_h", b["C_h"][:], ACT.Relu, "C_t")
    step("C_s1", b["C_s"][:], ACT.Tanh, "C_g1", P, bias=w["iso_b1"][:], scale=0.5)
    step("C_s2", b["C_u"][:], ACT.Tanh, "C_g2", P, bias=w["iso_b2"][:], scale=0.25)
    step("C_s3", b["C_h"][:], ACT.Tanh, "C_g3", bias=w["iso_bz"][:], scale=0.25)
    step("D_h", b["D_h"][:], ACT.Relu, "D_t")
    step("D_ra", b["D_n"][:, 0, :], ACT.Relu, "D_na", freed=("dve", "D_x"), bias=w["bn1"][:, 0:1])
    step("D_rb", b["D_n"][:, 1, :], ACT.Relu, "D_nb", bias=w["bn1"][:, 1:2])
    step("D_u", b["D_h"][:], ACT.Identity, "D_up", bias=w["bn2h"][:])
    return steps


def stream_vector(dve, s):
    b, w = s.b, s.w
    steps = {}

    def norm(stage, x, made, turned=None):
        st, mv, ve, rs, xn = (b[stage + n] for n in ("_st", "_mv", "_ve", "_rs", "_xn"))

        def stats(i, active):
            made(i)
            for t in range(TPC):
                ins = dve.bn_stats(st[:, t, :], x[:, t * D:(t + 1) * D])
            s.mark("dve", stage + "_st", ins)

        def aggregate(i, active):
            s.wait(dve, "dve", stage + "_st", i)
            dve.sem_inc(s.held, 1)
            for t in range(TPC):
                ins = dve.bn_aggr(mv[:, t, :], st[:, t, :])
            s.mark("dve", stage + "_ag", ins)

        def add_eps(i, active):
            s.wait(dve, "dve", stage + "_ag", i)
            s.mark("dve", stage + "_ve", dve.tensor_scalar(ve[:], mv[:, :, 1], EPS, None, ALU.add))

        def normalise(i, active):
            s.wait(dve, "pool", stage + "_rs", i)
            for t in range(TPC):
                e = slice(t * D, (t + 1) * D)
                ins = dve.tensor_scalar(xn[:, e], x[:, e], mv[:, t, 0:1], rs[:, t:t + 1], ALU.subtract, ALU.mult)
            s.mark("dve", stage + "_xn", ins)

        steps[stage + "_st"], steps[stage + "_ag"] = stats, aggregate
        steps[stage + "_ve"], steps[stage + "_xn"] = add_eps, normalise

    def simple(what, waits, op, after=None):
        def step(i, active):
            for e, v, before in waits:
                s.wait(dve, e, v, i, before)
            if after and after[1][0] in active:
                s.wait(dve, *after, i)
            s.mark("dve", what, op())
        steps[what] = step

    def elu(stage, l, ex, m, to, after=None):
        simple(f"{stage}_m{l}", [("act", f"{stage}_e{l}", 0)],
               lambda: dve.tensor_scalar(m[:], ex[:], 1.0, -1.0, ALU.min, ALU.add))
        simple(f"{stage}_h{l}", [("dve", f"{stage}_m{l}", 0)],
               lambda: dve.scalar_tensor_tensor(out=to[:], in0=s.ps[stage][:], scalar=w["b_rel"][:, l:l + 1], in1=m[:],
                                                op0=ALU.add, op1=ALU.max), after)

    norm("A", b["A_x"], lambda i: dve.wait_ge(s.x_in["A"], (i - s.first["A"]) * 16 + 16))
    elu("A", 0, b["A_xn"], b["A_m"], b["A_h"])
    elu("A", 1, b["A_xn"], b["A_m"], b["A_out"], ("pe", "B_l2"))
    elu("B", 2, b["B_ex"], b["B_m"], b["B_h"])
    elu("B", 3, b["B_ex"], b["B_m"], b["B_h"])

    def x1(i, active):
        s.wait(dve, "pe", "B_tx", i)
        dve.wait_ge(s.x_in["B"], (i - s.first["B"]) * 16 + 16)
        if "C" in active:
            s.wait(dve, "dve", "C_x", i)
        s.mark("dve", "B_x", dve.tensor_tensor(b["B_out"][:], s.ps["B"][:], b["B_x"][:], ALU.add))

    steps["B_x"] = x1
    norm("C", b["B_out"], lambda i: s.wait(dve, "dve", "B_x", i, before=1))
    simple("C_x", [("pe", "C_tx", 0)],
           lambda: dve.scalar_tensor_tensor(out=b["C_out"][:], in0=s.ps["C"][:], scalar=0.5, in1=b["B_out"][:],
                                            op0=ALU.mult, op1=ALU.add), ("dve", "D_x"))
    norm("D", b["C_out"], lambda i: s.wait(dve, "dve", "C_x", i, before=1))
    simple("D_xa", [("pe", "D_tx", 0)],
           lambda: dve.scalar_tensor_tensor(out=b["D_n"][:, 0, :], in0=b["D_xn"][:], scalar=0.0, in1=s.ps["D"][:],
                                            op0=ALU.max, op1=ALU.add))
    simple("D_x", [("dve", "D_xa", 0)],
           lambda: dve.tensor_tensor(b["D_out"][:], b["C_out"][:], b["D_n"][:, 0, :], ALU.add), ("dve", "E_o"))
    norm("E", b["D_out"], lambda i: s.wait(dve, "dve", "D_x", i, before=1))
    simple("E_r", [("dve", "E_xn", 0)],
           lambda: dve.tensor_scalar(b["E_xn"][:], b["E_xn"][:], 0.0, ALPHA, ALU.max, ALU.mult))

    def out(i, active):
        s.wait(dve, "dve", "E_r", i)
        dve.wait_ge(s.stored, (i - s.first["E"]) * 16 + 16)
        s.mark("dve", "E_o", dve.tensor_tensor(b["E_o"][:], b["D_out"][:], b["E_xn"][:], ALU.add))

    steps["E_o"] = out
    return steps


U = 5
PASSES = NCH // U
GROUPS = ((0, 1, 2), (3, 4))
LN = ["st", "ag", "ve", "rs", "xn"]
SLOT_STEPS = {
    "start": LN + ["t", "hh", "row"],
    "layer": ["agg", "sc", "ca", "l", "e", "m", "h", "tx", "y", "row"],
    "layer3": ["agg", "sc", "ca", "l", "e", "m", "h", "tx", "x"] + LN + ["t", "hh", "g", "row"],
    "gcn1": ["agg", "sc", "ca", "b", "tr", "a", "u", "ub", "s", "sg", "row"],
    "gcn2": ["agg", "sc", "ca", "b", "tr", "a", "u", "tu", "uT", "z", "ub", "s", "sg", "row"],
    "gcn3": ["agg", "sc", "ca", "b", "tr", "a", "u", "tu", "uT", "z", "tT", "tx", "x"] + LN + ["row", "t", "hh"],
    "edge": ["tv", "vT", "ma", "qa", "mb", "qb", "mc", "qc", "md", "qd", "m3", "msg", "agg", "sc", "ca", "na", "ra",
             "nb", "rb", "up", "uT", "tx", "xa", "x"] + LN + ["row", "c"],
    "hop": ["agg", "sc", "ca", "tx", "row"],
    "last_hop": ["agg", "sc", "ca", "tx", "row", "o"],
}
SLOT_ENGINE = {
    "pe": {"agg", "l", "tx", "t", "g", "tr", "tu", "z", "tv", "ma", "mb", "mc", "md", "m3", "na", "nb", "up"},
    "act": {"e", "y", "hh", "s", "uT", "tT", "vT", "qa", "qb", "qc", "qd", "ra", "rb"},
    "pool": {"rs"},
}
LAST_READ = {"start": ("act", "hh"), "layer": ("dve", "row"), "layer3": ("dve", "row"), "gcn1": ("dve", "a"),
             "gcn2": ("dve", "ub"), "gcn3": ("act", "hh"), "edge": ("dve", "xa"), "hop": ("dve", "row"),
             "last_hop": ("dve", "row")}


def merged(kind, stages, last_pass):
    placed = []
    slots = [(name, u) for g in GROUPS for name in SLOT_STEPS[kind] for u in g]
    for k, (name, u) in enumerate(slots):
        placed.append((k / len(slots), (name, u)))
    where = {s: p for p, s in placed}
    first_pe = next(n for n in SLOT_STEPS[kind] if n in SLOT_ENGINE["pe"])
    use = "agg" if "agg" in SLOT_STEPS[kind] else "xn" if kind == "start" else first_pe
    for u in range(U):
        p = where[(use if kind != "start" else "row", u)]
        placed.append((where[(SLOT_STEPS[kind][0], u)] - 1e-3, ("load", u)))
        if not last_pass:
            placed.append((p + 1e-4, ("ahead", u)))
            for t in range(TPC):
                lo, hi = p + 2e-3, 1.0
                placed.append((max(lo, (u * TPC + t + 1) / (U * TPC + 1)), ("gather%d" % t, u)))
        placed.append((where[(SLOT_STEPS[kind][-1], u)] + 1e-5, ("store", u)))
    for s in stages:
        n = len(STAGES[s])
        for k, name in enumerate(STAGES[s]):
            placed.append(((k + 1) / n * STAGE_END[s] + 1e-6 * ord(s), (name, None)))
    placed.sort(key=lambda x: x[0])
    return [s for _, s in placed]


def slot_pass(nc, a, w, g, kind, shared, stream_plan, table=None, ahead=None, out_table=None, xd=None,
              rows_in=None, layer=0):
    last = PASSES - 1
    gcn = kind in ("gcn1", "gcn2", "gcn3")
    width = HG if gcn else D
    row_width = TPC * HG if kind in ("gcn1", "gcn2") else CH
    YT = shared["YT"]
    has_x = kind in ("layer3", "gcn3", "edge", "last_hop")
    makes_x = kind in ("start", "layer3", "gcn3", "edge")
    has_agg = kind != "start"
    name = kind + str(layer)
    steps_ = SLOT_STEPS[kind]
    chunk0, active_in = stream_plan
    first = {s: next((i for i in range(PASSES) if s in active_in[i]), 0) for s in "ABCDE"}
    with Phase(nc) as ctx:
        def sb(n, shape, dt=F32):
            return [ctx.enter_context(nc.sbuf_tensor(f"{name}_{n}{u}", shape, dt)) for u in range(U)]
        sem = lambda n: ctx.sem(f"{name}_{n}")
        per_u = lambda n: [sem(f"{n}{u}") for u in range(U)]
        half_of = lambda tiles_, k: [t[:, k, :] for t in tiles_]
        wide = lambda n: sb(n, [P, CH])
        if kind == "start":
            xr, xn, rows = wide("xr"), wide("xn"), wide("rows")
        elif kind in ("layer", "layer3"):
            V, aggT, em = wide("V"), wide("aggT"), wide("em")
            ex, hT, xn, rows = aggT, aggT, em, em
            if kind == "layer3":
                xr = wide("xr")
                rows = sb("rows", [P, P])
                row_width = P
        elif gcn:
            V, aggT, own, bA, bB, bU = sb("V", [P, P]), wide("aggT"), *(sb(n, [P, P]) for n in ("own", "bA", "bB", "bU"))
            if kind == "gcn3":
                xr, xn, rows = wide("xr"), wide("xn"), aggT
                ex = xn
            else:
                rows = sb("rows", [P, P])
        elif kind == "edge":
            mB, mA, hT, xr, hr = sb("mB", [P, 2, CH]), sb("mA", [P, 2, CH]), wide("hT"), wide("xr"), wide("hr")
            V, aggT = half_of(mB, 0), half_of(mB, 1)
            em, ex, xn, rows = half_of(mA, 0), half_of(mA, 1), hT, hr
        else:
            V, aggT, rows = wide("V"), wide("aggT"), wide("rows")
            if kind == "last_hop":
                xr = wide("xr")
        if has_agg:
            mean = wide("mean")
            carry = sb("carry", [P, TPC])
        st, mv, ve, rs = sb("st", [P, TPC, 6]), sb("mv", [P, TPC, 2]), sb("ve", [P, TPC]), sb("rs", [P, TPC])
        idx = sb("idx", [P, TPC], I32)
        banks = [ctx.enter_context(nc.psum_tensor(f"{name}_ps{k}", [P, CH], F32)) for k in range(4)]
        ps = [banks[u % 4] for u in range(U)]
        stream_ps = {s: ctx.enter_context(nc.psum_tensor(f"{name}_all_ps{s}", [P, CH], F32)) for s in "ABCD"}
        engine_of = lambda n: next((e for e, names in SLOT_ENGINE.items() if n in names), "dve")
        tracks = {e: [Track(s_, [n for n in steps_ if engine_of(n) == e]) for s_ in per_u(e + "_done")]
                  for e in ("pe", "act", "pool", "dve")}
        stream = Stream(nc, ctx, name, shared["stream"], w, a, chunk0, first, stream_ps)
        z_in, v_in, x_in, row_out, x_out = (per_u(n) for n in ("z_in", "v_in", "x_in", "row_out", "x_out"))
        idx_made = per_u("idx_made")
        held, link = sem("held"), sem("link")
        block = ctx.enter_context(nc.Block())

        def wait(eng, e, what, i, u, before=0):
            eng.wait_ge(tracks[e][u].sem, tracks[e][u].at(i, what, before))

        def mark(e, u, ins):
            ins.then_inc(tracks[e][u].sem, 1)

        def begin(e, eng):
            for t in tracks[e]:
                t.begin(eng)
            stream.begin(e, eng)

        def run(eng, steps, before=None):
            def one_pass(i, active, last_pass):
                for what, u in merged(kind, active, last_pass):
                    if what in steps:
                        if u is None:
                            steps[what](i, active)
                        else:
                            steps[what](i, u)

            i = 0
            while i < last:
                j = i + 1
                while j < last and active_in[j] == active_in[i]:
                    j += 1
                if j - i > 1:
                    with eng.Fori(i, j) as k:
                        one_pass(k, active_in[i], False)
                else:
                    one_pass(i, active_in[i], False)
                i = j
            one_pass(last, active_in[last], True)

        def chunk_rows(t, i, u):
            return t[bass.ds(i * (U * CH) + u * CH, CH), :].rearrange("(p t) f -> p (t f)", t=TPC)

        def cols(i, u, t=0, n=CH):
            return bass.ds(i * (U * CH) + (u * CH + t * P), n)

        def columns(i, u):
            return bass.ds(i * (U * TPC) + u * TPC, TPC)

        def factors(name, i, u):
            return g[name][:, columns(i, u)].unsqueeze(2).to_broadcast([P, TPC, HG])

        def factor(name, i, u, t):
            return g[name][:, bass.ds(i * (U * TPC) + (u * TPC + t), 1)]

        @block.sync
        def _(sp):
            def ahead_of(i, u):
                if not has_agg:
                    return
                wait(sp, "pe", "agg", i, u, before=1)
                sp.dma_start(mean[u][:], shared["mean"][:, cols(i, u)]).then_inc(z_in[u], 16)
                sp.dma_start(V[u][:, 0:TPC * width], chunk_rows(ahead, i, u)).then_inc(z_in[u], 16)

            def load(i, u):
                if has_x:
                    if kind == "last_hop":
                        wait(sp, "dve", "o", i, u, before=1)
                    else:
                        sp.wait_ge(x_out[u], i * 16 + 16)
                    sp.dma_start(xr[u][:], chunk_rows(xd, i, u)).then_inc(x_in[u], 16)
                if kind == "edge":
                    sp.wait_ge(row_out[u], i * 16 + 16)
                    sp.sem_inc(held, 1)
                    wait(sp, "dve", "c", i, u, before=1)
                    sp.sem_inc(held, 1)
                    sp.dma_start(hr[u][:], chunk_rows(rows_in, i, u)).then_inc(x_in[u], 16)
                if gcn:
                    wait(sp, "dve", "b", i, u, before=1)
                    sp.dma_start(own[u][:], chunk_rows(rows_in, i, u)).then_inc(x_in[u], 16)

            def store(i, u):
                if makes_x:
                    wait(sp, "dve", "st" if kind == "start" else "x", i, u)
                    sp.dma_start(chunk_rows(xd, i, u), xr[u][:]).then_inc(x_out[u], 16)
                if kind != "last_hop":
                    wait(sp, "dve", "row", i, u)
                    sp.dma_start(chunk_rows(out_table, i, u), rows[u][:, 0:row_width]).then_inc(row_out[u], 16)

            for u in range(U):
                sp.sem_inc(x_out[u], 16)
                if kind != "last_hop":
                    sp.sem_inc(row_out[u], 16)
            sp.sem_inc(stream.stored, 16)
            for u in range(U):
                ahead_of(0, u)
            run(sp, {"load": load, "store": store, "ahead": lambda i, u: ahead_of(i + 1, u), **stream_sync(sp, stream)})
            for u in range(U):
                sp.wait_ge(x_out[u], 16 * PASSES + 16 if makes_x else 16)
                if kind != "last_hop":
                    sp.wait_ge(row_out[u], 16 * PASSES + 16)
            sp.wait_ge(stream.stored, 16 + 16 * sum("E" in x for x in active_in))

        @block.gpsimd
        def _(pool):
            bound = pool.to_reg((N if kind == "start" else NE) - 1)
            begin("pool", pool)

            def gather(i, u, t):
                if t == 0:
                    if kind == "start":
                        wait(pool, "dve", "st", i, u, before=1)
                    else:
                        wait(pool, "pe", "agg", i, u, before=1)
                    pool.tensor_copy(idx[u][:], g["dst" if kind == "start" else "row"][:, columns(i, u)]).then_inc(
                        idx_made[u], 1)
                    pool.wait_ge(idx_made[u], i + 1)
                    pool.sem_inc(held, 1)
                    if kind == "start":
                        pool.wait_ge(x_out[u], i * 16 + 16)
                        pool.sem_inc(held, 1)
                        wait(pool, "dve", "xn", i, u, before=1)
                    else:
                        pool.wait_ge(z_in[u], i * 32 + 32)
                    pool.sem_inc(held, 1)
                to, sem_, of = (xr[u], x_in[u], a["x"]) if kind == "start" else (V[u], v_in[u], table)
                pool.indirect_dma_start(to[:, t * width:(t + 1) * width], None, of,
                                        bass.IndirectOffsetOnAxis(idx[u][:, t:t + 1], 0),
                                        bounds_check=bound, oob_is_err=False).then_inc(sem_, 16)

            def root(i, u):
                wait(pool, "dve", "ve", i, u)
                mark("pool", u, pool.tensor_tensor(rs[u][:], ve[u][:], w["power"][:, 0:TPC], ALU.pow))

            for u in range(U):
                for t in range(TPC):
                    gather(0, u, t)
            steps = {"gather%d" % t: (lambda i, u, t=t: gather(i + 1, u, t)) for t in range(TPC)}
            run(pool, {**steps, "rs": root, **stream_gpsimd(pool, stream)})

        @block.tensor
        def _(pe):
            begin("pe", pe)
            first_pe = next(n for n in steps_ if engine_of(n) == "pe")

            def step(what, waits, op):
                def run_(i, u):
                    for e, v in waits:
                        if e == "v_in":
                            pe.wait_ge(v_in[u], i * 64 + 64)
                        elif e == "mean_in":
                            pe.wait_ge(z_in[u], i * 32 + 32)
                        else:
                            wait(pe, e, v, i, u)
                    if what == first_pe:
                        wait(pe, *LAST_READ[kind], i, u, before=1)
                        if u == 0:
                            wait(pe, *LAST_READ[kind], i, 4, before=1)
                        if u == 4:
                            wait(pe, *LAST_READ[kind], i, 0)
                    if what == "tr":
                        pe.sem_inc(held, 1)
                    mark("pe", u, op(i, u))
                return run_

            def turn(src):
                def op(i, u):
                    for t in range(TPC):
                        e = slice(t * P, (t + 1) * P)
                        ins = pe.transpose(ps[u][:, e], src[u][:, e], w["ident"][:])
                    return ins
                return op

            def average(i, u):
                for t in range(TPC):
                    e = slice(t * P, (t + 1) * P)
                    ins = pe.matmul(ps[u][0:width, e], V[u][:, t * width:(t + 1) * width], mean[u][:, e],
                                    start=True, stop=True)
                return ins

            def pair(w1, rhs1, w2):
                def op(i, u):
                    pe.matmul(ps[u][:], w1, rhs1[u][:], start=True, stop=False)
                    return pe.matmul(ps[u][:], w2, YT[:, cols(i, u)], start=False, stop=True)
                return op

            def halves(wt, src, c):
                def op(i, u):
                    for k in range(2):
                        ins = pe.matmul(ps[u][:], wt[:, k, c], src[u][:, k, :], start=k == 0, stop=k == 1)
                    return ins
                return op

            def turn_narrow(i, u):
                for t in range(TPC):
                    ins = pe.transpose(ps[u][:, t * HG:(t + 1) * HG], aggT[u][0:HG, t * P:(t + 1) * P],
                                       w["ident"][0:HG, 0:HG])
                return ins

            def z(i, u):
                if kind == "gcn2":
                    return pe.matmul(ps[u][:, 0:P], bA[u][:], w["bd2"][:], start=True, stop=True)
                for t in range(TPC):
                    ins = pe.matmul(ps[u][:, t * P:(t + 1) * P], w["wc"][:, t, :], bA[u][:], start=True, stop=True)
                return ins

            def first_gcn(i, u):
                for t in range(TPC):
                    ins = pe.matmul(ps[u][:, t * HG:(t + 1) * HG], hT[u][:, t * P:(t + 1) * P], w["w1"][:],
                                    start=True, stop=True)
                return ins

            def messages(i, u):
                for t in range(TPC):
                    e = slice(t * P, (t + 1) * P)
                    for k in range(2):
                        ins = pe.matmul(ps[u][:, e], mB[u][:, k, e], w["wm3"][:, k, :], start=k == 0, stop=k == 1)
                return ins

            lo, hi = slice(0, P), slice(P, 2 * P)
            steps = {"agg": step("agg", [("dve", "msg"), ("mean_in", 0)] if kind == "edge"
                                 else [("v_in", 0), ("mean_in", 0)], average)} if has_agg else {}
            if kind in ("layer", "layer3"):
                steps["l"] = step("l", [("dve", "ca")], pair(w["rel"][:, layer, :], aggT, w["root"][:, layer, :]))
                steps["tx"] = step("tx", [("dve", "h")], turn(hT))
            if kind in ("start", "layer3", "gcn3"):
                steps["t"] = step("t", [("dve", "xn")], turn(xn))
            if kind == "layer3":
                steps["g"] = step("g", [("act", "hh")], first_gcn)
            if gcn:
                steps["tr"] = step("tr", [("dve", "ca")], turn_narrow)
            if kind in ("gcn2", "gcn3"):
                steps["tu"] = step("tu", [("dve", "u")], lambda i, u: pe.transpose(ps[u][:, 0:P], bU[u][:], w["ident"][:]))
                steps["z"] = step("z", [("act", "uT")], z)
            if kind == "gcn3":
                steps["tx"] = step("tx", [("act", "tT")], turn(ex))
            if kind in ("hop", "last_hop"):
                steps["tx"] = step("tx", [("dve", "ca")], turn(aggT))
            if kind == "edge":
                steps["tv"] = step("tv", [("v_in", 0)], turn(V))
                steps["ma"] = step("ma", [("act", "vT")], pair(w["wm1"][:, 0, lo], hT, w["wm1"][:, 1, lo]))
                steps["mb"] = step("mb", [("act", "qa")], pair(w["wm1"][:, 0, hi], hT, w["wm1"][:, 1, hi]))
                steps["mc"] = step("mc", [("act", "qb")], halves(w["wm2"], mA, lo))
                steps["md"] = step("md", [("act", "qc")], halves(w["wm2"], mA, hi))
                steps["m3"] = step("m3", [("act", "qd")], messages)
                steps["na"] = step("na", [("dve", "ca")], pair(w["wn1"][:, 1, lo], aggT, w["wn1"][:, 0, lo]))
                steps["nb"] = step("nb", [("act", "ra")], pair(w["wn1"][:, 1, hi], aggT, w["wn1"][:, 0, hi]))
                steps["up"] = step("up", [("act", "rb")], halves(w["wn2"], mA, slice(0, P)))
                steps["tx"] = step("tx", [("act", "uT")], turn(em))
            run(pe, {**steps, **stream_tensor(pe, stream)})

        @block.scalar
        def _(act):
            begin("act", act)

            def step(to, func, producer, n=CH, freed=None, **kw):
                def run_(i, u):
                    wait(act, "pe", producer, i, u)
                    if freed:
                        wait(act, *freed, i, u, before=1)
                    mark("act", u, act.activation(to(i, u), ps[u][:, 0:n], func, **kw))
                return run_

            def keep(i, u):
                wait(act, "dve", "h", i, u)
                mark("act", u, act.activation(YT[:, cols(i, u)], hT[u][:], ACT.Identity))

            def sigmoid_half(i, u):
                wait(act, "dve", "ub", i, u)
                mark("act", u, act.activation(bA[u][:], bU[u][:], ACT.Tanh, scale=0.5))

            steps = {}
            if kind in ("layer", "layer3"):
                steps["e"] = step(lambda i, u: ex[u][:], ACT.Exp, "l", bias=w["b_rel"][:, layer:layer + 1])
                steps["y"] = keep
            if kind in ("start", "gcn3"):
                steps["hh"] = step(lambda i, u: YT[:, cols(i, u)], ACT.Relu, "t")
            if kind == "layer3":
                steps["hh"] = step(lambda i, u: hT[u][:], ACT.Relu, "t")
            if gcn:
                steps["s"] = sigmoid_half
                steps["uT"] = step(lambda i, u: bA[u][:], ACT.Identity, "tu", P)
            if kind == "gcn3":
                steps["tT"] = step(lambda i, u: ex[u][:], ACT.Tanh, "z", bias=w["dst_bz"][:], scale=0.5)
            if kind == "edge":
                steps["vT"] = step(lambda i, u: hT[u][:], ACT.Identity, "tv", freed=("dve", "row"))
                for k, (m, q) in enumerate((("ma", "qa"), ("mb", "qb"))):
                    steps[q] = step(lambda i, u, k=k: mA[u][:, k, :], ACT.Relu, m, bias=w["bm1"][:, k:k + 1])
                for k, (m, q) in enumerate((("mc", "qc"), ("md", "qd"))):
                    steps[q] = step(lambda i, u, k=k: mB[u][:, k, :], ACT.Relu, m, bias=w["bm2"][:, k:k + 1])
                for k, (m, q) in enumerate((("na", "ra"), ("nb", "rb"))):
                    steps[q] = step(lambda i, u, k=k: mA[u][:, k, :], ACT.Relu, m, bias=w["bn1"][:, k:k + 1])
                steps["uT"] = step(lambda i, u: em[u][:], ACT.Identity, "up", bias=w["bn2h"][:])
            run(act, {**steps, **stream_scalar(act, stream)})

        @block.vector
        def _(dve):
            begin("dve", dve)

            def stored(i, u):
                dve.wait_ge(row_out[u], i * 16 + 16)

            def carry_on(i, u):
                wait(dve, "pe", "agg", i, u)
                wait(dve, "dve", "sc", i, u - 1 if u else U - 1, before=0 if u else 1)
                wait(dve, "dve", "ca", i, u, before=1)
                before = carry[u - 1 if u else U - 1][0:width, TPC - 1:TPC]
                ends = g["cont"][0:width, cols(i, u)].rearrange("p (t e) -> p t e", e=P)[:, :, P - 1]
                sums = ps[u][0:width, :].rearrange("p (t e) -> p t e", e=P)[:, :, P - 1]
                mark("dve", u, dve.tensor_tensor_scan(carry[u][0:width, :], ends, sums, before, ALU.mult, ALU.add))

            def complete(i, u):
                wait(dve, "dve", "sc", i, u)
                if kind == "layer":
                    wait(dve, "act", "y", i, u, before=1)
                if kind == "gcn3":
                    stored(i, u)
                for t in range(TPC):
                    before = (carry[u][0:width, t - 1:t] if t else
                              carry[u - 1 if u else U - 1][0:width, TPC - 1:TPC])
                    e = slice(t * P, (t + 1) * P)
                    ins = dve.scalar_tensor_tensor(out=aggT[u][0:width, e], in0=g["cont"][0:width, cols(i, u, t, P)],
                                                   scalar=before, in1=ps[u][0:width, e], op0=ALU.mult, op1=ALU.add)
                mark("dve", u, ins)

            def stats(i, u):
                if kind == "start":
                    dve.wait_ge(x_in[u], i * 64 + 64)
                else:
                    wait(dve, "dve", "x", i, u)
                for t in range(TPC):
                    ins = dve.bn_stats(st[u][:, t, :], xr[u][:, t * D:(t + 1) * D])
                mark("dve", u, ins)

            def aggregate(i, u):
                wait(dve, "dve", "st", i, u)
                dve.sem_inc(held, 1)
                for t in range(TPC):
                    ins = dve.bn_aggr(mv[u][:, t, :], st[u][:, t, :])
                mark("dve", u, ins)

            def add_eps(i, u):
                wait(dve, "dve", "ag", i, u)
                mark("dve", u, dve.tensor_scalar(ve[u][:], mv[u][:, :, 1], EPS, None, ALU.add))

            def normalise(i, u):
                wait(dve, "pool", "rs", i, u)
                if kind == "start":
                    wait(dve, "pe", "t", i, u, before=1)
                for t in range(TPC):
                    e = slice(t * D, (t + 1) * D)
                    ins = dve.tensor_scalar(xn[u][:, e], xr[u][:, e], mv[u][:, t, 0:1], rs[u][:, t:t + 1],
                                            ALU.subtract, ALU.mult)
                mark("dve", u, ins)

            def step(waits, op, free_rows=False):
                def run_(i, u):
                    for e, v in waits:
                        if e == "x_in":
                            dve.wait_ge(x_in[u], i * v + v)
                        else:
                            wait(dve, e, v, i, u)
                    if free_rows:
                        stored(i, u)
                    mark("dve", u, op(i, u))
                return run_

            def scaled(to, of, name_):
                return lambda i, u: dve.tensor_tensor(tiles(to[u][:, 0:P]), tiles(of[u][:, 0:P]), factors(name_, i, u),
                                                      ALU.mult)

            def by_row(wt, n):
                return w[wt][:].unsqueeze(1).to_broadcast([P, TPC, n])

            def relu_times_norm(i, u):
                for t in range(TPC):
                    e = slice(t * D, (t + 1) * D)
                    ins = dve.tensor_scalar(rows[u][:, e], xn[u][:, e], 0.0, factor("norm", i, u, t), ALU.max, ALU.mult)
                return ins

            def output(i, u):
                for t in range(TPC):
                    e = slice(t * D, (t + 1) * D)
                    ins = dve.scalar_tensor_tensor(out=YT[:, cols(i, u, t, P)], in0=rows[u][:, e],
                                                   scalar=factor("root_deg", i, u, t), in1=xr[u][:, e],
                                                   op0=ALU.mult, op1=ALU.add)
                return ins

            steps = {"st": stats, "ag": aggregate, "ve": add_eps, "xn": normalise, "sc": carry_on, "ca": complete}
            if kind in ("start", "gcn3"):
                steps["row"] = step([("dve", "xn")], lambda i, u: dve.tensor_scalar(
                    rows[u][:], xn[u][:], 0.0, None, ALU.max), free_rows=True)
            if kind in ("layer", "layer3"):
                steps["m"] = step([("act", "e")], lambda i, u: dve.tensor_scalar(
                    em[u][:], ex[u][:], 1.0, -1.0, ALU.min, ALU.add), free_rows=kind == "layer")
                steps["h"] = step([("dve", "m")], lambda i, u: dve.scalar_tensor_tensor(
                    out=hT[u][:], in0=ps[u][:], scalar=w["b_rel"][:, layer:layer + 1], in1=em[u][:],
                    op0=ALU.add, op1=ALU.max))
            if kind == "layer":
                steps["row"] = step([("pe", "tx")], lambda i, u: dve.tensor_copy(rows[u][:], ps[u][:]))
            if kind == "layer3":
                steps["x"] = step([("pe", "tx"), ("x_in", 16)], lambda i, u: dve.tensor_tensor(
                    xr[u][:], ps[u][:], xr[u][:], ALU.add))
                steps["row"] = step([("pe", "g")], scaled(rows, ps, "dinv"), free_rows=True)
            if gcn:
                steps["a"] = step([("pe", "tr")], scaled(bA, ps, "f1"))
                steps["b"] = step([("x_in", 32 if kind == "gcn3" else 16)], scaled(bB, own, "dinv"))
                steps["u"] = step([("dve", "a"), ("dve", "b")], lambda i, u: dve.tensor_tensor(
                    bU[u][:], bA[u][:], bB[u][:], ALU.add))
            if kind in ("gcn1", "gcn2"):
                first_ = kind == "gcn1"
                steps["ub"] = step([("dve", "u")] if first_ else [("pe", "z")], lambda i, u: dve.tensor_tensor(
                    tiles(bU[u][:]), tiles((bU if first_ else ps)[u][:, 0:P]), by_row("b1row" if first_ else "b2row", HG),
                    ALU.add))
                steps["sg"] = step([("act", "s")], lambda i, u: dve.tensor_scalar(
                    bB[u][:], bA[u][:], 0.5, 0.5, ALU.mult, ALU.add))
                steps["row"] = step([("dve", "sg")], scaled(rows, bB, "dinv"), free_rows=True)
            if kind == "gcn3":
                steps["x"] = step([("pe", "tx"), ("x_in", 32)], lambda i, u: dve.scalar_tensor_tensor(
                    out=xr[u][:], in0=ps[u][:], scalar=0.5, in1=xr[u][:], op0=ALU.mult, op1=ALU.add))
            if kind == "edge":
                steps["msg"] = step([("pe", "m3")], lambda i, u: dve.tensor_tensor(
                    tiles(V[u][:]), tiles(ps[u][:]), by_row("bm3row", D), ALU.add))
                steps["xa"] = step([("pe", "tx"), ("x_in", 32)], lambda i, u: dve.tensor_tensor(
                    ex[u][:], ps[u][:], hr[u][:], ALU.add))
                steps["x"] = step([("dve", "xa")], lambda i, u: dve.tensor_tensor(
                    xr[u][:], xr[u][:], ex[u][:], ALU.add))
                steps["row"] = step([("dve", "xn")], relu_times_norm)
                steps["c"] = step([("dve", "row")], lambda i, u: dve.tensor_scalar(
                    YT[:, cols(i, u)], rows[u][:], ALPHA, None, ALU.mult))
            if kind in ("hop", "last_hop"):
                steps["row"] = step([("pe", "tx")], lambda i, u: dve.scalar_tensor_tensor(
                    out=rows[u][:], in0=ps[u][:], scalar=1.0 - ALPHA, in1=YT[:, cols(i, u)], op0=ALU.mult,
                    op1=ALU.add), free_rows=kind == "hop")
            if kind == "last_hop":
                steps["o"] = step([("dve", "row"), ("x_in", 16)], output)
            if has_agg:
                dve.memset(carry[U - 1][:], 0.0).then_inc(link, 1)
                dve.wait_ge(link, 1)
            mine = {n: f for n, f in steps.items() if n in steps_}
            run(dve, {**mine, **stream_vector(dve, stream)})


def write_rows(nc, a, g, rows):
    with Phase(nc) as ctx:
        written = ctx.sem("rows_written")
        block = ctx.enter_context(nc.Block())

        @block.gpsimd
        def _(pool):
            bound = pool.to_reg(N - 1)
            for t in range(NT):
                pool.indirect_dma_start(a["out"], bass.IndirectOffsetOnAxis(g["last"][:, t:t + 1], 0),
                                        rows[:, t * D:(t + 1) * D], None,
                                        bounds_check=bound, oob_is_err=False).then_inc(written, 16)
            pool.wait_ge(written, 16 * NT)


def complete_slots(nc, YT, dst_flat):
    with Phase(nc) as ctx:
        bc = ctx.enter_context(nc.sbuf_tensor("fix_dst", [P, NE], F32))
        mask = ctx.enter_context(nc.sbuf_tensor("fix_mask", [P, P], F32))
        diff = ctx.enter_context(nc.sbuf_tensor("fix_diff", [P, P], F32))
        bc_in = ctx.sem("fix_dst_in")
        ev = Events(ctx.sem("fix_done"), ["mask", "diff", "slots"], 1, 1)
        block = ctx.enter_context(nc.Block())

        @block.sync
        def _(sp):
            sp.dma_start(bc[:], dst_flat.partition_broadcast(P)).then_inc(bc_in, 16)

        @block.vector
        def _(dve):
            dve.sem_inc(ev.sem, ev.size)
            dve.wait_ge(bc_in, 16)
            with dve.Fori(0, NT - 1) as i:
                tile, following = bass.ds((NT - 2) * P - i * P, P), bass.ds((NT - 1) * P - i * P, 1)
                dve.wait_ge(ev.sem, ev.at(i, "slots", 0, before=1))
                dve.tensor_scalar(mask[:], bc[:, tile], bc[:, following], None, ALU.is_equal).then_inc(ev.sem, 1)
                dve.wait_ge(ev.sem, ev.at(i, "mask", 0))
                dve.scalar_tensor_tensor(out=diff[:], in0=YT[:, tile], scalar=YT[:, following], in1=mask[:],
                                         op0=ALU.subtract, op1=ALU.mult).then_inc(ev.sem, 1)
                dve.wait_ge(ev.sem, ev.at(i, "diff", 0))
                dve.tensor_tensor(YT[:, tile], YT[:, tile], diff[:], ALU.subtract).then_inc(ev.sem, 1)


def stream_schedule(runs, chunks, chunk0):
    total = runs * PASSES
    assert chunks + len(STAGES) - 1 <= total
    active = ["".join(s for lag, s in enumerate("ABCDE") if lag <= p < chunks + lag) for p in range(total)]
    return [(chunk0 + r * PASSES, active[r * PASSES:(r + 1) * PASSES]) for r in range(runs)]


def gnn_kernel(nc, a):
    with ExitStack() as ctx:
        sb = lambda name, shape, dt: ctx.enter_context(nc.sbuf_tensor(name, shape, dt))
        dram = lambda name, shape, dt=F32: nc.dram_tensor(name, shape, dt, kind="Internal").ap()
        w = load_weights(nc, a, sb, None, None)
        isolated_rows(nc, a, w, "all", 7, 1)
        pairs = dram("pairs", (NE + 2, 2), I32)
        dst_flat = dram("dst_flat", (NE,))
        mean = dram("mean", (P, NE))
        with ExitStack() as early:
            c = constants(nc, lambda name, shape, dt: early.enter_context(nc.sbuf_tensor("s" + name, shape, dt)), 0)
            sort_edges(nc, a, w, c, pairs)
        g = edge_table_tiles(sb)
        with ExitStack() as early:
            c = constants(nc, lambda name, shape, dt: early.enter_context(nc.sbuf_tensor(name, shape, dt)), 1)
            edge_tables(nc, a, w, c, pairs, g, dst_flat, mean)
        taps = [dram(f"tap{k}", (NE, HG if k in (4, 5, 6) else D)) for k in range(10)]
        isolated_rows(nc, a, w, "src", 5, NCH // 5, taps, g["src"])
        shared = {"YT": sb("YT", [P, NE], F32), "mean": mean, "stream": stream_tiles(sb)}
        xd = dram("xd", (NE, D))
        T = [dram(f"table{k}", (NE, HG if k in (4, 5, 6) else D)) for k in range(8)]
        H = [dram(f"hop_table{k}", (NE, D)) for k in range(2)]
        plans = iter(stream_schedule(19, 91, 7))
        step = lambda kind, **kw: slot_pass(nc, a, w, g, kind, shared, next(plans), **kw)
        step("start", out_table=T[0], xd=xd)
        for l in range(LAYERS - 1):
            step("layer", layer=l, table=T[l], ahead=taps[l], out_table=T[l + 1])
        step("layer3", layer=3, table=T[3], ahead=taps[3], out_table=T[4], xd=xd)
        step("gcn1", table=T[4], ahead=taps[4], out_table=T[5], rows_in=T[4])
        step("gcn2", table=T[5], ahead=taps[5], out_table=T[6], rows_in=T[5])
        step("gcn3", table=T[6], ahead=taps[6], out_table=T[7], xd=xd, rows_in=T[6])
        complete_slots(nc, shared["YT"], dst_flat)
        step("edge", table=T[7], ahead=taps[7], out_table=H[0], xd=xd, rows_in=T[7])
        for k in range(HOPS - 1):
            step("hop", layer=k, table=H[k % 2], ahead=taps[8 if k == 0 else 9], out_table=H[(k + 1) % 2])
        step("last_hop", table=H[(HOPS - 1) % 2], ahead=taps[9], xd=xd)
        write_rows(nc, a, g, shared["YT"])


_INS = ["x", "src", "dst", "L0_gnn_Ws_rel", "L0_gnn_bs_rel", "L0_gnn_Ws_root",
        "L1_gnn_W1", "L1_gnn_b1", "L1_gnn_W2", "L1_gnn_b2", "L1_gnn_W3", "L1_gnn_b3", "L1_gnn_Wlin", "L1_gnn_blin",
        "L2_gnn_Wm1", "L2_gnn_bm1", "L2_gnn_Wm2", "L2_gnn_bm2", "L2_gnn_Wm3", "L2_gnn_bm3",
        "L2_gnn_Wn1", "L2_gnn_bn1", "L2_gnn_Wn2", "L2_gnn_bn2"]


def kernel(**inputs):
    import numpy as _np
    import concourse.bacc as _bacc
    from concourse import mybir as _mybir
    from concourse.bass_utils import run_bass_kernel_spmd as _run

    nc = _bacc.Bacc("TRN2", target_bir_lowering=False, num_devices=1)
    arrays, aps = {}, {}
    for name in _INS:
        a = _np.ascontiguousarray(inputs[name])
        arrays[f"in_{name}"] = a
        aps[name] = nc.dram_tensor(f"in_{name}", a.shape, _mybir.dt.from_np(a.dtype), kind="ExternalInput").ap()
    aps["out"] = nc.dram_tensor("out_0", (50000, 128), _mybir.dt.float32, kind="ExternalOutput").ap()
    gnn_kernel(nc, aps)
    r = _run(nc, [arrays], core_ids=[0])
    return r.results[0]["out_0"]
```

```python
import numpy as np
import concourse.bass as bass
from concourse import mybir
from contextlib import ExitStack

F32 = mybir.dt.float32
I32 = mybir.dt.int32
U8 = mybir.dt.uint8
ALU = mybir.AluOpType
ACT = mybir.ActivationFunctionType

N = 50000
D = 128
E = 12500
HG = 32
LAYERS = 4
HOPS = 10
ALPHA = 0.1
EPS = 1e-5
P = 128
TPC = 4
CH = TPC * P
NCH = -(-E // CH)
NT = NCH * TPC
NE = NCH * CH
PAD = NE - E
FAR = 1 << 20
NODE_ROWS = -(-(N + 1) // P) * P


class Events:

    def __init__(self, sem, names, chunks, lead=0):
        self.sem, self.names, self.chunks, self.lead = sem, names, chunks, lead
        self.size = len(names) * chunks

    def at(self, i, name, u, before=0):
        return i * self.size + ((self.lead - before) * self.size + self.names.index(name) * self.chunks + u + 1)


def tiles(ap):
    return ap.rearrange("p (t f) -> p t f", t=TPC)


class Phase(ExitStack):

    def __init__(self, nc):
        super().__init__()
        self.nc, self.sems = nc, []
        self.callback(self.clear)

    def sem(self, name):
        self.sems.append(self.nc.alloc_semaphore(name))
        return self.sems[-1]

    def clear(self):
        self.nc.clear_and_free_semaphores(self.sems)
        self.nc.all_engine_barrier()


def load_weights(nc, a, sb, pb, sem):
    w = {}

    def tile(name, shape):
        w[name] = sb("w_" + name, shape, F32)
        return w[name]

    root, rel = tile("root", [P, LAYERS, D]), tile("rel", [P, LAYERS, D])
    b_rel = tile("b_rel", [P, LAYERS])
    w1, wlin = tile("w1", [P, HG]), tile("wlin", [HG, D])
    w3t = tile("w3t", [HG, TPC, HG])
    bd2, wc = tile("bd2", [P, P]), tile("wc", [P, TPC, D])
    b3 = tile("b3", [HG, 1])
    b1row, b2row, bm3row = tile("b1row", [P, HG]), tile("b2row", [P, HG]), tile("bm3row", [P, D])
    wm1, wm2, wm3 = tile("wm1", [P, 2, 256]), tile("wm2", [P, 2, 256]), tile("wm3", [P, 2, D])
    wn1, wn2 = tile("wn1", [P, 2, 256]), tile("wn2", [P, 2, D])
    bm1, bm2, bn1 = tile("bm1", [P, 2]), tile("bm2", [P, 2]), tile("bn1", [P, 2])
    raw = tile("raw", [P, 4])
    iso_b1, iso_b2, iso_bz = tile("iso_b1", [P, 1]), tile("iso_b2", [P, 1]), tile("iso_bz", [P, 1])
    dst_bz, bn2h = tile("dst_bz", [P, 1]), tile("bn2h", [P, 1])
    ones, ident = tile("ones", [P, 1]), tile("ident", [P, P])
    bz = tile("bz", [P, 1])
    power = tile("power", [P, CH // P * 2])
    with Phase(nc) as ctx:
        ps = ctx.enter_context(nc.psum_tensor("ps_setup", [P, 3, 512], F32))
        loaded, zeroed, made, folded, summed = (ctx.sem(s) for s in (
            "weights_loaded", "bd2_zeroed", "ident_made", "pe_folded", "dve_summed"))
        block = ctx.enter_context(nc.Block())
        column = lambda ap: ap.unsqueeze(1)
        plain = [
            (root[:], a["L0_gnn_Ws_root"].rearrange("l k m -> k l m")),
            (rel[:], a["L0_gnn_Ws_rel"].rearrange("l k m -> k l m")),
            (b_rel[:], a["L0_gnn_bs_rel"].rearrange("l m -> m l")),
            (w1[:], a["L1_gnn_W1"]), (wlin[:], a["L1_gnn_Wlin"]),
            (b3[:], column(a["L1_gnn_b3"])),
            (b1row[:], a["L1_gnn_b1"].partition_broadcast(P)), (b2row[:], a["L1_gnn_b2"].partition_broadcast(P)),
            (bm3row[:], a["L2_gnn_bm3"].partition_broadcast(P)),
            (wm1[:], a["L2_gnn_Wm1"].rearrange("(b k) m -> k b m", b=2)),
            (wm2[:], a["L2_gnn_Wm2"].rearrange("(b k) m -> k b m", b=2)),
            (wm3[:], a["L2_gnn_Wm3"].rearrange("(b k) m -> k b m", b=2)),
            (wn1[:], a["L2_gnn_Wn1"].rearrange("(b k) m -> k b m", b=2)),
            (wn2[:], a["L2_gnn_Wn2"].rearrange("(b k) m -> k b m", b=2)),
            (bm1[:], a["L2_gnn_bm1"].rearrange("(b k) -> k b", b=2)),
            (bm2[:], a["L2_gnn_bm2"].rearrange("(b k) -> k b", b=2)),
            (bn1[:], a["L2_gnn_bn1"].rearrange("(b k) -> k b", b=2)),
            (raw[:, 2:3], column(a["L1_gnn_blin"])), (raw[:, 3:4], column(a["L2_gnn_bn2"])),
        ]
        packed = []
        for t in range(TPC):
            rows = slice(t * HG, (t + 1) * HG)
            packed += [(raw[rows, 0:1], column(a["L1_gnn_b1"])), (raw[rows, 1:2], column(a["L1_gnn_b2"])),
                       (bd2[rows, rows], a["L1_gnn_W2"]),
                       (w3t[:, t, :], a["L1_gnn_W3"].rearrange("i k -> k i"))]

        @block.sync
        def _(sp):
            with nc.allow_non_contiguous_dma("small weights and biases, once"):
                for dst, src in plain:
                    sp.dma_start(dst, src).then_inc(loaded, 16)
                sp.wait_ge(zeroed, 1)
                for dst, src in packed:
                    sp.dma_start(dst, src).then_inc(loaded, 16)

        @block.gpsimd
        def _(pool):
            pool.memset(ident[:], 0.0).then_inc(made, 1)
            pool.wait_ge(made, 1)
            pool.affine_select(out=ident[:], in_=ident[:], compare_op=ALU.not_equal, fill=1.0, base=0,
                               pattern=[[-1, P]], channel_multiplier=1).then_inc(made, 1)

        @block.tensor
        def _(pe):
            pe.wait_ge(loaded, 16 * (len(plain) + len(packed)))
            pe.wait_ge(summed, 1)
            pe.matmul(ps[:, 0, 0:D], w3t[:].rearrange("k t i -> k (t i)"), wlin[:], start=True, stop=True)
            pe.matmul(ps[:, 1, 0:1], bd2[:], ones[:], start=True, stop=True)
            pe.matmul(ps[:, 2, 0:1], wlin[:], b3[:], start=True, stop=True).then_inc(folded, 1)
            pe.wait_ge(summed, 2)
            pe.matmul(ps[:, 0, 0:1], wc[:, 0, :], ones[:], start=True, stop=True).then_inc(folded, 1)

        @block.vector
        def _(dve):
            dve.memset(bd2[:], 0.0).then_inc(zeroed, 1)
            dve.memset(power[:], -0.5)
            dve.memset(wc[:], 0.0)
            dve.memset(ones[:], 1.0).then_inc(summed, 1)
            dve.wait_ge(loaded, 16 * (len(plain) + len(packed)))
            dve.tensor_scalar(iso_b1[:], raw[:, 0:1], 0.5, None, ALU.mult)
            dve.tensor_scalar(iso_b2[:], raw[:, 1:2], 0.5, None, ALU.mult)
            dve.tensor_scalar(bn2h[:], raw[:, 3:4], 0.5, None, ALU.add)
            dve.wait_ge(folded, 1)
            dve.tensor_copy(bz[:], ps[:, 2, 0:1])
            dve.wait_ge(summed, 1)
            for t in range(TPC):
                g = slice(t * HG, (t + 1) * HG)
                ins = dve.tensor_copy(wc[g, t, :], ps[g, 0, 0:D])
            ins.then_inc(summed, 1)
            dve.wait_ge(summed, 2)
            dve.scalar_tensor_tensor(out=iso_b2[:], in0=ps[:, 1, 0:1], scalar=0.25, in1=iso_b2[:],
                                     op0=ALU.mult, op1=ALU.add)
            dve.tensor_tensor(bz[:], bz[:], raw[:, 2:3], ALU.add).then_inc(summed, 1)
            dve.wait_ge(summed, 3)
            dve.tensor_scalar(dst_bz[:], bz[:], 0.5, None, ALU.mult).then_inc(summed, 1)
            dve.wait_ge(folded, 2)
            dve.wait_ge(summed, 4)
            dve.scalar_tensor_tensor(out=iso_bz[:], in0=ps[:, 0, 0:1], scalar=0.25, in1=dst_bz[:],
                                     op0=ALU.mult, op1=ALU.add)
    return w


def isolated_rows(nc, a, w, name, chunks, passes, taps=None, slots=None):
    U = chunks
    whole = taps is None
    PE_ = (["t0"] + [f"l{l}" for l in range(LAYERS)] + ["tx1", "t1", "g1", "g2", "g3", "tx2", "t2", "na", "nb", "up"]
           + ["tx3"])
    if not whole:
        PE_ = ["t0", "l0", "p1", "l1", "p2", "l2", "p3", "l3", "tx1", "t1", "g1", "pg", "ps1", "g2", "ps2", "g3",
               "tx2", "t2", "na", "nb", "up", "tx3"]
    ACT_ = ["h0", "e0", "e1", "e2", "e3", "h1", "s1", "s2", "tT", "h2", "na", "nb", "uT"]
    if not whole:
        ACT_ = ["h0", "e0", "e1", "e2", "e3", "h1", "pg", "s1", "s2", "tT", "h2", "na", "nb", "uT"]
    ln = [[f"st{k}", f"ag{k}", f"ve{k}", f"xn{k}"] for k in range(4)]
    elu = [[f"m{l}", f"h{l}"] for l in range(LAYERS)]
    if whole:
        DVE_ = ln[0] + sum(elu, []) + ["x1"] + ln[1] + ["x2"] + ln[2] + ["x3a", "x3"] + ln[3] + ["r", "o"]
    else:
        DVE_ = (ln[0] + ["q0"] + elu[0] + ["q1"] + elu[1] + ["q2"] + elu[2] + ["q3"] + elu[3] + ["x1"] + ln[1]
                + ["q4", "s1", "q5", "s2", "q6", "x2"] + ln[2] + ["q7", "x3a", "x3"] + ln[3] + ["q8", "q9"])
    with Phase(nc) as ctx:
        sb = lambda n, shape: [ctx.enter_context(nc.sbuf_tensor(f"{name}_{n}{u}", shape, F32)) for u in range(U)]
        sem = lambda n: ctx.sem(f"{name}_{n}")
        xin, xw, xn, ex, em, hT, out = (sb(n, [P, CH]) for n in ("xin", "xw", "xn", "ex", "em", "hT", "out"))
        sT, sU, nT = sb("sT", [P, P]), sb("sU", [P, P]), sb("nT", [P, 2, CH])
        st, mv, ve, rs = sb("st", [P, TPC, 6]), sb("mv", [P, TPC, 2]), sb("ve", [P, TPC]), sb("rs", [P, TPC])
        ps = [ctx.enter_context(nc.psum_tensor(f"{name}_ps{u}", [P, CH], F32)) for u in range(U)]
        x_in = [sem(f"x_in{u}") for u in range(U)]
        x_used = [sem(f"x_used{u}") for u in range(U)]
        stored = [sem(f"stored{u}") for u in range(U)]
        pe_ev = Events(sem("pe_done"), PE_, U)
        act_ev = Events(sem("act_done"), ACT_, U)
        dve_ev = Events(sem("dve_done"), DVE_, U)
        pool_ev = Events(sem("pool_done"), [f"rs{k}" for k in range(4)], U)
        held = sem("held")
        NTAP = 10
        if not whole:
            tap = [sb(f"tap{k}", [P, CH]) for k in range(2)]
            idx = [ctx.enter_context(nc.sbuf_tensor(f"{name}_idx{u}", [P, TPC], I32)) for u in range(U)]
            idx_in = sem("idx_in")
            tap_stored = [[sem(f"tap{k}_stored{u}") for u in range(U)] for k in range(2)]
        block = ctx.enter_context(nc.Block())
        last = passes - 1

        def wait(eng, ev, i, what, u):
            eng.wait_ge(ev.sem, ev.at(i, what, u))

        def loop(eng, body):
            if last:
                with eng.Fori(0, last) as i:
                    body(i)
            body(last)

        def row0(i, u):
            if isinstance(i, int) and whole:
                return min((i * U + u) * CH, N - CH)
            return i * (U * CH) + u * CH

        def dram(t, i, u):
            r0 = row0(i, u)
            rows = t[bass.ds(r0, CH), :] if not isinstance(r0, int) else t[r0:r0 + CH, :]
            return rows.rearrange("(p t) f -> p (t f)", t=TPC)

        @block.sync
        def _(sp):
            def body(i):
                if whole:
                    for u in range(U):
                        sp.wait_ge(x_used[u], i + 1)
                        sp.dma_start(xin[u][:], dram(a["x"], i, u)).then_inc(x_in[u], 16)
                    for u in range(U):
                        wait(sp, dve_ev, i, "o", u)
                        if isinstance(i, int) and u == U - 1:
                            sp.wait_ge(stored[u - 1], 16 * (i + 2))
                        sp.dma_start(dram(a["out"], i, u), out[u][:]).then_inc(stored[u], 16)
                else:
                    for k in range(NTAP):
                        for u in range(U):
                            wait(sp, dve_ev, i, f"q{k}", u)
                            wide = taps[k].shape[1] == D
                            src = tap[k % 2][u][:] if wide else tap[k % 2][u][:, 0:P]
                            sp.dma_start(dram(taps[k], i, u), src).then_inc(tap_stored[k % 2][u], 16)
            for u in range(U):
                sp.sem_inc(stored[u], 16)
                if not whole:
                    for k in range(2):
                        sp.sem_inc(tap_stored[k][u], 16)
            loop(sp, body)
            for u in range(U):
                if whole:
                    sp.wait_ge(stored[u], 16 * passes + 16)
                else:
                    for k in range(2):
                        sp.wait_ge(tap_stored[k][u], 16 * passes * NTAP // 2 + 16)

        @block.gpsimd
        def _(pool):
            if not whole:
                def fetch(i):
                    for u in range(U):
                        pool.wait_ge(x_used[u], i + 1)
                        c0 = i * (U * TPC) + u * TPC
                        pool.tensor_copy(idx[u][:], slots[:, bass.ds(c0, TPC)]).then_inc(idx_in, 1)
                        pool.wait_ge(idx_in, i * U + (u + 1))
                        pool.sem_inc(held, 1)
                        for t in range(TPC):
                            pool.indirect_dma_start(
                                xin[u][:, t * D:(t + 1) * D], None, a["x"],
                                bass.IndirectOffsetOnAxis(idx[u][:, t:t + 1], 0),
                                bounds_check=bound, oob_is_err=False).then_inc(x_in[u], 16)

            bound = pool.to_reg(N - 1)

            def body(i):
                for k in range(4):
                    if k == 2 and not whole and i is not last:
                        fetch(i + 1)
                    for u in range(U):
                        wait(pool, dve_ev, i, f"ve{k}", u)
                        pool.tensor_tensor(rs[u][:], ve[u][:], w["power"][:, 0:TPC], ALU.pow).then_inc(pool_ev.sem, 1)
            if not whole:
                fetch(0)
            loop(pool, body)

        @block.tensor
        def _(pe):
            def done(ins):
                ins.then_inc(pe_ev.sem, 1)

            def to_features(i, u, k):
                wait(pe, dve_ev, i, f"xn{k}", u)
                for t in range(TPC):
                    c = slice(t * P, (t + 1) * P)
                    ins = pe.transpose(ps[u][:, c], xn[u][:, c], w["ident"][:])
                done(ins)

            def back(src, u):
                for t in range(TPC):
                    c = slice(t * P, (t + 1) * P)
                    ins = pe.transpose(ps[u][:, c], src[:, c], w["ident"][:])
                done(ins)

            def body(i):
                us = range(U)
                for u in us:
                    to_features(i, u, 0)
                for l in range(LAYERS):
                    for u in us:
                        if l == 0:
                            wait(pe, act_ev, i, "h0", u)
                        else:
                            wait(pe, dve_ev, i, f"h{l - 1}", u)
                            if not whole:
                                wait(pe, dve_ev, i, f"q{l}", u)
                        done(pe.matmul(ps[u][:], w["root"][:, l, :], hT[u][:], start=True, stop=True))
                    if not whole and l < LAYERS - 1:
                        for u in us:
                            wait(pe, dve_ev, i, f"h{l}", u)
                            back(hT[u], u)
                for u in us:
                    wait(pe, dve_ev, i, f"h{LAYERS - 1}", u)
                    back(hT[u], u)
                for u in us:
                    to_features(i, u, 1)
                for u in us:
                    wait(pe, act_ev, i, "h1", u)
                    for t in range(TPC):
                        ins = pe.matmul(ps[u][t * HG:(t + 1) * HG, 0:P], w["w1"][:], hT[u][:, t * P:(t + 1) * P],
                                        start=True, stop=True)
                    done(ins)
                if not whole:
                    for u in us:
                        wait(pe, act_ev, i, "s1", u)
                        done(pe.transpose(ps[u][:, P:2 * P], sU[u][:], w["ident"][:]))
                    for u in us:
                        wait(pe, dve_ev, i, "q4", u)
                        wait(pe, dve_ev, i, "s1", u)
                        done(pe.transpose(ps[u][:, 0:P], sU[u][:], w["ident"][:]))
                for u in us:
                    if whole:
                        wait(pe, act_ev, i, "s1", u)
                    else:
                        wait(pe, dve_ev, i, "q5", u)
                    done(pe.matmul(ps[u][:, 0:P], w["bd2"][:], sT[u][:], start=True, stop=True))
                if not whole:
                    for u in us:
                        wait(pe, dve_ev, i, "s2", u)
                        done(pe.transpose(ps[u][:, 0:P], xn[u][:, 0:P], w["ident"][:]))
                for u in us:
                    if whole:
                        wait(pe, act_ev, i, "s2", u)
                    else:
                        wait(pe, dve_ev, i, "q6", u)
                    for t in range(TPC):
                        ins = pe.matmul(ps[u][:, t * P:(t + 1) * P], w["wc"][:, t, :], sU[u][:], start=True, stop=True)
                    done(ins)
                for u in us:
                    wait(pe, act_ev, i, "tT", u)
                    back(ex[u], u)
                for u in us:
                    to_features(i, u, 2)
                for b, what in ((0, "na"), (1, "nb")):
                    for u in us:
                        wait(pe, act_ev, i, "h2" if b == 0 else "na", u)
                        done(pe.matmul(ps[u][:], w["wn1"][:, 0, b * P:(b + 1) * P], hT[u][:], start=True, stop=True))
                for u in us:
                    wait(pe, act_ev, i, "nb", u)
                    for b in range(2):
                        ins = pe.matmul(ps[u][:], w["wn2"][:, b, :], nT[u][:, b, :], start=b == 0, stop=b == 1)
                    done(ins)
                for u in us:
                    wait(pe, act_ev, i, "uT", u)
                    back(em[u], u)
            loop(pe, body)

        @block.scalar
        def _(act):
            def step(i, u, what, out_ap, func, producer, **kw):
                wait(act, pe_ev, i, producer, u)
                act.activation(out_ap, ps[u][:, 0:out_ap.shape[1]], func, **kw).then_inc(act_ev.sem, 1)

            def body(i):
                us = range(U)
                for u in us:
                    step(i, u, "h0", hT[u][:], ACT.Relu, "t0")
                for l in range(LAYERS):
                    for u in us:
                        step(i, u, f"e{l}", ex[u][:], ACT.Exp, f"l{l}", bias=w["b_rel"][:, l:l + 1])
                for u in us:
                    step(i, u, "h1", hT[u][:], ACT.Relu, "t1")
                if not whole:
                    for u in us:
                        step(i, u, "pg", sU[u][:], ACT.Identity, "g1")
                for u in us:
                    step(i, u, "s1", sT[u][:], ACT.Tanh, "g1", bias=w["iso_b1"][:], scale=0.5)
                for u in us:
                    if not whole:
                        wait(act, pe_ev, i, "ps1", u)
                    step(i, u, "s2", sU[u][:], ACT.Tanh, "g2", bias=w["iso_b2"][:], scale=0.25)
                for u in us:
                    step(i, u, "tT", ex[u][:], ACT.Tanh, "g3", bias=w["iso_bz"][:], scale=0.25)
                for u in us:
                    step(i, u, "h2", hT[u][:], ACT.Relu, "t2")
                for b, what in ((0, "na"), (1, "nb")):
                    for u in us:
                        step(i, u, what, nT[u][:, b, :], ACT.Relu, what, bias=w["bn1"][:, b:b + 1])
                for u in us:
                    step(i, u, "uT", em[u][:], ACT.Identity, "up", bias=w["bn2h"][:])
            loop(act, body)

        @block.vector
        def _(dve):
            def done(ins):
                ins.then_inc(dve_ev.sem, 1)

            def layernorm(i, k, x, before, used=None):
                us = range(U)
                for u in us:
                    if before == "x_in":
                        dve.wait_ge(x_in[u], (16 if whole else 64) * (i + 1))
                    else:
                        wait(dve, dve_ev, i, before, u)
                    for t in range(TPC):
                        ins = dve.bn_stats(st[u][:, t, :], x[u][:, t * D:(t + 1) * D])
                        if used is not None and t == 0:
                            ins.then_inc(used[u], 1)
                    done(ins)
                wait(dve, dve_ev, i, f"st{k}", U - 1)
                dve.sem_inc(held, 1)
                for u in us:
                    for t in range(TPC):
                        ins = dve.bn_aggr(mv[u][:, t, :], st[u][:, t, :])
                    done(ins)
                for u in us:
                    wait(dve, dve_ev, i, f"ag{k}", u)
                    done(dve.tensor_scalar(ve[u][:], mv[u][:, :, 1], EPS, None, ALU.add))
                for u in us:
                    wait(dve, pool_ev, i, f"rs{k}", u)
                    for t in range(TPC):
                        c = slice(t * D, (t + 1) * D)
                        ins = dve.tensor_scalar(xn[u][:, c], x[u][:, c], mv[u][:, t, 0:1], rs[u][:, t:t + 1],
                                                ALU.subtract, ALU.mult)
                    done(ins)

            def to_tap(i, k, make):
                for u in range(U):
                    dve.wait_ge(tap_stored[k % 2][u], i * (16 * NTAP // 2) + 16 * (k // 2 + 1))
                    done(make(u, tap[k % 2][u]))

            def body(i):
                us = range(U)
                layernorm(i, 0, xin, "x_in")
                if not whole:
                    def make0(u, to):
                        wait(dve, dve_ev, i, "xn0", u)
                        return dve.tensor_scalar(to[:], xn[u][:], 0.0, None, ALU.max)
                    to_tap(i, 0, make0)
                for l in range(LAYERS):
                    for u in us:
                        wait(dve, act_ev, i, f"e{l}", u)
                        done(dve.tensor_scalar(em[u][:], ex[u][:], 1.0, -1.0, ALU.min, ALU.add))
                    for u in us:
                        wait(dve, dve_ev, i, f"m{l}", u)
                        done(dve.scalar_tensor_tensor(out=hT[u][:], in0=ps[u][:], scalar=w["b_rel"][:, l:l + 1],
                                                      in1=em[u][:], op0=ALU.add, op1=ALU.max))
                    if not whole and l < LAYERS - 1:
                        def make(u, to, l=l):
                            wait(dve, pe_ev, i, f"p{l + 1}", u)
                            return dve.tensor_copy(to[:], ps[u][:])
                        to_tap(i, l + 1, make)
                for u in us:
                    wait(dve, pe_ev, i, "tx1", u)
                    done(dve.tensor_tensor(xw[u][:], ps[u][:], xin[u][:], ALU.add))
                layernorm(i, 1, xw, "x1", x_used)
                if not whole:
                    def make4(u, to):
                        wait(dve, pe_ev, i, "pg", u)
                        return dve.tensor_copy(to[:, 0:P], ps[u][:, P:2 * P])
                    to_tap(i, 4, make4)
                    for u in us:
                        wait(dve, act_ev, i, "s1", u)
                        done(dve.tensor_scalar(sU[u][:], sT[u][:], 0.5, 0.5, ALU.mult, ALU.add))

                    def make5(u, to):
                        wait(dve, pe_ev, i, "ps1", u)
                        return dve.tensor_copy(to[:, 0:P], ps[u][:, 0:P])
                    to_tap(i, 5, make5)
                    for u in us:
                        wait(dve, act_ev, i, "s2", u)
                        done(dve.tensor_scalar(xn[u][:, 0:P], sU[u][:], 0.5, 0.5, ALU.mult, ALU.add))

                    def make6(u, to):
                        wait(dve, pe_ev, i, "ps2", u)
                        return dve.tensor_copy(to[:, 0:P], ps[u][:, 0:P])
                    to_tap(i, 6, make6)
                for u in us:
                    wait(dve, pe_ev, i, "tx2", u)
                    done(dve.scalar_tensor_tensor(out=xw[u][:], in0=ps[u][:], scalar=0.5, in1=xw[u][:],
                                                  op0=ALU.mult, op1=ALU.add))
                layernorm(i, 2, xw, "x2")
                if not whole:
                    def make7(u, to):
                        wait(dve, dve_ev, i, "xn2", u)
                        return dve.tensor_scalar(to[:], xn[u][:], 0.0, None, ALU.max)
                    to_tap(i, 7, make7)
                for u in us:
                    wait(dve, pe_ev, i, "tx3", u)
                    done(dve.scalar_tensor_tensor(out=ex[u][:], in0=xn[u][:], scalar=0.0, in1=ps[u][:],
                                                  op0=ALU.max, op1=ALU.add))
                for u in us:
                    wait(dve, dve_ev, i, "x3a", u)
                    done(dve.tensor_tensor(xw[u][:], xw[u][:], ex[u][:], ALU.add))
                layernorm(i, 3, xw, "x3")
                if whole:
                    for u in us:
                        wait(dve, dve_ev, i, "xn3", u)
                        done(dve.tensor_scalar(ex[u][:], xn[u][:], 0.0, ALPHA, ALU.max, ALU.mult))
                    for u in us:
                        wait(dve, dve_ev, i, "r", u)
                        dve.wait_ge(stored[u], 16 * i + 16)
                        done(dve.tensor_tensor(out[u][:], xw[u][:], ex[u][:], ALU.add))
                else:
                    def make8(u, to):
                        wait(dve, dve_ev, i, "xn3", u)
                        return dve.tensor_scalar(to[:], xn[u][:], 0.0, None, ALU.max)
                    to_tap(i, 8, make8)

                    def make9(u, to):
                        return dve.tensor_scalar(to[:], xn[u][:], 0.0, ALPHA, ALU.max, ALU.mult)
                    to_tap(i, 9, make9)
            for u in range(U):
                dve.sem_inc(x_used[u], 1)
            loop(dve, body)


def constants(nc, sb, n):
    c = {}
    HI = NODE_ROWS // P
    c["row_i"] = sb("c_row_i", [P, HI], I32)
    c["row"] = sb("c_row", [P, HI], F32)
    c["part_i"] = sb("c_part_i", [P, 1], I32)
    c["part"] = sb("c_part", [P, 1], F32)
    c["below"] = sb("c_below", [P, P], F32)
    c["above"] = sb("c_above", [P, P], F32)
    c["slot1"] = sb("c_slot1", [P, NT], I32)
    c["pos1"] = sb("c_pos1", [P, P], F32)
    c["pos1_i"] = sb("c_pos1_i", [P, P], I32)
    with Phase(nc) as ctx:
        counted = ctx.sem(f"iota_written{n}")
        cast = ctx.sem(f"iota_cast{n}")
        block = ctx.enter_context(nc.Block())

        @block.gpsimd
        def _(pool):
            pool.iota(c["row_i"][:], [[1, HI]], base=0, channel_multiplier=0)
            pool.iota(c["part_i"][:], [[1, 1]], base=0, channel_multiplier=1)
            pool.iota(c["slot1"][:], [[CH, NCH], [1, TPC]], base=1, channel_multiplier=TPC)
            pool.iota(c["pos1_i"][:], [[1, P]], base=1, channel_multiplier=P).then_inc(counted, 1)

        @block.vector
        def _(dve):
            dve.wait_ge(counted, 1)
            dve.tensor_copy(c["pos1"][:], c["pos1_i"][:])
            dve.tensor_copy(c["row"][:], c["row_i"][:])
            dve.tensor_copy(c["part"][:], c["part_i"][:]).then_inc(cast, 1)
            dve.wait_ge(cast, 1)
            dve.tensor_scalar(c["below"][:], c["row"][:, 0:P], c["part"][:], None, ALU.is_lt)
            dve.tensor_scalar(c["above"][:], c["row"][:, 0:P], c["part"][:], None, ALU.is_gt)
    return c


def sort_edges(nc, a, w, c, pairs):
    BF = mybir.dt.bfloat16
    HI = NODE_ROWS // P
    FULL, REST = E // P, E % P
    U = TPC
    with Phase(nc) as ctx:
        sb = lambda n, shape, dt=F32: ctx.enter_context(nc.sbuf_tensor("sort_" + n, shape, dt))
        sem = lambda n: ctx.sem("sort_" + n)
        dst_r, src_r, lo_r = sb("dst_r", [NT, P], I32), sb("src_r", [NT, P], I32), sb("lo_r", [NT, P], I32)
        rows_f = sb("rows_f", [NT, 3, P])
        cols = sb("cols", [P, 3, NT])
        dst_c, src_c, hi_c = (sb(n, [P, NT], I32) for n in ("dst_c", "src_c", "hi_c"))
        hi_f = sb("hi_f", [P, NT])
        guard = sb("guard", [1, 4], I32)
        dst_b, lo_b = sb("dst_b", [P, NE]), sb("lo_b", [P, NE])
        zero = sb("zero", [P, P], BF)
        count, total, upto, start = (sb(n, [P, HI]) for n in ("count", "total", "upto", "start"))
        ones = sb("ones", [P, P])
        ring = lambda n, width, dt=F32: [sb(f"{n}{u}", [P, width], dt) for u in range(U)]
        hot_lo, hot_hi, lo_t, table = ring("hot_lo", P, BF), ring("hot_hi", HI, BF), ring("lo_t", P), ring("table", HI)
        same, looked, rank, base = ring("same", P), ring("looked", HI), ring("rank", 1), ring("base", 1)
        to, pair = ring("to", 1, I32), ring("pair", 2, I32)
        ps_t = [ctx.enter_context(nc.psum_tensor(f"sort_ps_t{k}", [P, 512], F32)) for k in range(3)]
        ps_c = ctx.enter_context(nc.psum_tensor("sort_ps_c", [P, 512], F32))
        ps_l = [ctx.enter_context(nc.psum_tensor(f"sort_ps_l{u}", [P, 512], F32)) for u in range(U)]
        flat = nc.dram_tensor("sort_flat", (2, NE), F32, kind="Internal").ap()
        padded, loaded, link = sem("padded"), sem("loaded"), sem("dve_link")
        rows_made, turned, counted, tot_made = (sem(n) for n in ("rows_made", "turned", "counted", "totals_made"))
        flat_out, guard_out, b_in, started = sem("flat_out"), sem("guard_out"), sem("broadcasts_in"), sem("started")
        hot = Events(sem("hot_made"), ["hot"], U)
        hot_used = [sem(f"hot_used{u}") for u in range(U)]
        copied, looked_up = sem("table_copied"), sem("looked_up")
        walk = Events(sem("dve_walk"), ["hot", "same", "rank", "base", "pair", "place"], U)
        scattered = [sem(f"scattered{u}") for u in range(U)]
        held = sem("pool_held")
        block = ctx.enter_context(nc.Block())

        @block.sync
        def _(sp):
            sp.wait_ge(padded, 1)
            for to_sb, of in ((dst_r, a["dst"]), (src_r, a["src"])):
                sp.dma_start(to_sb[0:FULL, :], of[0:FULL * P].rearrange("(r e) -> r e", e=P)).then_inc(loaded, 16)
                sp.dma_start(to_sb[FULL:FULL + 1, 0:REST], of[FULL * P:E].unsqueeze(0)).then_inc(loaded, 16)
            sp.dma_start(pairs[0:1, :], guard[:, 0:2]).then_inc(guard_out, 16)
            sp.dma_start(pairs[NE + 1:NE + 2, :], guard[:, 2:4]).then_inc(guard_out, 16)
            sp.wait_ge(rows_made, 1)
            for k in range(2):
                sp.dma_start(flat[k, :].rearrange("(r e) -> r e", e=P), rows_f[:, k, :]).then_inc(flat_out, 16)
            sp.wait_ge(flat_out, 32)
            for k, to_sb in ((0, dst_b), (1, lo_b)):
                sp.dma_start(to_sb[:], flat[k, :].partition_broadcast(P)).then_inc(b_in, 16)
            sp.wait_ge(guard_out, 32)

        @block.gpsimd
        def _(pool):
            bound = pool.to_reg(NE)
            with pool.Fori(0, NCH) as i:
                for u in range(U):
                    pool.wait_ge(walk.sem, walk.at(i, "place", u))
                    pool.sem_inc(held, 1)
                    pool.indirect_dma_start(pairs, bass.IndirectOffsetOnAxis(to[u][:], 0), pair[u][:], None,
                                            bounds_check=bound, oob_is_err=False).then_inc(scattered[u], 16)
            for u in range(U):
                pool.wait_ge(scattered[u], 16 * NCH)

        @block.tensor
        def _(pe):
            for u in range(U):
                pe.sem_inc(hot_used[u], 1)
            pe.wait_ge(rows_made, 1)
            for k in range(3):
                ins = pe.transpose(ps_t[k][:, 0:NT], rows_f[:, k, :], w["ident"][0:NT, 0:NT])
            ins.then_inc(turned, 1)
            pe.wait_ge(hot.sem, hot.at(0, "hot", 0))
            pe.matmul(ps_c[:, 0:HI], zero[:], hot_hi[0][:], start=True, stop=True, skip_group_check=True)
            with pe.Fori(0, NCH) as i:
                for u in range(U):
                    pe.wait_ge(hot.sem, hot.at(i, "hot", u))
                    pe.matmul(ps_c[:, 0:HI], hot_lo[u][:], hot_hi[u][:], start=False, stop=True,
                              skip_group_check=True).then_inc(hot_used[u], 1)
            pe.wait_ge(tot_made, 1)
            pe.matmul(ps_l[0][:, 0:HI], ones[:], count[:], start=True, stop=True)
            pe.matmul(ps_l[1][:, 0:HI], c["above"][:], count[:], start=True, stop=True).then_inc(counted, 1)
            pe.wait_ge(started, 1)
            pe.matmul(ps_c[:, 0:HI], w["ident"][:], start[:], start=True, stop=True,
                      skip_group_check=True).then_inc(looked_up, 1)
            with pe.Fori(0, NCH) as i:
                for u in range(U):
                    pe.wait_ge(walk.sem, walk.at(i, "hot", u))
                    pe.wait_ge(copied, i * U + (u + 1))
                    pe.matmul(ps_l[u][:, 0:HI], lo_t[u][:], table[u][:], start=True, stop=True)
                    pe.matmul(ps_c[:, 0:HI], hot_lo[u][:], hot_hi[u][:], start=False, stop=True,
                              skip_group_check=True).then_inc(looked_up, 1)

        @block.scalar
        def _(act):
            with act.Fori(0, NCH) as i:
                for u in range(U):
                    act.wait_ge(looked_up, i * U + (u + 1))
                    act.activation(table[u][:], ps_c[:, 0:HI], ACT.Identity).then_inc(copied, 1)

        @block.vector
        def _(dve):
            n = [0]

            def linked(ins):
                n[0] += 1
                ins.then_inc(link, 1)
                dve.wait_ge(link, n[0])

            def hot_rows(i, u, t):
                dve.tensor_scalar(hot_lo[u][:], c["row"][:, 0:P], cols[:, 1, bass.ds(t, 1)], None, ALU.is_equal)
                return dve.tensor_scalar(hot_hi[u][:], c["row"][:], hi_f[:, bass.ds(t, 1)], None, ALU.is_equal)

            dve.memset(guard[:, 0:2], -1)
            dve.memset(guard[:, 2:4], -2)
            dve.memset(src_r[:], 0)
            dve.memset(ones[:], 1.0)
            dve.memset(zero[:], 0.0)
            dve.memset(dst_r[:], N).then_inc(padded, 1)
            dve.wait_ge(loaded, 64)
            dve.tensor_copy(rows_f[:, 0, :], dst_r[:])
            dve.tensor_copy(rows_f[:, 2, :], src_r[:])
            linked(dve.tensor_scalar(lo_r[:], dst_r[:], P - 1, None, ALU.bitwise_and))
            dve.tensor_copy(rows_f[:, 1, :], lo_r[:]).then_inc(rows_made, 1)
            dve.wait_ge(turned, 1)
            for k in range(3):
                ins = dve.tensor_copy(cols[:, k, :], ps_t[k][:, 0:NT])
            linked(ins)
            dve.tensor_copy(src_c[:], cols[:, 2, :])
            linked(dve.tensor_copy(dst_c[:], cols[:, 0, :]))
            linked(dve.tensor_scalar(hi_c[:], dst_c[:], 7, None, ALU.arith_shift_right))
            linked(dve.tensor_copy(hi_f[:], hi_c[:]))
            with dve.Fori(0, NCH) as i:
                for u in range(U):
                    dve.wait_ge(hot_used[u], i + 1)
                    hot_rows(i, u, i * U + u).then_inc(hot.sem, 1)
            for u in range(U):
                dve.wait_ge(hot_used[u], NCH + 1)
            dve.tensor_copy(count[:], ps_c[:, 0:HI]).then_inc(tot_made, 1)
            dve.wait_ge(counted, 1)
            linked(dve.tensor_copy(total[:], ps_l[0][:, 0:HI]))
            linked(dve.tensor_tensor_scan(upto[:], total[:], total[:], 0.0, ALU.add, ALU.bypass))
            linked(dve.tensor_tensor(upto[:], upto[:], total[:], ALU.subtract))
            dve.tensor_tensor(start[:], upto[:], ps_l[1][:, 0:HI], ALU.add).then_inc(started, 1)
            dve.wait_ge(b_in, 32)
            def tile_walk(i):
                def mine(name, u):
                    dve.wait_ge(walk.sem, walk.at(i, name, u))

                def done(ins):
                    ins.then_inc(walk.sem, 1)

                for u in range(U):
                    e = bass.ds(i * CH + u * P, P)
                    dve.tensor_scalar(lo_t[u][:], lo_b[:, e], c["part"][:], None, ALU.is_equal)
                    done(hot_rows(i, u, i * U + u))
                for u in range(U):
                    e = bass.ds(i * CH + u * P, P)
                    done(dve.tensor_scalar(same[u][:], dst_b[:, e], cols[:, 0, bass.ds(i * U + u, 1)], None,
                                           ALU.is_equal))
                for u in range(U):
                    mine("same", u)
                    done(dve.tensor_tensor_reduce(out=same[u][:], in0=same[u][:], in1=c["below"][:], scale=1.0,
                                                  scalar=1.0, op0=ALU.mult, op1=ALU.add, accum_out=rank[u][:]))
                for u in range(U):
                    dve.wait_ge(looked_up, i * U + (u + 2))
                    done(dve.tensor_tensor_reduce(out=looked[u][:], in0=ps_l[u][:, 0:HI], in1=hot_hi[u][:], scale=1.0,
                                                  scalar=0.0, op0=ALU.mult, op1=ALU.add, accum_out=base[u][:]))
                for u in range(U):
                    if not isinstance(i, int):
                        dve.wait_ge(scattered[u], i * 16)
                    dve.tensor_copy(pair[u][:, 0:1], dst_c[:, bass.ds(i * U + u, 1)])
                    done(dve.tensor_copy(pair[u][:, 1:2], src_c[:, bass.ds(i * U + u, 1)]))
                for u in range(U):
                    mine("base", u)
                    done(dve.tensor_tensor(to[u][:], base[u][:], rank[u][:], ALU.add))

            tile_walk(0)
            with dve.Fori(1, NCH) as i:
                tile_walk(i)


def edge_tables(nc, a, w, c, pairs, g, flat, mean_out):
    with Phase(nc) as ctx:
        t_ = lambda n, shape, dt=F32: ctx.enter_context(nc.sbuf_tensor("idx_" + n, shape, dt))
        sem = lambda n: ctx.sem("idx_" + n)
        near = [t_(f"near{k}", [NT, P, 2], I32) for k in range(3)]
        d = [t_(f"d{k}", [NT, P]) for k in range(3)]
        first, last, f_idx, l_idx, far = (t_(n, [NT, P]) for n in ("first", "lastr", "f_idx", "l_idx", "far"))
        out_r = t_("out_r", [NT, 5, P])
        cols = t_("cols", [P, 5, NT])
        row_f, row_l, carry_f, carry_l = (t_(n, [1, P + 1]) for n in ("row_f", "row_l", "carry_f", "carry_l"))
        back_f, back_l = t_("back_f", [NT, 1]), t_("back_l", [NT, 1])
        deg1, tmp = t_("deg1", [P, NT]), t_("tmp", [P, NT])
        half = t_("half", [P, NT])
        zero = t_("zero", [P, NODE_ROWS // P], I32)
        found = t_("found", [P, NT], I32)
        found_f = t_("found_f", [P, NT])
        bc = t_("bc", [P, NE])
        mean = t_("mean", [P, NE])
        ps = [ctx.enter_context(nc.psum_tensor(f"idx_ps{k}", [P, 512], F32)) for k in range(6)]
        node_row = nc.dram_tensor("node_row", (NODE_ROWS, 1), I32, kind="Internal").ap()
        loaded, link, made, turned, flat_out, b_in, zeroed, zero_out = (sem(n) for n in (
            "loaded", "dve_link", "made", "turned", "flat_out", "b_in", "zeroed", "zero_out"))
        scattered, fetched, powers, cols_made = sem("scattered"), sem("fetched"), sem("powers"), sem("cols_made")
        mean_made, mean_stored = sem("mean_made"), sem("mean_stored")
        block = ctx.enter_context(nc.Block())

        @block.sync
        def _(sp):
            for k in range(3):
                sp.dma_start(near[k][:].rearrange("r e k -> r (e k)"),
                             pairs[k:k + NE, :].rearrange("(r e) k -> r (e k)", e=P)).then_inc(loaded, 16)
            sp.wait_ge(zeroed, 1)
            sp.dma_start(node_row.rearrange("(p f) o -> p (f o)", p=P), zero[:]).then_inc(zero_out, 16)
            sp.wait_ge(made, 1)
            sp.dma_start(flat.rearrange("(r e) -> r e", e=P), d[1][:]).then_inc(flat_out, 16)
            sp.wait_ge(flat_out, 16)
            sp.dma_start(bc[:], flat.partition_broadcast(P)).then_inc(b_in, 16)
            sp.wait_ge(mean_made, 1)
            sp.dma_start(mean_out, mean[:]).then_inc(mean_stored, 16)
            sp.wait_ge(mean_stored, 16)

        @block.gpsimd
        def _(pool):
            pool.wait_ge(cols_made, 1)
            pool.tensor_tensor(g["norm"][:], cols[:, 2, :], half[:], ALU.pow).then_inc(powers, 1)
            pool.wait_ge(cols_made, 2)
            pool.tensor_tensor(g["dinv"][:], deg1[:], half[:], ALU.pow).then_inc(powers, 1)
            pool.wait_ge(zero_out, 16)
            pool.wait_ge(cols_made, 3)
            for t in range(NT):
                pool.indirect_dma_start(node_row, bass.IndirectOffsetOnAxis(g["last"][:, t:t + 1], 0),
                                        c["slot1"][:, t:t + 1], None, bounds_check=NODE_ROWS - 1,
                                        oob_is_err=False).then_inc(scattered, 16)
            pool.wait_ge(scattered, 16 * NT)
            for t in range(NT):
                pool.indirect_dma_start(found[:, t:t + 1], None, node_row,
                                        bass.IndirectOffsetOnAxis(g["src"][:, t:t + 1], 0),
                                        bounds_check=N - 1, oob_is_err=False).then_inc(fetched, 16)

        @block.tensor
        def _(pe):
            pe.wait_ge(made, 2)
            pe.transpose(ps[0][0:1, 0:NT], f_idx[:, P - 1:P], w["ident"][0:NT, 0:NT])
            pe.transpose(ps[1][0:1, 0:NT], l_idx[:, 0:1], w["ident"][0:NT, 0:NT]).then_inc(turned, 1)
            pe.wait_ge(made, 3)
            pe.transpose(ps[2][0:NT, 0:1], carry_f[:, 0:NT], w["ident"][0:1, 0:1])
            pe.transpose(ps[3][0:NT, 0:1], carry_l[:, 1:NT + 1], w["ident"][0:1, 0:1]).then_inc(turned, 1)
            pe.wait_ge(made, 4)
            for k in range(5):
                ins = pe.transpose(ps[(4, 5, 0, 1, 4)[k]][:, (0, 0, 0, 0, 128)[k]:(0, 0, 0, 0, 128)[k] + NT],
                                   out_r[:, k, :], w["ident"][0:NT, 0:NT])
            ins.then_inc(turned, 1)

        @block.vector
        def _(dve):
            n = [0]

            def linked(ins):
                n[0] += 1
                ins.then_inc(link, 1)
                dve.wait_ge(link, n[0])

            BIG = float(4 * NE)
            dve.memset(half[:], -0.5)
            dve.memset(far[:], float(FAR))
            dve.memset(carry_f[:], 0.0)
            dve.memset(carry_l[:], BIG)
            dve.memset(g["cont"][:, 0:P], 0)
            dve.memset(zero[:], 0).then_inc(zeroed, 1)
            dve.wait_ge(loaded, 48)
            dve.tensor_copy(d[0][:], near[0][:, :, 0])
            dve.tensor_copy(d[2][:], near[2][:, :, 0])
            dve.tensor_copy(out_r[:, 1, :], near[1][:, :, 1])
            dve.tensor_copy(d[1][:], near[1][:, :, 0]).then_inc(made, 1)
            dve.wait_ge(made, 1)
            dve.tensor_tensor(first[:], d[1][:], d[0][:], ALU.not_equal)
            linked(dve.tensor_tensor(last[:], d[1][:], d[2][:], ALU.not_equal))
            dve.tensor_tensor(f_idx[:], first[:], c["pos1"][0:NT, :], ALU.mult)
            linked(dve.tensor_tensor(l_idx[:], last[:], c["pos1"][0:NT, :], ALU.mult))
            linked(dve.tensor_scalar(far[:], last[:], -BIG, BIG, ALU.mult, ALU.add))
            linked(dve.tensor_tensor(l_idx[:], l_idx[:], far[:], ALU.add))
            linked(dve.tensor_tensor_scan(f_idx[:], f_idx[:], f_idx[:], 0.0, ALU.max, ALU.max))
            dve.tensor_tensor_scan(l_idx[:, ::-1], l_idx[:, ::-1], l_idx[:, ::-1], BIG, ALU.min,
                                   ALU.min).then_inc(made, 1)
            dve.wait_ge(turned, 1)
            dve.tensor_copy(row_f[:, 0:NT], ps[0][0:1, 0:NT])
            linked(dve.tensor_copy(row_l[:, 0:NT], ps[1][0:1, 0:NT]))
            dve.tensor_tensor_scan(carry_f[:, 1:NT + 1], row_f[:, 0:NT], row_f[:, 0:NT], 0.0, ALU.max, ALU.max)
            dve.tensor_tensor_scan(carry_l[:, 0:NT][:, ::-1], row_l[:, 0:NT][:, ::-1], row_l[:, 0:NT][:, ::-1], BIG,
                                   ALU.min, ALU.min).then_inc(made, 1)
            dve.wait_ge(turned, 2)
            dve.tensor_copy(back_f[:], ps[2][0:NT, 0:1])
            linked(dve.tensor_copy(back_l[:], ps[3][0:NT, 0:1]))
            dve.tensor_scalar(f_idx[:], f_idx[:], back_f[:], None, ALU.max)
            linked(dve.tensor_scalar(l_idx[:], l_idx[:], back_l[:], None, ALU.min))
            linked(dve.tensor_tensor(out_r[:, 2, :], l_idx[:], f_idx[:], ALU.subtract))
            dve.tensor_scalar(out_r[:, 2, :], out_r[:, 2, :], 1.0, None, ALU.add)
            dve.tensor_copy(out_r[:, 0, :], d[1][:])
            dve.tensor_scalar(out_r[:, 4, :], d[1][:], float(N - 1), None, ALU.min)
            linked(dve.tensor_scalar(far[:], last[:], -float(FAR), float(FAR), ALU.mult, ALU.add))
            dve.tensor_tensor(out_r[:, 3, :], d[1][:], far[:], ALU.add).then_inc(made, 1)
            dve.wait_ge(turned, 3)
            for k in range(5):
                ins = dve.tensor_copy(cols[:, k, :], ps[(4, 5, 0, 1, 4)[k]][:, (0, 0, 0, 0, 128)[k]:(0, 0, 0, 0, 128)[k] + NT])
            ins.then_inc(cols_made, 1)
            dve.wait_ge(cols_made, 1)
            dve.tensor_scalar(deg1[:], cols[:, 2, :], 1.0, None, ALU.add).then_inc(cols_made, 1)
            dve.tensor_copy(g["src"][:], cols[:, 1, :])
            dve.tensor_copy(g["dst"][:], cols[:, 4, :])
            dve.tensor_copy(g["last"][:], cols[:, 3, :]).then_inc(cols_made, 1)
            linked(dve.reciprocal(g["inv_deg"][:], cols[:, 2, :]))
            dve.wait_ge(powers, 2)
            dve.tensor_tensor(g["root_deg"][:], cols[:, 2, :], g["norm"][:], ALU.mult)
            dve.tensor_tensor(g["f1"][:], cols[:, 2, :], g["dinv"][:], ALU.mult)
            dve.wait_ge(b_in, 16)
            for t in range(NT):
                e = slice(t * P, (t + 1) * P)
                dve.tensor_scalar(mean[:, e], bc[:, e], cols[:, 0, t:t + 1], g["inv_deg"][:, t:t + 1],
                                  ALU.is_equal, ALU.mult)
                if t:
                    dve.tensor_scalar(g["cont"][:, e], bc[:, e], bc[:, t * P - 1:t * P], None, ALU.is_equal)
            dve.memset(half[:, 0:1], 0.0).then_inc(mean_made, 1)
            dve.wait_ge(fetched, 16 * NT)
            linked(dve.tensor_copy(found_f[:], found[:]))
            linked(dve.tensor_scalar(tmp[:], found_f[:], 0.0, float(FAR), ALU.is_equal, ALU.mult))
            linked(dve.tensor_tensor(tmp[:], tmp[:], found_f[:], ALU.add))
            linked(dve.tensor_scalar(tmp[:], tmp[:], -1.0, None, ALU.add))
            linked(dve.tensor_copy(g["row"][:], tmp[:]))


def edge_table_tiles(sb):
    g = {}
    for name in ("inv_deg", "norm", "root_deg", "dinv", "f1"):
        g[name] = sb("g_" + name, [P, NT], F32)
    for name in ("src", "dst", "last", "row"):
        g[name] = sb("g_" + name, [P, NT], I32)
    g["cont"] = sb("g_cont", [P, NE], U8)
    return g


STAGES = {
    "A": ["A_load", "A_st", "A_ag", "A_ve", "A_rs", "A_nm", "A_xn", "A_t", "A_h", "A_l0", "A_e0", "A_m0", "A_h0",
          "A_l1", "A_e1", "A_m1", "A_h1"],
    "B": ["B_load", "B_l2", "B_e2", "B_m2", "B_h2", "B_l3", "B_e3", "B_m3", "B_h3", "B_tx", "B_x"],
    "C": ["C_st", "C_ag", "C_ve", "C_rs", "C_nm", "C_xn", "C_t", "C_h", "C_g1", "C_s1", "C_g2", "C_s2", "C_g3", "C_s3",
          "C_tx", "C_x"],
    "D": ["D_st", "D_ag", "D_ve", "D_rs", "D_nm", "D_xn", "D_t", "D_h", "D_na", "D_ra", "D_nb", "D_rb", "D_up", "D_u",
          "D_tx", "D_xa", "D_x"],
    "E": ["E_st", "E_ag", "E_ve", "E_rs", "E_nm", "E_xn", "E_o", "E_store"],
}


class Track:

    def __init__(self, sem, names, first=0):
        self.sem, self.names, self.first = sem, names, first

    def begin(self, eng):
        if self.names:
            eng.sem_inc(self.sem, len(self.names))

    def at(self, i, name, before=0):
        n = len(self.names)
        return (i - self.first) * n + ((1 - before) * n + self.names.index(name) + 1)


def stream_tiles(sb):
    wide = lambda n: sb("all_" + n, [P, CH], F32)
    b = {n: wide(n) for n in ("A_x", "A_xn", "A_m", "A_out", "B_x", "B_ex", "B_m", "B_h", "B_out", "C_xn",
                              "C_h", "C_out", "D_xn", "D_h", "D_out", "E_xn", "E_o")}
    b["A_h"] = b["A_x"]
    b["D_n"] = sb("all_D_n", [P, 2, CH], F32)
    b["C_s"], b["C_u"] = sb("all_C_s", [P, P], F32), sb("all_C_u", [P, P], F32)
    for s in "ACDE":
        b[s + "_st"], b[s + "_mv"] = sb(f"all_{s}_st", [P, TPC, 6], F32), sb(f"all_{s}_mv", [P, TPC, 2], F32)
        for n in ("_ve", "_rs", "_nm"):
            b[s + n] = sb(f"all_{s}{n}", [P, TPC], F32)
    return b


STREAM_PE = {"A": ["A_t", "A_l0", "A_l1"], "B": ["B_l2", "B_l3", "B_tx"],
             "C": ["C_t", "C_g1", "C_g2", "C_g3", "C_tx"], "D": ["D_t", "D_na", "D_nb", "D_up", "D_tx"], "E": []}
STREAM_ACT = {"A": ["A_xn", "A_h", "A_e0", "A_e1"], "B": ["B_e2", "B_e3"], "C": ["C_xn", "C_h", "C_s1", "C_s2", "C_s3"],
              "D": ["D_xn", "D_h", "D_ra", "D_rb", "D_u"], "E": ["E_xn"]}
STREAM_DVE = {"A": ["A_st", "A_ag", "A_ve", "A_nm", "A_m0", "A_h0", "A_m1", "A_h1"],
              "B": ["B_m2", "B_h2", "B_m3", "B_h3", "B_x"],
              "C": ["C_st", "C_ag", "C_ve", "C_nm", "C_x"],
              "D": ["D_st", "D_ag", "D_ve", "D_nm", "D_xa", "D_x"],
              "E": ["E_st", "E_ag", "E_ve", "E_nm", "E_o"]}
STREAM_POOL = {s: [f"{s}_rs"] if s in "ACDE" else [] for s in "ABCDE"}


class Stream:

    def __init__(self, nc, ctx, name, b, w, a, chunk0, first, ps):
        self.b, self.w, self.a, self.chunk0, self.ps = b, w, a, chunk0, ps
        self.first = first
        names = {"pe": STREAM_PE, "act": STREAM_ACT, "dve": STREAM_DVE, "pool": STREAM_POOL}
        self.tracks = {e: {s: Track(ctx.sem(f"{name}_all_{e}_{s}"), n[s], first[s]) for s in "ABCDE" if n[s]}
                       for e, n in names.items()}
        self.x_in = {s: ctx.sem(f"{name}_all_{s}_x_in") for s in "AB"}
        self.stored = ctx.sem(f"{name}_all_stored")
        self.held = ctx.sem(f"{name}_all_held")

    def begin(self, e, eng):
        for t in self.tracks[e].values():
            t.begin(eng)

    def wait(self, eng, e, what, i, before=0):
        t = self.tracks[e][what[0]]
        eng.wait_ge(t.sem, t.at(i, what, before))

    def mark(self, e, what, ins):
        ins.then_inc(self.tracks[e][what[0]].sem, 1)

    def rows(self, t, i, lag):
        chunk = self.chunk0 - lag + i
        r0 = min(chunk * CH, N - CH) if isinstance(i, int) else i * CH + (self.chunk0 - lag) * CH
        at = slice(r0, r0 + CH) if isinstance(r0, int) else bass.ds(r0, CH)
        return t[at, :].rearrange("(p t) f -> p (t f)", t=TPC)


def stream_sync(sp, s):
    b = s.b

    def load(stage, lag, freed):
        def step(i, active):
            s.wait(sp, *freed, i, before=1)
            sp.sem_inc(s.held, 1)
            sp.dma_start(b[stage + "_x"][:], s.rows(s.a["x"], i, lag)).then_inc(s.x_in[stage], 16)
        return step

    def store(i, active):
        s.wait(sp, "dve", "E_o", i)
        sp.sem_inc(s.held, 1)
        sp.dma_start(s.rows(s.a["out"], i, 4), b["E_o"][:]).then_inc(s.stored, 16)

    return {"A_load": load("A", 0, ("pe", "A_l1")), "B_load": load("B", 1, ("dve", "B_x")), "E_store": store}


def stream_gpsimd(pool, s):
    def root(stage):
        def step(i, active):
            s.wait(pool, "dve", stage + "_ve", i)
            s.mark("pool", stage + "_rs", pool.tensor_tensor(s.b[stage + "_rs"][:], s.b[stage + "_ve"][:],
                                                             s.w["power"][:, 0:TPC], ALU.pow))
        return step
    return {f"{k}_rs": root(k) for k in "ACDE"}


def stream_tensor(pe, s):
    b, w = s.b, s.w
    steps = {}

    def turn(what, src, waits):
        def step(i, active):
            for e, v in waits:
                s.wait(pe, e, v, i)
            if what in ("A_t", "C_t", "D_t"):
                s.wait(pe, "dve", {"A": "A_h1", "C": "C_x", "D": "D_xa"}[what[0]], i, before=1)
            for t in range(TPC):
                e = slice(t * P, (t + 1) * P)
                ins = pe.transpose(s.ps[what[0]][:, e], src[:, e], w["ident"][:])
            s.mark("pe", what, ins)
        steps[what] = step

    def product(what, lhsT, rhs, waits, n=CH):
        def step(i, active):
            for e, v, before in waits:
                s.wait(pe, e, v, i, before)
            for k, (l, r) in enumerate(zip(lhsT, rhs)):
                ins = pe.matmul(s.ps[what[0]][:, 0:n], l, r, start=k == 0, stop=k == len(lhsT) - 1)
            s.mark("pe", what, ins)
        steps[what] = step

    root = lambda l: [w["root"][:, l, :]]
    turn("A_t", b["A_xn"], [("act", "A_xn")])
    product("A_l0", root(0), [b["A_h"][:]], [("act", "A_h", 0)])
    product("A_l1", root(1), [b["A_h"][:]], [("dve", "A_h0", 0)])
    product("B_l2", root(2), [b["A_out"][:]], [("dve", "A_h1", 1), ("dve", "B_x", 1)])
    product("B_l3", root(3), [b["B_h"][:]], [("dve", "B_h2", 0)])
    turn("B_tx", b["B_h"], [("dve", "B_h3")])
    turn("C_t", b["C_xn"], [("act", "C_xn")])

    def g1(i, active):
        s.wait(pe, "act", "C_h", i)
        for t in range(TPC):
            ins = pe.matmul(s.ps["C"][t * HG:(t + 1) * HG, 0:P], w["w1"][:], b["C_h"][:, t * P:(t + 1) * P],
                            start=True, stop=True)
        s.mark("pe", "C_g1", ins)

    def g3(i, active):
        s.wait(pe, "act", "C_s2", i)
        for t in range(TPC):
            ins = pe.matmul(s.ps["C"][:, t * P:(t + 1) * P], w["wc"][:, t, :], b["C_u"][:], start=True, stop=True)
        s.mark("pe", "C_g3", ins)

    steps["C_g1"], steps["C_g3"] = g1, g3
    product("C_g2", [w["bd2"][:]], [b["C_s"][:]], [("act", "C_s1", 0)], P)
    turn("C_tx", b["C_h"], [("act", "C_s3")])
    turn("D_t", b["D_xn"], [("act", "D_xn")])
    product("D_na", [w["wn1"][:, 0, 0:P]], [b["D_h"][:]], [("act", "D_h", 0)])
    product("D_nb", [w["wn1"][:, 0, P:2 * P]], [b["D_h"][:]], [("act", "D_ra", 0)])
    product("D_up", [w["wn2"][:, k, :] for k in range(2)], [b["D_n"][:, k, :] for k in range(2)], [("act", "D_rb", 0)])
    turn("D_tx", b["D_h"], [("act", "D_u")])
    return steps


def stream_scalar(act, s):
    b, w = s.b, s.w
    steps = {}

    def step(what, to, func, producer, n=CH, freed=None, **kw):
        def run(i, active):
            s.wait(act, "pe", producer, i)
            if freed:
                s.wait(act, *freed, i, before=1)
            s.mark("act", what, act.activation(to, s.ps[what[0]][:, 0:n], func, **kw))
        steps[what] = run

    def normalise(stage, x, last_use=None):
        def run(i, active):
            s.wait(act, "dve", stage + "_nm", i)
            if last_use:
                s.wait(act, *last_use, i, before=1)
            for t in range(TPC):
                e = slice(t * D, (t + 1) * D)
                ins = act.activation(b[stage + "_xn"][:, e], x[:, e], ACT.Relu, bias=b[stage + "_nm"][:, t:t + 1],
                                     scale=b[stage + "_rs"][:, t:t + 1])
            s.mark("act", stage + "_xn", ins)
        steps[stage + "_xn"] = run

    normalise("A", b["A_x"], ("dve", "A_m1"))
    normalise("C", b["B_out"], ("pe", "C_t"))
    normalise("D", b["C_out"], ("dve", "D_xa"))
    normalise("E", b["D_out"], ("dve", "E_o"))
    step("A_h", b["A_h"][:], ACT.Relu, "A_t")
    for st, l in (("A", 0), ("A", 1), ("B", 2), ("B", 3)):
        step(f"{st}_e{l}", b["A_xn" if st == "A" else "B_ex"][:], ACT.Exp, f"{st}_l{l}", bias=w["b_rel"][:, l:l + 1])
    step("C_h", b["C_h"][:], ACT.Relu, "C_t")
    step("C_s1", b["C_s"][:], ACT.Tanh, "C_g1", P, bias=w["iso_b1"][:], scale=0.5)
    step("C_s2", b["C_u"][:], ACT.Tanh, "C_g2", P, bias=w["iso_b2"][:], scale=0.25)
    step("C_s3", b["C_h"][:], ACT.Tanh, "C_g3", bias=w["iso_bz"][:], scale=0.25)
    step("D_h", b["D_h"][:], ACT.Relu, "D_t")
    step("D_ra", b["D_n"][:, 0, :], ACT.Relu, "D_na", freed=("dve", "D_x"), bias=w["bn1"][:, 0:1])
    step("D_rb", b["D_n"][:, 1, :], ACT.Relu, "D_nb", bias=w["bn1"][:, 1:2])
    step("D_u", b["D_h"][:], ACT.Identity, "D_up", bias=w["bn2h"][:])
    return steps


def stream_vector(dve, s):
    b, w = s.b, s.w
    steps = {}

    def norm(stage, x, made, turned=None):
        st, mv, ve, rs = (b[stage + n] for n in ("_st", "_mv", "_ve", "_rs"))

        def stats(i, active):
            made(i)
            for t in range(TPC):
                ins = dve.bn_stats(st[:, t, :], x[:, t * D:(t + 1) * D])
            s.mark("dve", stage + "_st", ins)

        def aggregate(i, active):
            s.wait(dve, "dve", stage + "_st", i)
            dve.sem_inc(s.held, 1)
            for t in range(TPC):
                ins = dve.bn_aggr(mv[:, t, :], st[:, t, :])
            s.mark("dve", stage + "_ag", ins)

        def add_eps(i, active):
            s.wait(dve, "dve", stage + "_ag", i)
            s.wait(dve, "act", stage + "_xn", i, before=1)
            s.mark("dve", stage + "_ve", dve.tensor_scalar(ve[:], mv[:, :, 1], EPS, None, ALU.add))

        def shift(i, active):
            s.wait(dve, "pool", stage + "_rs", i)
            s.mark("dve", stage + "_nm", dve.scalar_tensor_tensor(
                out=b[stage + "_nm"][:], in0=mv[:, :, 0], scalar=-1.0, in1=rs[:], op0=ALU.mult, op1=ALU.mult))

        steps[stage + "_st"], steps[stage + "_ag"] = stats, aggregate
        steps[stage + "_ve"], steps[stage + "_nm"] = add_eps, shift

    def simple(what, waits, op, after=None):
        def step(i, active):
            for e, v, before in waits:
                s.wait(dve, e, v, i, before)
            if after and after[1][0] in active:
                s.wait(dve, *after, i)
            s.mark("dve", what, op())
        steps[what] = step

    def elu(stage, l, ex, m, to, after=None):
        simple(f"{stage}_m{l}", [("act", f"{stage}_e{l}", 0)],
               lambda: dve.tensor_scalar(m[:], ex[:], 1.0, -1.0, ALU.min, ALU.add))
        simple(f"{stage}_h{l}", [("dve", f"{stage}_m{l}", 0)],
               lambda: dve.scalar_tensor_tensor(out=to[:], in0=s.ps[stage][:], scalar=w["b_rel"][:, l:l + 1], in1=m[:],
                                                op0=ALU.add, op1=ALU.max), after)

    norm("A", b["A_x"], lambda i: dve.wait_ge(s.x_in["A"], (i - s.first["A"]) * 16 + 16))
    elu("A", 0, b["A_xn"], b["A_m"], b["A_h"])
    elu("A", 1, b["A_xn"], b["A_m"], b["A_out"], ("pe", "B_l2"))
    elu("B", 2, b["B_ex"], b["B_m"], b["B_h"])
    elu("B", 3, b["B_ex"], b["B_m"], b["B_h"])

    def x1(i, active):
        s.wait(dve, "pe", "B_tx", i)
        dve.wait_ge(s.x_in["B"], (i - s.first["B"]) * 16 + 16)
        if "C" in active:
            s.wait(dve, "dve", "C_x", i)
        s.mark("dve", "B_x", dve.tensor_tensor(b["B_out"][:], s.ps["B"][:], b["B_x"][:], ALU.add))

    steps["B_x"] = x1
    norm("C", b["B_out"], lambda i: s.wait(dve, "dve", "B_x", i, before=1))
    simple("C_x", [("pe", "C_tx", 0)],
           lambda: dve.scalar_tensor_tensor(out=b["C_out"][:], in0=s.ps["C"][:], scalar=0.5, in1=b["B_out"][:],
                                            op0=ALU.mult, op1=ALU.add), ("dve", "D_x"))
    norm("D", b["C_out"], lambda i: s.wait(dve, "dve", "C_x", i, before=1))
    simple("D_xa", [("pe", "D_tx", 0)],
           lambda: dve.tensor_tensor(b["D_n"][:, 0, :], b["D_xn"][:], s.ps["D"][:], ALU.add))
    simple("D_x", [("dve", "D_xa", 0)],
           lambda: dve.tensor_tensor(b["D_out"][:], b["C_out"][:], b["D_n"][:, 0, :], ALU.add), ("dve", "E_o"))
    norm("E", b["D_out"], lambda i: s.wait(dve, "dve", "D_x", i, before=1))

    def out(i, active):
        s.wait(dve, "act", "E_xn", i)
        dve.wait_ge(s.stored, (i - s.first["E"]) * 16 + 16)
        s.mark("dve", "E_o", dve.scalar_tensor_tensor(out=b["E_o"][:], in0=b["E_xn"][:], scalar=ALPHA,
                                                      in1=b["D_out"][:], op0=ALU.mult, op1=ALU.add))

    steps["E_o"] = out
    return steps


U = 5
PASSES = NCH // U
GROUPS = ((0, 1, 2), (3, 4))
LN = ["st", "ag", "ve", "rs", "nm", "xn"]
SLOT_STEPS = {
    "start": LN + ["t", "hh"],
    "layer": ["agg", "sc", "ca", "l", "e", "m", "h", "tx", "y", "row"],
    "layer3": ["agg", "sc", "ca", "l", "e", "m", "h", "tx", "x"] + LN + ["t", "hh", "g", "row"],
    "gcn1": ["agg", "sc", "ca", "b", "tr", "a", "u", "ub", "s", "sg", "row"],
    "gcn2": ["agg", "sc", "ca", "b", "tr", "a", "u", "tu", "uT", "z", "ub", "s", "sg", "row"],
    "gcn3": ["agg", "sc", "ca", "b", "tr", "a", "u", "tu", "uT", "z", "tT", "tx", "x"] + LN + ["t", "hh"],
    "edge": ["tv", "vT", "ma", "qa", "mb", "qb", "mc", "qc", "md", "qd", "m3", "msg", "agg", "sc", "ca", "na", "ra",
             "nb", "rb", "up", "uT", "tx", "xa", "x"] + LN + ["row", "c"],
    "hop": ["agg", "sc", "ca", "tx", "row"],
    "last_hop": ["agg", "sc", "ca", "tx", "row", "o"],
}
SLOT_ENGINE = {
    "pe": {"agg", "l", "tx", "t", "g", "tr", "tu", "z", "tv", "ma", "mb", "mc", "md", "m3", "na", "nb", "up"},
    "act": {"xn", "e", "y", "hh", "s", "uT", "tT", "vT", "qa", "qb", "qc", "qd", "ra", "rb"},
    "pool": {"rs"},
}
LAST_READ = {"start": ("act", "hh"), "layer": ("dve", "row"), "layer3": ("dve", "row"), "gcn1": ("dve", "a"),
             "gcn2": ("dve", "ub"), "gcn3": ("act", "hh"), "edge": ("dve", "xa"), "hop": ("dve", "row"),
             "last_hop": ("dve", "row")}


BY_ENGINE = {"pe": 0.85, "act": 0.57, "dve": 0.6, "pool": 0.95, "sp": 0.05}
TAKES = {"st": 0.8, "ag": 0.3, "ve": 0.07, "nm": 0.07, "xn": 1.0, "m": 0.34, "m0": 0.34, "m1": 0.34, "m2": 0.34,
         "m3": 0.34, "h": 0.66, "h0": 0.66, "h1": 0.66, "h2": 0.66, "h3": 0.66, "sc": 0.13, "ca": 1.04, "up": 1.7,
         "l": 1.7, "ma": 1.7, "mb": 1.7, "mc": 1.7, "md": 1.7, "na": 1.7, "nb": 1.7, "s": 0.25, "s1": 0.25,
         "s2": 0.25, "sg": 0.2, "a": 0.2, "b": 0.2, "u": 0.2, "ub": 0.2, "tu": 0.25, "uT": 0.57, "c": 0.34}
TRIALS = 120
DMA_TAKES, SIGNAL_TAKES = 2.5, 0.35
STREAM_AFTER = {"A_h1": "B_l2", "B_x": "C_x", "C_x": "D_x", "D_x": "E_o"}
STREAM_AFTER_LAST = {"A_load": ["A_l1"], "B_load": ["B_x"], "B_l2": ["A_h1", "B_x"], "C_st": ["B_x"], "D_st": ["C_x"],
                     "E_st": ["D_x"], "A_t": ["A_h1"], "C_t": ["C_x"], "D_t": ["D_xa"], "D_ra": ["D_x"],
                     "A_xn": ["A_m1"], "E_xn": ["E_o"], "E_o": ["E_store"]}


def step_graph(kind, stages, first_pass, last_pass):
    g = {}

    def add(s, engine, takes, seen, after, after_last=()):
        g[s] = (engine, takes, seen, list(after), list(after_last))

    names = SLOT_STEPS[kind]
    engine_of = lambda n: next((e for e, m in SLOT_ENGINE.items() if n in m), "dve")
    first_pe = next(n for n in names if engine_of(n) == "pe")
    frees = "agg" if "agg" in names else "xn"
    last_read = LAST_READ[kind][1]
    for u in range(U):
        add(("load", u), "sp", 0.05, DMA_TAKES, [], [("store", u)])
        before = None
        for n in names:
            e = engine_of(n)
            after = [(before, u)] if before else []
            after_last = [(n, u)]
            if n in ("b", "x", "xa"):
                after += [("load", u)]
            if n == names[0] or n == "agg":
                after_last += [(f"gather{t}", u) for t in range(TPC)]
                if first_pass:
                    after.append((f"first{TPC - 1}", u))
            if n == "sc":
                (after if u else after_last).append(("sc", u - 1 if u else U - 1))
            if n == first_pe:
                after_last += [(last_read, u)] + ([(last_read, 4)] if u == 0 else [])
                after += [(last_read, 0)] if u == 4 else []
            add((n, u), e, TAKES.get(n, BY_ENGINE[e]) if n != "uT" or kind == "edge" else 0.25, SIGNAL_TAKES, after, after_last)
            before = n if n != "y" else before
        if first_pass:
            add(("first_ahead", u), "sp", 0.05, DMA_TAKES, [])
            for t in range(TPC):
                add((f"first{t}", u), "pool", 1.05, DMA_TAKES, [("first_ahead", u) if t == 0 else (f"first{t - 1}", u)])
        if not last_pass:
            add(("ahead", u), "sp", 0.05, DMA_TAKES, [(frees, u)])
            for t in range(TPC):
                add((f"gather{t}", u), "pool", 1.05, DMA_TAKES, [("ahead", u) if t == 0 else (f"gather{t - 1}", u)])
        add(("store", u), "sp", 0.05, DMA_TAKES, [(names[-1], u)])
    stream_engine = {n: e for e, by in (("pe", STREAM_PE), ("act", STREAM_ACT), ("pool", STREAM_POOL), ("dve", STREAM_DVE))
                     for m in by.values() for n in m}
    for st in stages:
        before = None
        for n in STAGES[st]:
            e = stream_engine.get(n, "sp")
            after = [(before, None)] if before and before != "B_load" else []
            if n == "B_x":
                after.append(("B_load", None))
            if n in STREAM_AFTER and STREAM_AFTER[n][0] in stages:
                after.append((STREAM_AFTER[n], None))
            takes = TAKES.get(n[2:], BY_ENGINE[e]) if e != "pe" or n == "D_up" else 0.25 if n == "C_g2" else 0.85
            add((n, None), e, takes, DMA_TAKES if e == "sp" else SIGNAL_TAKES, after,
                [(m, None) for m in STREAM_AFTER_LAST.get(n, [])])
            before = n
    return g


def merged(kind, stages, first_pass, last_pass, cache={}):
    key = (kind, stages, first_pass, last_pass)
    if key in cache:
        return cache[key]
    g = step_graph(*key)
    order_in = {s: k for k, s in enumerate(g)}
    users = {s: [] for s in g}
    for s, (_, _, _, after, _) in g.items():
        for d in after:
            users[d].append(s)
    way = {}

    def to_go(s):
        if s not in way:
            way[s] = g[s][1] + g[s][2] + max((to_go(d) for d in users[s]), default=0.0)
        return way[s]

    load = {}
    for s in g:
        to_go(s)
    for s in g:
        if last_pass and s[1] is not None:
            way[s] += 20.0
        if s[0][:-1] in ("gather", "first"):
            way[s] = U - s[1]
        load[g[s][0]] = load.get(g[s][0], 0.0) + g[s][1]
    busiest = max(load.values())

    def schedule(release):
        free, end, start = {e: 0.0 for e in load}, {}, {}
        left = {s: len(g[s][3]) for s in g}
        if first_pass:
            release = {**release, **{s: 10.0 for s in g if s[1] is None}}
        ready = {s: release.get(s, 0.0) for s in g if not left[s]}
        while ready:
            t, _, _, s = min((max(free[g[s][0]], r), -way[s], order_in[s], s) for s, r in ready.items())
            _, _, s = min((-way[x], order_in[x], x) for x, r in ready.items()
                          if g[x][0] == g[s][0] and max(free[g[x][0]], r) <= t + 0.05)
            t = max(free[g[s][0]], ready.pop(s))
            start[s], free[g[s][0]], end[s] = t, t + g[s][1], t + g[s][1] + g[s][2]
            for d in users[s]:
                left[d] -= 1
                if not left[d]:
                    ready[d] = max([release.get(d, 0.0)] + [end[x] for x in g[d][3]])
        return start, end

    def trial(order, passes):
        free, last, ends = {e: 0.0 for e in load}, {}, []
        for _ in range(passes):
            now = {}
            for s in order:
                e, takes, seen, after, after_last = g[s]
                t = max([free[e]] + [now[d] for d in after] + [last.get(d, 0.0) for d in after_last])
                free[e], now[s] = t + takes, t + takes + seen
            last = now
            ends.append(max(free.values()))
        return ends[-1] if passes < 4 else ends[-1] - ends[-4]

    single = first_pass or last_pass
    best, straight, rng = None, dict(way), np.random.default_rng(0)
    for k in range(TRIALS):
        period = busiest * (1.0, 1.05, 1.1, 1.2, 1.35, 1.5)[k % 6]
        release = {}
        spread = 0.0 if k < 6 else rng.choice([0.05, 0.1, 0.3])
        for s in g:
            way[s] = straight[s] * (1.0 + spread * rng.random())
        tried = dict(way)
        for _ in range(1 if first_pass else 3):
            start, end = schedule(release)
            order = sorted(g, key=lambda s: (start[s], order_in[s]))
            took = trial(order, 1 if single else 8)
            if best is None or took < best[0] - 1e-9:
                best, straight = (took, order), tried
            release = {s: max([0.0] + [end[d] - period for d in g[s][4] if d in end]) for s in g}
    cache[key] = best[1]
    return best[1]


def slot_pass(nc, a, w, g, kind, shared, stream_plan, table=None, ahead=None, out_table=None, xd=None,
              rows_in=None, layer=0, repeats=1):
    total = PASSES * repeats
    if repeats == 1:
        table, ahead, out_table = [table], [ahead], [out_table]
    gcn = kind in ("gcn1", "gcn2", "gcn3")
    width = HG if gcn else D
    row_width = TPC * HG if kind in ("gcn1", "gcn2") else CH
    YT = shared["YT"]
    has_x = kind in ("layer3", "gcn3", "edge", "last_hop")
    makes_x = kind in ("start", "layer3", "gcn3", "edge")
    has_agg = kind != "start"
    name = kind + str(layer)
    steps_ = SLOT_STEPS[kind]
    chunk0, active_in = stream_plan
    first = {s: next((i for i in range(total) if s in active_in[i]), 0) for s in "ABCDE"}
    rep = 0
    with Phase(nc) as ctx:
        def sb(n, shape, dt=F32):
            return [ctx.enter_context(nc.sbuf_tensor(f"{name}_{n}{u}", shape, dt)) for u in range(U)]
        sem = lambda n: ctx.sem(f"{name}_{n}")
        per_u = lambda n: [sem(f"{n}{u}") for u in range(U)]
        half_of = lambda tiles_, k: [t[:, k, :] for t in tiles_]
        wide = lambda n: sb(n, [P, CH])
        if kind == "start":
            xr, xn = wide("xr"), wide("xn")
            rows = xn
        elif kind in ("layer", "layer3"):
            V, aggT, em = wide("V"), wide("aggT"), wide("em")
            ex, hT, xn, rows = aggT, aggT, em, em
            if kind == "layer3":
                xr = wide("xr")
                rows = sb("rows", [P, P])
                row_width = P
        elif gcn:
            V, aggT, own, bA, bB, bU = sb("V", [P, P]), wide("aggT"), *(sb(n, [P, P]) for n in ("own", "bA", "bB", "bU"))
            if kind == "gcn3":
                xr, xn = wide("xr"), wide("xn")
                ex = rows = xn
            else:
                rows = sb("rows", [P, P])
        elif kind == "edge":
            mB, mA, hT, xr, hr = sb("mB", [P, 2, CH]), sb("mA", [P, 2, CH]), wide("hT"), wide("xr"), wide("hr")
            V, aggT = half_of(mB, 0), half_of(mB, 1)
            em, ex, xn, rows = half_of(mA, 0), half_of(mA, 1), hT, hr
        else:
            V, aggT, rows = wide("V"), wide("aggT"), wide("rows")
            if kind == "last_hop":
                xr = wide("xr")
        if has_agg:
            mean = wide("mean")
            carry = sb("carry", [P, TPC])
        st, mv = sb("st", [P, TPC, 6]), sb("mv", [P, TPC, 2])
        ve, rs, nm = (sb(n, [P, TPC]) for n in ("ve", "rs", "nm"))
        idx = sb("idx", [P, TPC], I32)
        banks = [ctx.enter_context(nc.psum_tensor(f"{name}_ps{k}", [P, CH], F32)) for k in range(4)]
        ps = [banks[u % 4] for u in range(U)]
        stream_ps = {s: ctx.enter_context(nc.psum_tensor(f"{name}_all_ps{s}", [P, CH], F32)) for s in "ABCD"}
        engine_of = lambda n: next((e for e, names in SLOT_ENGINE.items() if n in names), "dve")
        tracks = {e: [Track(s_, [n for n in steps_ if engine_of(n) == e]) for s_ in per_u(e + "_done")]
                  for e in ("pe", "act", "pool", "dve")}
        stream = Stream(nc, ctx, name, shared["stream"], w, a, chunk0, first, stream_ps)
        z_in, v_in, x_in, row_out, x_out = (per_u(n) for n in ("z_in", "v_in", "x_in", "row_out", "x_out"))
        idx_made = per_u("idx_made")
        held, link = sem("held"), sem("link")
        block = ctx.enter_context(nc.Block())

        def wait(eng, e, what, i, u, before=0):
            eng.wait_ge(tracks[e][u].sem, tracks[e][u].at(i, what, before))

        def mark(e, u, ins):
            ins.then_inc(tracks[e][u].sem, 1)

        def begin(e, eng):
            for t in tracks[e]:
                t.begin(eng)
            stream.begin(e, eng)

        def run(eng, steps, before=None):
            nonlocal rep

            def one_pass(i, active, first_pass, last_pass):
                for what, u in merged(kind, active, first_pass, last_pass):
                    if what in steps:
                        if u is None:
                            steps[what](i, active)
                        else:
                            steps[what](i, u)

            for rep in range(repeats):
                i, last = rep * PASSES, (rep + 1) * PASSES - 1
                one_pass(i, active_in[i], True, False)
                i += 1
                while i < last:
                    j = i + 1
                    while j < last and active_in[j] == active_in[i]:
                        j += 1
                    if j - i > 1:
                        with eng.Fori(i, j) as k:
                            one_pass(k, active_in[i], False, False)
                    else:
                        one_pass(i, active_in[i], False, False)
                    i = j
                one_pass(last, active_in[last], False, True)
            rep = 0

        def slot_pass_of(i):
            return i - rep * PASSES

        def chunk_rows(t, i, u):
            return t[bass.ds(slot_pass_of(i) * (U * CH) + u * CH, CH), :].rearrange("(p t) f -> p (t f)", t=TPC)

        def cols(i, u, t=0, n=CH):
            return bass.ds(slot_pass_of(i) * (U * CH) + (u * CH + t * P), n)

        def columns(i, u):
            return bass.ds(slot_pass_of(i) * (U * TPC) + u * TPC, TPC)

        def factors(name, i, u):
            return g[name][:, columns(i, u)].unsqueeze(2).to_broadcast([P, TPC, HG])

        def factor(name, i, u, t):
            return g[name][:, bass.ds(slot_pass_of(i) * (U * TPC) + (u * TPC + t), 1)]

        @block.sync
        def _(sp):
            def ahead_of(i, u):
                if not has_agg:
                    return
                wait(sp, "pe", "agg", i, u, before=1)
                sp.sem_inc(held, 1)
                sp.dma_start(mean[u][:], shared["mean"][:, cols(i, u)]).then_inc(z_in[u], 16)
                sp.dma_start(V[u][:, 0:TPC * width], chunk_rows(ahead[rep], i, u)).then_inc(z_in[u], 16)

            def load(i, u):
                if has_x:
                    if kind == "last_hop":
                        wait(sp, "dve", "o", i, u, before=1)
                    else:
                        sp.wait_ge(x_out[u], i * 16 + 16)
                    sp.sem_inc(held, 1)
                    sp.dma_start(xr[u][:], chunk_rows(xd, i, u)).then_inc(x_in[u], 16)
                if kind == "edge":
                    sp.wait_ge(row_out[u], i * 16 + 16)
                    sp.sem_inc(held, 1)
                    wait(sp, "dve", "c", i, u, before=1)
                    sp.sem_inc(held, 1)
                    sp.dma_start(hr[u][:], chunk_rows(rows_in, i, u)).then_inc(x_in[u], 16)
                if gcn:
                    wait(sp, "dve", "b", i, u, before=1)
                    sp.sem_inc(held, 1)
                    sp.dma_start(own[u][:], chunk_rows(rows_in, i, u)).then_inc(x_in[u], 16)

            def store(i, u):
                if makes_x:
                    wait(sp, "dve", "st" if kind == "start" else "x", i, u)
                    sp.sem_inc(held, 1)
                    sp.dma_start(chunk_rows(xd, i, u), xr[u][:]).then_inc(x_out[u], 16)
                if kind != "last_hop":
                    wait(sp, *(("dve", "row") if "row" in steps_ else ("act", "xn")), i, u)
                    sp.sem_inc(held, 1)
                    sp.dma_start(chunk_rows(out_table[rep], i, u), rows[u][:, 0:row_width]).then_inc(row_out[u], 16)

            for u in range(U):
                sp.sem_inc(x_out[u], 16)
                if kind != "last_hop":
                    sp.sem_inc(row_out[u], 16)
            sp.sem_inc(stream.stored, 16)
            run(sp, {"load": load, "store": store, "first_ahead": ahead_of, "ahead": lambda i, u: ahead_of(i + 1, u), **stream_sync(sp, stream)})
            for u in range(U):
                sp.wait_ge(x_out[u], 16 * total + 16 if makes_x else 16)
                if kind != "last_hop":
                    sp.wait_ge(row_out[u], 16 * total + 16)
            sp.wait_ge(stream.stored, 16 + 16 * sum("E" in x for x in active_in))

        @block.gpsimd
        def _(pool):
            bound = pool.to_reg((N if kind == "start" else NE) - 1)
            begin("pool", pool)

            def gather(i, u, t):
                if t == 0:
                    if kind == "start":
                        wait(pool, "dve", "st", i, u, before=1)
                    else:
                        wait(pool, "pe", "agg", i, u, before=1)
                    pool.tensor_copy(idx[u][:], g["dst" if kind == "start" else "row"][:, columns(i, u)]).then_inc(
                        idx_made[u], 1)
                    pool.wait_ge(idx_made[u], i + 1)
                    pool.sem_inc(held, 1)
                    if kind == "start":
                        pool.wait_ge(x_out[u], i * 16 + 16)
                        pool.sem_inc(held, 1)
                        wait(pool, "act", "xn", i, u, before=1)
                    else:
                        pool.wait_ge(z_in[u], i * 32 + 32)
                    pool.sem_inc(held, 1)
                to, sem_, of = (xr[u], x_in[u], a["x"]) if kind == "start" else (V[u], v_in[u], table[rep])
                pool.indirect_dma_start(to[:, t * width:(t + 1) * width], None, of,
                                        bass.IndirectOffsetOnAxis(idx[u][:, t:t + 1], 0),
                                        bounds_check=bound, oob_is_err=False).then_inc(sem_, 16)

            def root(i, u):
                wait(pool, "dve", "ve", i, u)
                mark("pool", u, pool.tensor_tensor(rs[u][:], ve[u][:], w["power"][:, 0:TPC], ALU.pow))

            def first_gather(i, u, t):
                if rep and u == t == 0:
                    for v in range(U):
                        pool.wait_ge(row_out[v], i * 16 + 16)
                gather(i, u, t)

            steps = {"first%d" % t: (lambda i, u, t=t: first_gather(i, u, t)) for t in range(TPC)}
            steps |= {"gather%d" % t: (lambda i, u, t=t: gather(i + 1, u, t)) for t in range(TPC)}
            run(pool, {**steps, "rs": root, **stream_gpsimd(pool, stream)})

        @block.tensor
        def _(pe):
            begin("pe", pe)
            first_pe = next(n for n in steps_ if engine_of(n) == "pe")

            def step(what, waits, op):
                def run_(i, u):
                    for e, v in waits:
                        if e == "v_in":
                            pe.wait_ge(v_in[u], i * 64 + 64)
                        elif e == "mean_in":
                            pe.wait_ge(z_in[u], i * 32 + 32)
                        else:
                            wait(pe, e, v, i, u)
                    if what == first_pe:
                        wait(pe, *LAST_READ[kind], i, u, before=1)
                        if u == 0:
                            wait(pe, *LAST_READ[kind], i, 4, before=1)
                        if u == 4:
                            wait(pe, *LAST_READ[kind], i, 0)
                    if what == "tr":
                        pe.sem_inc(held, 1)
                    mark("pe", u, op(i, u))
                return run_

            def turn(src):
                def op(i, u):
                    for t in range(TPC):
                        e = slice(t * P, (t + 1) * P)
                        ins = pe.transpose(ps[u][:, e], src[u][:, e], w["ident"][:])
                    return ins
                return op

            def average(i, u):
                for t in range(TPC):
                    e = slice(t * P, (t + 1) * P)
                    ins = pe.matmul(ps[u][0:width, e], V[u][:, t * width:(t + 1) * width], mean[u][:, e],
                                    start=True, stop=True)
                return ins

            def pair(w1, rhs1, w2):
                def op(i, u):
                    pe.matmul(ps[u][:], w1, rhs1[u][:], start=True, stop=False)
                    return pe.matmul(ps[u][:], w2, YT[:, cols(i, u)], start=False, stop=True)
                return op

            def halves(wt, src, c):
                def op(i, u):
                    for k in range(2):
                        ins = pe.matmul(ps[u][:], wt[:, k, c], src[u][:, k, :], start=k == 0, stop=k == 1)
                    return ins
                return op

            def turn_narrow(i, u):
                for t in range(TPC):
                    ins = pe.transpose(ps[u][:, t * HG:(t + 1) * HG], aggT[u][0:HG, t * P:(t + 1) * P],
                                       w["ident"][0:HG, 0:HG])
                return ins

            def z(i, u):
                if kind == "gcn2":
                    return pe.matmul(ps[u][:, 0:P], bA[u][:], w["bd2"][:], start=True, stop=True)
                for t in range(TPC):
                    ins = pe.matmul(ps[u][:, t * P:(t + 1) * P], w["wc"][:, t, :], bA[u][:], start=True, stop=True)
                return ins

            def first_gcn(i, u):
                for t in range(TPC):
                    ins = pe.matmul(ps[u][:, t * HG:(t + 1) * HG], hT[u][:, t * P:(t + 1) * P], w["w1"][:],
                                    start=True, stop=True)
                return ins

            def messages(i, u):
                for t in range(TPC):
                    e = slice(t * P, (t + 1) * P)
                    for k in range(2):
                        ins = pe.matmul(ps[u][:, e], mB[u][:, k, e], w["wm3"][:, k, :], start=k == 0, stop=k == 1)
                return ins

            lo, hi = slice(0, P), slice(P, 2 * P)
            steps = {"agg": step("agg", [("dve", "msg"), ("mean_in", 0)] if kind == "edge"
                                 else [("v_in", 0), ("mean_in", 0)], average)} if has_agg else {}
            if kind in ("layer", "layer3"):
                steps["l"] = step("l", [("dve", "ca")], pair(w["rel"][:, layer, :], aggT, w["root"][:, layer, :]))
                steps["tx"] = step("tx", [("dve", "h")], turn(hT))
            if kind in ("start", "layer3", "gcn3"):
                steps["t"] = step("t", [("act", "xn")], turn(xn))
            if kind == "layer3":
                steps["g"] = step("g", [("act", "hh")], first_gcn)
            if gcn:
                steps["tr"] = step("tr", [("dve", "ca")], turn_narrow)
            if kind in ("gcn2", "gcn3"):
                steps["tu"] = step("tu", [("dve", "u")], lambda i, u: pe.transpose(ps[u][:, 0:P], bU[u][:], w["ident"][:]))
                steps["z"] = step("z", [("act", "uT")], z)
            if kind == "gcn3":
                steps["tx"] = step("tx", [("act", "tT")], turn(ex))
            if kind in ("hop", "last_hop"):
                steps["tx"] = step("tx", [("dve", "ca")], turn(aggT))
            if kind == "edge":
                steps["tv"] = step("tv", [("v_in", 0)], turn(V))
                steps["ma"] = step("ma", [("act", "vT")], pair(w["wm1"][:, 0, lo], hT, w["wm1"][:, 1, lo]))
                steps["mb"] = step("mb", [("act", "qa")], pair(w["wm1"][:, 0, hi], hT, w["wm1"][:, 1, hi]))
                steps["mc"] = step("mc", [("act", "qb")], halves(w["wm2"], mA, lo))
                steps["md"] = step("md", [("act", "qc")], halves(w["wm2"], mA, hi))
                steps["m3"] = step("m3", [("act", "qd")], messages)
                steps["na"] = step("na", [("dve", "ca")], pair(w["wn1"][:, 1, lo], aggT, w["wn1"][:, 0, lo]))
                steps["nb"] = step("nb", [("act", "ra")], pair(w["wn1"][:, 1, hi], aggT, w["wn1"][:, 0, hi]))
                steps["up"] = step("up", [("act", "rb")], halves(w["wn2"], mA, slice(0, P)))
                steps["tx"] = step("tx", [("act", "uT")], turn(em))
            run(pe, {**steps, **stream_tensor(pe, stream)})

        @block.scalar
        def _(act):
            begin("act", act)

            def normalise(i, u):
                wait(act, "dve", "nm", i, u)
                if kind == "start":
                    act.wait_ge(row_out[u], i * 16 + 16)
                    wait(act, "pe", "t", i, u, before=1)
                for t in range(TPC):
                    e = slice(t * D, (t + 1) * D)
                    ins = act.activation(xn[u][:, e], xr[u][:, e], ACT.Relu, bias=nm[u][:, t:t + 1],
                                         scale=rs[u][:, t:t + 1])
                mark("act", u, ins)

            def step(to, func, producer, n=CH, freed=None, **kw):
                def run_(i, u):
                    wait(act, "pe", producer, i, u)
                    if kind == "gcn3" and producer == "z":
                        act.wait_ge(row_out[u], i * 16 + 16)
                        wait(act, "pe", "t", i, u, before=1)
                    if freed:
                        wait(act, *freed, i, u, before=1)
                    mark("act", u, act.activation(to(i, u), ps[u][:, 0:n], func, **kw))
                return run_

            def keep(i, u):
                wait(act, "dve", "h", i, u)
                mark("act", u, act.activation(YT[:, cols(i, u)], hT[u][:], ACT.Identity))

            def sigmoid_half(i, u):
                wait(act, "dve", "ub", i, u)
                mark("act", u, act.activation(bA[u][:], bU[u][:], ACT.Tanh, scale=0.5))

            steps = {"xn": normalise} if "xn" in steps_ else {}
            if kind in ("layer", "layer3"):
                steps["e"] = step(lambda i, u: ex[u][:], ACT.Exp, "l", bias=w["b_rel"][:, layer:layer + 1])
                steps["y"] = keep
            if kind in ("start", "gcn3"):
                steps["hh"] = step(lambda i, u: YT[:, cols(i, u)], ACT.Relu, "t")
            if kind == "layer3":
                steps["hh"] = step(lambda i, u: hT[u][:], ACT.Relu, "t")
            if gcn:
                steps["s"] = sigmoid_half
                steps["uT"] = step(lambda i, u: bA[u][:], ACT.Identity, "tu", P)
            if kind == "gcn3":
                steps["tT"] = step(lambda i, u: ex[u][:], ACT.Tanh, "z", bias=w["dst_bz"][:], scale=0.5)
            if kind == "edge":
                steps["vT"] = step(lambda i, u: hT[u][:], ACT.Identity, "tv", freed=("dve", "row"))
                for k, (m, q) in enumerate((("ma", "qa"), ("mb", "qb"))):
                    steps[q] = step(lambda i, u, k=k: mA[u][:, k, :], ACT.Relu, m, bias=w["bm1"][:, k:k + 1])
                for k, (m, q) in enumerate((("mc", "qc"), ("md", "qd"))):
                    steps[q] = step(lambda i, u, k=k: mB[u][:, k, :], ACT.Relu, m, bias=w["bm2"][:, k:k + 1])
                for k, (m, q) in enumerate((("na", "ra"), ("nb", "rb"))):
                    steps[q] = step(lambda i, u, k=k: mA[u][:, k, :], ACT.Relu, m, bias=w["bn1"][:, k:k + 1])
                steps["uT"] = step(lambda i, u: em[u][:], ACT.Identity, "up", bias=w["bn2h"][:])
            run(act, {**steps, **stream_scalar(act, stream)})

        @block.vector
        def _(dve):
            begin("dve", dve)

            def stored(i, u):
                dve.wait_ge(row_out[u], i * 16 + 16)

            def carry_on(i, u):
                wait(dve, "pe", "agg", i, u)
                wait(dve, "dve", "sc", i, u - 1 if u else U - 1, before=0 if u else 1)
                wait(dve, "dve", "ca", i, u, before=1)
                before = carry[u - 1 if u else U - 1][0:width, TPC - 1:TPC]
                ends = g["cont"][0:width, cols(i, u)].rearrange("p (t e) -> p t e", e=P)[:, :, P - 1]
                sums = ps[u][0:width, :].rearrange("p (t e) -> p t e", e=P)[:, :, P - 1]
                mark("dve", u, dve.tensor_tensor_scan(carry[u][0:width, :], ends, sums, before, ALU.mult, ALU.add))

            def complete(i, u):
                wait(dve, "dve", "sc", i, u)
                if kind == "layer":
                    wait(dve, "act", "y", i, u, before=1)
                for t in range(TPC):
                    before = (carry[u][0:width, t - 1:t] if t else
                              carry[u - 1 if u else U - 1][0:width, TPC - 1:TPC])
                    e = slice(t * P, (t + 1) * P)
                    ins = dve.scalar_tensor_tensor(out=aggT[u][0:width, e], in0=g["cont"][0:width, cols(i, u, t, P)],
                                                   scalar=before, in1=ps[u][0:width, e], op0=ALU.mult, op1=ALU.add)
                mark("dve", u, ins)

            def stats(i, u):
                if kind == "start":
                    dve.wait_ge(x_in[u], i * 64 + 64)
                else:
                    wait(dve, "dve", "x", i, u)
                for t in range(TPC):
                    ins = dve.bn_stats(st[u][:, t, :], xr[u][:, t * D:(t + 1) * D])
                mark("dve", u, ins)

            def aggregate(i, u):
                wait(dve, "dve", "st", i, u)
                dve.sem_inc(held, 1)
                for t in range(TPC):
                    ins = dve.bn_aggr(mv[u][:, t, :], st[u][:, t, :])
                mark("dve", u, ins)

            def add_eps(i, u):
                wait(dve, "dve", "ag", i, u)
                wait(dve, "act", "xn", i, u, before=1)
                mark("dve", u, dve.tensor_scalar(ve[u][:], mv[u][:, :, 1], EPS, None, ALU.add))

            def shift(i, u):
                wait(dve, "pool", "rs", i, u)
                mark("dve", u, dve.scalar_tensor_tensor(out=nm[u][:], in0=mv[u][:, :, 0], scalar=-1.0, in1=rs[u][:],
                                                        op0=ALU.mult, op1=ALU.mult))

            def step(waits, op, free_rows=False):
                def run_(i, u):
                    for e, v in waits:
                        if e == "x_in":
                            dve.wait_ge(x_in[u], i * v + v)
                        else:
                            wait(dve, e, v, i, u)
                    if free_rows:
                        stored(i, u)
                    mark("dve", u, op(i, u))
                return run_

            def scaled(to, of, name_):
                return lambda i, u: dve.tensor_tensor(tiles(to[u][:, 0:P]), tiles(of[u][:, 0:P]), factors(name_, i, u),
                                                      ALU.mult)

            def by_row(wt, n):
                return w[wt][:].unsqueeze(1).to_broadcast([P, TPC, n])

            def times_norm(i, u):
                for t in range(TPC):
                    e = slice(t * D, (t + 1) * D)
                    ins = dve.tensor_scalar(rows[u][:, e], xn[u][:, e], factor("norm", i, u, t), None, ALU.mult)
                return ins

            def output(i, u):
                for t in range(TPC):
                    e = slice(t * D, (t + 1) * D)
                    ins = dve.scalar_tensor_tensor(out=YT[:, cols(i, u, t, P)], in0=rows[u][:, e],
                                                   scalar=factor("root_deg", i, u, t), in1=xr[u][:, e],
                                                   op0=ALU.mult, op1=ALU.add)
                return ins

            steps = {"st": stats, "ag": aggregate, "ve": add_eps, "nm": shift, "sc": carry_on, "ca": complete}
            if kind in ("layer", "layer3"):
                steps["m"] = step([("act", "e")], lambda i, u: dve.tensor_scalar(
                    em[u][:], ex[u][:], 1.0, -1.0, ALU.min, ALU.add), free_rows=kind == "layer")
                steps["h"] = step([("dve", "m")], lambda i, u: dve.scalar_tensor_tensor(
                    out=hT[u][:], in0=ps[u][:], scalar=w["b_rel"][:, layer:layer + 1], in1=em[u][:],
                    op0=ALU.add, op1=ALU.max))
            if kind == "layer":
                steps["row"] = step([("pe", "tx")], lambda i, u: dve.tensor_copy(rows[u][:], ps[u][:]))
            if kind == "layer3":
                steps["x"] = step([("pe", "tx"), ("x_in", 16)], lambda i, u: dve.tensor_tensor(
                    xr[u][:], ps[u][:], xr[u][:], ALU.add))
                steps["row"] = step([("pe", "g")], scaled(rows, ps, "dinv"), free_rows=True)
            if gcn:
                steps["a"] = step([("pe", "tr")], scaled(bA, ps, "f1"))
                steps["b"] = step([("x_in", 32 if kind == "gcn3" else 16)], scaled(bB, own, "dinv"))
                steps["u"] = step([("dve", "a"), ("dve", "b")], lambda i, u: dve.tensor_tensor(
                    bU[u][:], bA[u][:], bB[u][:], ALU.add))
            if kind in ("gcn1", "gcn2"):
                first_ = kind == "gcn1"
                steps["ub"] = step([("dve", "u")] if first_ else [("pe", "z")], lambda i, u: dve.tensor_tensor(
                    tiles(bU[u][:]), tiles((bU if first_ else ps)[u][:, 0:P]), by_row("b1row" if first_ else "b2row", HG),
                    ALU.add))
                steps["sg"] = step([("act", "s")], lambda i, u: dve.tensor_scalar(
                    bB[u][:], bA[u][:], 0.5, 0.5, ALU.mult, ALU.add))
                steps["row"] = step([("dve", "sg")], scaled(rows, bB, "dinv"), free_rows=True)
            if kind == "gcn3":
                steps["x"] = step([("pe", "tx"), ("x_in", 32)], lambda i, u: dve.scalar_tensor_tensor(
                    out=xr[u][:], in0=ps[u][:], scalar=0.5, in1=xr[u][:], op0=ALU.mult, op1=ALU.add))
            if kind == "edge":
                steps["msg"] = step([("pe", "m3")], lambda i, u: dve.tensor_tensor(
                    tiles(V[u][:]), tiles(ps[u][:]), by_row("bm3row", D), ALU.add))
                steps["xa"] = step([("pe", "tx"), ("x_in", 32)], lambda i, u: dve.tensor_tensor(
                    ex[u][:], ps[u][:], hr[u][:], ALU.add))
                steps["x"] = step([("dve", "xa")], lambda i, u: dve.tensor_tensor(
                    xr[u][:], xr[u][:], ex[u][:], ALU.add))
                steps["row"] = step([("act", "xn")], times_norm)
                steps["c"] = step([("dve", "row")], lambda i, u: dve.tensor_scalar(
                    YT[:, cols(i, u)], rows[u][:], ALPHA, None, ALU.mult))
            if kind in ("hop", "last_hop"):
                steps["row"] = step([("pe", "tx")], lambda i, u: dve.scalar_tensor_tensor(
                    out=rows[u][:], in0=ps[u][:], scalar=1.0 - ALPHA, in1=YT[:, cols(i, u)], op0=ALU.mult,
                    op1=ALU.add), free_rows=kind == "hop")
            if kind == "last_hop":
                steps["o"] = step([("dve", "row"), ("x_in", 16)], output)
            if has_agg:
                dve.memset(carry[U - 1][:], 0.0).then_inc(link, 1)
                dve.wait_ge(link, 1)
            mine = {n: f for n, f in steps.items() if n in steps_}
            run(dve, {**mine, **stream_vector(dve, stream)})


def write_rows(nc, a, g, rows):
    with Phase(nc) as ctx:
        written = ctx.sem("rows_written")
        block = ctx.enter_context(nc.Block())

        @block.gpsimd
        def _(pool):
            bound = pool.to_reg(N - 1)
            for t in range(NT):
                pool.indirect_dma_start(a["out"], bass.IndirectOffsetOnAxis(g["last"][:, t:t + 1], 0),
                                        rows[:, t * D:(t + 1) * D], None,
                                        bounds_check=bound, oob_is_err=False).then_inc(written, 16)
            pool.wait_ge(written, 16 * NT)


def complete_slots(nc, YT, dst_flat):
    T = NT - 1
    with Phase(nc) as ctx:
        sb = lambda n, shape: ctx.enter_context(nc.sbuf_tensor("fix_" + n, shape, F32))
        bc = sb("dst", [P, NE])
        ends, goes_on = [sb(f"ends{k}", [P, T]) for k in range(2)], [sb(f"goes_on{k}", [P, T]) for k in range(2)]
        diff = sb("diff", [P, T])
        mask, change = [sb(f"mask{k}", [P, CH]) for k in range(2)], [sb(f"change{k}", [P, CH]) for k in range(2)]
        bc_in, done = ctx.sem("fix_dst_in"), ctx.sem("fix_done")
        block = ctx.enter_context(nc.Block())

        @block.sync
        def _(sp):
            sp.dma_start(bc[:], dst_flat.partition_broadcast(P)).then_inc(bc_in, 16)

        @block.vector
        def _(dve):
            first = lambda t: tiles_of(t[:])[:, :, 0]
            tiles_of = lambda ap: ap.rearrange("p (t f) -> p t f", f=P)
            count = 0

            def step(ins):
                nonlocal count
                count += 1
                ins.then_inc(done, 1)
                dve.wait_ge(done, count)

            dve.wait_ge(bc_in, 16)
            step(dve.tensor_copy(ends[0][:], first(YT)[:, 1:NT]))
            dve.tensor_tensor(goes_on[0][:, 0:T - 1], first(bc)[:, 1:T], first(bc)[:, 2:NT], ALU.is_equal)
            step(dve.memset(goes_on[0][:, T - 1:T], 0.0))
            k, reach = 0, 1
            while reach < T:
                old, new = k, 1 - k
                n = T - reach
                step(dve.tensor_tensor(diff[:, 0:n], ends[old][:, reach:T], ends[old][:, 0:n], ALU.subtract))
                step(dve.tensor_tensor(diff[:, 0:n], diff[:, 0:n], goes_on[old][:, 0:n], ALU.mult))
                dve.tensor_tensor(ends[new][:, 0:n], ends[old][:, 0:n], diff[:, 0:n], ALU.add)
                dve.tensor_copy(ends[new][:, n:T], ends[old][:, n:T])
                dve.tensor_tensor(goes_on[new][:, 0:n], goes_on[old][:, 0:n], goes_on[old][:, reach:T], ALU.mult)
                step(dve.memset(goes_on[new][:, n:T], 0.0))
                k, reach = new, 2 * reach
            for c in range(NCH):
                n = min(TPC, T - c * TPC)
                u = c % 2
                at, wide = slice(c * CH, c * CH + n * P), slice(0, n * P)
                spread = lambda t, t0: t[:, t0:t0 + n].unsqueeze(2).to_broadcast([P, n, P])
                following = tiles_of(bc[:])[:, c * TPC + 1:c * TPC + 1 + n, 0:1].to_broadcast([P, n, P])
                dve.tensor_tensor(tiles_of(mask[u][:, wide]), tiles_of(bc[:, at]), following, ALU.is_equal)
                step(dve.tensor_tensor(tiles_of(change[u][:, wide]), tiles_of(YT[:, at]), spread(ends[k], c * TPC),
                                       ALU.subtract))
                step(dve.tensor_tensor(mask[u][:, wide], mask[u][:, wide], change[u][:, wide], ALU.mult))
                dve.tensor_tensor(YT[:, at], YT[:, at], mask[u][:, wide], ALU.subtract).then_inc(done, 1)
                count += 1


def stream_schedule(runs, chunks, chunk0):
    total = sum(runs) * PASSES
    assert chunks + len(STAGES) - 1 <= total
    active = ["".join(s for lag, s in enumerate("ABCDE") if lag <= p < chunks + lag) for p in range(total)]
    begin = [sum(runs[:k]) * PASSES for k in range(len(runs) + 1)]
    return [(chunk0 + i, active[i:j]) for i, j in zip(begin, begin[1:])]


def gnn_kernel(nc, a):
    with ExitStack() as ctx:
        sb = lambda name, shape, dt: ctx.enter_context(nc.sbuf_tensor(name, shape, dt))
        dram = lambda name, shape, dt=F32: nc.dram_tensor(name, shape, dt, kind="Internal").ap()
        w = load_weights(nc, a, sb, None, None)
        isolated_rows(nc, a, w, "all", 7, 1)
        pairs = dram("pairs", (NE + 2, 2), I32)
        dst_flat = dram("dst_flat", (NE,))
        mean = dram("mean", (P, NE))
        with ExitStack() as early:
            c = constants(nc, lambda name, shape, dt: early.enter_context(nc.sbuf_tensor("s" + name, shape, dt)), 0)
            sort_edges(nc, a, w, c, pairs)
        g = edge_table_tiles(sb)
        with ExitStack() as early:
            c = constants(nc, lambda name, shape, dt: early.enter_context(nc.sbuf_tensor(name, shape, dt)), 1)
            edge_tables(nc, a, w, c, pairs, g, dst_flat, mean)
        taps = [dram(f"tap{k}", (NE, HG if k in (4, 5, 6) else D)) for k in range(10)]
        isolated_rows(nc, a, w, "src", 5, NCH // 5, taps, g["src"])
        shared = {"YT": sb("YT", [P, NE], F32), "mean": mean, "stream": stream_tiles(sb)}
        xd = dram("xd", (NE, D))
        T = [dram(f"table{k}", (NE, HG if k in (4, 5, 6) else D)) for k in range(8)]
        H = [dram(f"hop_table{k}", (NE, D)) for k in range(2)]
        plans = iter(stream_schedule([1] * 9 + [HOPS - 1, 1], 91, 7))
        step = lambda kind, **kw: slot_pass(nc, a, w, g, kind, shared, next(plans), **kw)
        step("start", out_table=T[0], xd=xd)
        for l in range(LAYERS - 1):
            step("layer", layer=l, table=T[l], ahead=taps[l], out_table=T[l + 1])
        step("layer3", layer=3, table=T[3], ahead=taps[3], out_table=T[4], xd=xd)
        step("gcn1", table=T[4], ahead=taps[4], out_table=T[5], rows_in=T[4])
        step("gcn2", table=T[5], ahead=taps[5], out_table=T[6], rows_in=T[5])
        step("gcn3", table=T[6], ahead=taps[6], out_table=T[7], xd=xd, rows_in=T[6])
        complete_slots(nc, shared["YT"], dst_flat)
        step("edge", table=T[7], ahead=taps[7], out_table=H[0], xd=xd, rows_in=T[7])
        hops = range(HOPS - 1)
        step("hop", repeats=HOPS - 1, table=[H[k % 2] for k in hops], ahead=[taps[9 if k else 8] for k in hops],
             out_table=[H[(k + 1) % 2] for k in hops])
        step("last_hop", table=H[(HOPS - 1) % 2], ahead=taps[9], xd=xd)
        write_rows(nc, a, g, shared["YT"])


_INS = ["x", "src", "dst", "L0_gnn_Ws_rel", "L0_gnn_bs_rel", "L0_gnn_Ws_root",
        "L1_gnn_W1", "L1_gnn_b1", "L1_gnn_W2", "L1_gnn_b2", "L1_gnn_W3", "L1_gnn_b3", "L1_gnn_Wlin", "L1_gnn_blin",
        "L2_gnn_Wm1", "L2_gnn_bm1", "L2_gnn_Wm2", "L2_gnn_bm2", "L2_gnn_Wm3", "L2_gnn_bm3",
        "L2_gnn_Wn1", "L2_gnn_bn1", "L2_gnn_Wn2", "L2_gnn_bn2"]


def kernel(**inputs):
    import numpy as _np
    import concourse.bacc as _bacc
    from concourse import mybir as _mybir
    from concourse.bass_utils import run_bass_kernel_spmd as _run

    nc = _bacc.Bacc("TRN2", target_bir_lowering=False, num_devices=1)
    arrays, aps = {}, {}
    for name in _INS:
        a = _np.ascontiguousarray(inputs[name])
        arrays[f"in_{name}"] = a
        aps[name] = nc.dram_tensor(f"in_{name}", a.shape, _mybir.dt.from_np(a.dtype), kind="ExternalInput").ap()
    aps["out"] = nc.dram_tensor("out_0", (50000, 128), _mybir.dt.float32, kind="ExternalOutput").ap()
    gnn_kernel(nc, aps)
    r = _run(nc, [arrays], core_ids=[0])
    return r.results[0]["out_0"]
```
